# Optimizing a Trainium2 kernel written in Bass

```python
import numpy as np
import jax
import jax.numpy as jnp

def _softmax(x, axis=-1):
    return jax.nn.softmax(x, axis=axis)

def _gelu(x):
    return jax.nn.gelu(x, approximate=True)

def _silu(x):
    return jax.nn.silu(x)

def _sigmoid(x):
    return jax.nn.sigmoid(x)

def _layernorm(x, axis=-1, eps=1e-05):
    m = jnp.mean(x, axis=axis, keepdims=True)
    v = jnp.var(x, axis=axis, keepdims=True)
    return (x - m) / jnp.sqrt(v + eps)

def _scatter_add(tgt, idx, src, axis=0):
    return tgt.at[idx].add(src)

def _segment_sum(src, seg, n):
    return jax.ops.segment_sum(src, seg, n)
kernel_name = 'mk_adj_preln_d4_adj_r2_e67ba2'

def setup_inputs(seed: int=0):
    np.random.seed(seed)
    _w = jnp.asarray

    def _rec_inputs():
        import jax
        import jax.numpy as jnp
        _gk = jax.random.key(seed)
        x = -0.0005207 + 1.001 * jax.random.normal(jax.random.fold_in(_gk, 1), (4096, 128), jnp.float32)
        _a = jax.random.bernoulli(jax.random.fold_in(_gk, 2), 0.000488281, (4096, 4096))
        _a = jnp.logical_or(_a, jnp.swapaxes(_a, -1, -2))
        _a = jnp.logical_or(_a, jnp.eye(4096, dtype=bool))
        _af = _a.astype(jnp.float32)
        _af = _af * jax.random.uniform(jax.random.fold_in(_gk, 3), (4096, 4096), jnp.float32, 0.05, 6.10351e-05)
        adj = _af
        return (x, adj)
    x, adj = _rec_inputs()

    def _L0_gnn_setup():
        import jax, jax.numpy as jnp
        import numpy as np
        N, D, H = (8192, 128, 256)
        C = 1.0
        EPS_GIN = 0.0
        MIN_NORM = 1e-07

        def _arcosh(z):
            z = jnp.clip(z, 1.0 + MIN_NORM, None)
            return jnp.log(z + jnp.sqrt(z * z - 1.0))

        def exp_map_zero(u, c):
            sqrtK = 1.0 / jnp.sqrt(c)
            x = u[..., 1:]
            n = jnp.clip(jnp.linalg.norm(x, axis=-1, keepdims=True), MIN_NORM, None)
            theta = n / sqrtK
            return jnp.concatenate([sqrtK * jnp.cosh(theta), sqrtK * jnp.sinh(theta) * x / n], axis=-1)

        def log_map_zero(p, c):
            sqrtK = 1.0 / jnp.sqrt(c)
            y = p[..., 1:]
            n = jnp.clip(jnp.linalg.norm(y, axis=-1, keepdims=True), MIN_NORM, None)
            theta = _arcosh(p[..., :1] / sqrtK)
            return jnp.concatenate([jnp.zeros_like(theta), sqrtK * theta * y / n], axis=-1)
        key = jax.random.key(seed)
        k1, k2, k3, k4 = jax.random.split(key, 4)
        x = jax.random.normal(k1, (N, D), dtype=jnp.float32)
        adj = jax.random.uniform(k2, (N, N), dtype=jnp.float32) / N
        W1 = jax.random.normal(k3, (D, H), dtype=jnp.float32) * (1.0 / np.sqrt(D))
        b1 = jnp.zeros((H,), dtype=jnp.float32)
        W2 = jax.random.normal(k4, (H, D), dtype=jnp.float32) * (1.0 / np.sqrt(H))
        b2 = jnp.zeros((D,), dtype=jnp.float32)
        return {'x': x, 'adj': adj, 'W1': W1, 'b1': b1, 'W2': W2, 'b2': b2}
    _L0_gnn_all = _L0_gnn_setup()
    _L0_gnn_in = {k: v for k, v in _L0_gnn_all.items() if k in ('W1', 'b1', 'W2', 'b2')}
    del _L0_gnn_all

    def _L1_gnn_setup():
        import jax, jax.numpy as jnp
        import numpy as np
        N = 4096
        D = 128
        EDGE_P = 0.005
        key = jax.random.key(seed)
        kx, ka, kb = jax.random.split(key, 3)
        x = jax.random.normal(kx, (N, D), dtype=jnp.float32)
        adj = (jax.random.uniform(ka, (N, N)) < EDGE_P).astype(jnp.float32)
        adj = jnp.maximum(adj, jnp.eye(N, dtype=jnp.float32))
        beta = jax.random.uniform(kb, (1,), dtype=jnp.float32)
        return {'x': x, 'adj': adj, 'beta': beta}
    _L1_gnn_all = _L1_gnn_setup()
    _L1_gnn_in = {k: v for k, v in _L1_gnn_all.items() if k in ('beta',)}
    del _L1_gnn_all

    def _L2_gnn_setup():
        import jax, jax.numpy as jnp
        import numpy as np
        N = 4096
        F_IN = 128
        H = 2
        DH = 64
        NEG = -1000000000.0
        key = jax.random.key(seed)
        k1, k2, k3, k4, k5 = jax.random.split(key, 5)
        node_features = jax.random.normal(k1, (N, F_IN), dtype=jnp.float32)
        adj = (jax.random.uniform(k2, (N, N)) < 32.0 / N).astype(jnp.float32)
        adj = jnp.maximum(adj, jnp.eye(N, dtype=jnp.float32))
        W = jax.random.normal(k3, (H, F_IN, DH), dtype=jnp.float32) * 0.1
        a_self = jax.random.normal(k4, (H, DH), dtype=jnp.float32) * 0.1
        a_neigh = jax.random.normal(k5, (H, DH), dtype=jnp.float32) * 0.1
        bias = jnp.zeros((H * DH,), dtype=jnp.float32)
        return {'node_features': node_features, 'adj_matrix': adj, 'W': W, 'a_self': a_self, 'a_neigh': a_neigh, 'bias': bias}
    _L2_gnn_all = _L2_gnn_setup()
    _L2_gnn_in = {k: v for k, v in _L2_gnn_all.items() if k in ('W', 'a_self', 'a_neigh', 'bias')}
    del _L2_gnn_all

    def _L3_gnn_setup():
        import jax, jax.numpy as jnp
        import numpy as np
        N, F_IN, F_OUT, H = (4096, 128, 128, 4)
        NEG = -1000000000.0
        key = jax.random.key(seed)
        k1, k2, k3, k4, k5 = jax.random.split(key, 5)
        x = jax.random.normal(k1, (N, F_IN), dtype=jnp.float32)
        edge = jax.random.uniform(k2, (N, N)) < 0.05
        mask = jnp.where(edge, 0.0, NEG).astype(jnp.float32)

        def xavier(k, shape, fan_in, fan_out):
            lim = float(np.sqrt(6.0 / (fan_in + fan_out)))
            return jax.random.uniform(k, shape, minval=-lim, maxval=lim, dtype=jnp.float32)
        W = xavier(k3, (H, F_IN, F_OUT), F_IN, F_OUT)
        a_src = xavier(k4, (H, F_OUT), F_OUT, 1)
        a_tgt = xavier(k5, (H, F_OUT), F_OUT, 1)
        return {'x': x, 'mask': mask, 'W': W, 'a_src': a_src, 'a_tgt': a_tgt}
    _L3_gnn_all = _L3_gnn_setup()
    _L3_gnn_in = {k: v for k, v in _L3_gnn_all.items() if k in ('W', 'a_src', 'a_tgt')}
    del _L3_gnn_all
    return {'x': x, 'adj': adj, 'L0_gnn_W1': _L0_gnn_in['W1'], 'L0_gnn_b1': _L0_gnn_in['b1'], 'L0_gnn_W2': _L0_gnn_in['W2'], 'L0_gnn_b2': _L0_gnn_in['b2'], 'L1_gnn_beta': _L1_gnn_in['beta'], 'L2_gnn_W': _L2_gnn_in['W'], 'L2_gnn_a_self': _L2_gnn_in['a_self'], 'L2_gnn_a_neigh': _L2_gnn_in['a_neigh'], 'L2_gnn_bias': _L2_gnn_in['bias'], 'L3_gnn_W': _L3_gnn_in['W'], 'L3_gnn_a_src': _L3_gnn_in['a_src'], 'L3_gnn_a_tgt': _L3_gnn_in['a_tgt']}

def reference(x, adj, L0_gnn_W1, L0_gnn_b1, L0_gnn_W2, L0_gnn_b2, L1_gnn_beta, L2_gnn_W, L2_gnn_a_self, L2_gnn_a_neigh, L2_gnn_bias, L3_gnn_W, L3_gnn_a_src, L3_gnn_a_tgt):
    import jax
    import jax.numpy as jnp

    def _L0_gnn_ref(x, adj, W1, b1, W2, b2):
        import jax, jax.numpy as jnp
        import numpy as np
        N, D, H = (8192, 128, 256)
        C = 1.0
        EPS_GIN = 0.0
        MIN_NORM = 1e-07

        def _arcosh(z):
            z = jnp.clip(z, 1.0 + MIN_NORM, None)
            return jnp.log(z + jnp.sqrt(z * z - 1.0))

        def exp_map_zero(u, c):
            sqrtK = 1.0 / jnp.sqrt(c)
            x = u[..., 1:]
            n = jnp.clip(jnp.linalg.norm(x, axis=-1, keepdims=True), MIN_NORM, None)
            theta = n / sqrtK
            return jnp.concatenate([sqrtK * jnp.cosh(theta), sqrtK * jnp.sinh(theta) * x / n], axis=-1)

        def log_map_zero(p, c):
            sqrtK = 1.0 / jnp.sqrt(c)
            y = p[..., 1:]
            n = jnp.clip(jnp.linalg.norm(y, axis=-1, keepdims=True), MIN_NORM, None)
            theta = _arcosh(p[..., :1] / sqrtK)
            return jnp.concatenate([jnp.zeros_like(theta), sqrtK * theta * y / n], axis=-1)
        h = exp_map_zero(x, C)
        agg = exp_map_zero(adj @ log_map_zero(h, C), C)
        out = exp_map_zero(log_map_zero(agg, C) + (1.0 + EPS_GIN) * log_map_zero(h, C), C)
        t = jax.nn.relu(out @ W1 + b1) @ W2 + b2
        return t

    def _L1_gnn_ref(x, adj, beta):
        import jax, jax.numpy as jnp
        import numpy as np
        N = 4096
        D = 128
        EDGE_P = 0.005
        norm2 = jnp.linalg.norm(x, axis=1, keepdims=True)
        cos = beta[0] * (x @ x.T) / (norm2 @ norm2.T + 1e-07)
        masked = cos + (1.0 - adj) * -1000000000.0
        P = jax.nn.softmax(masked, axis=1)
        return P @ x

    def _L2_gnn_ref(node_features, adj_matrix, W, a_self, a_neigh, bias):
        import jax, jax.numpy as jnp
        import numpy as np
        N = 4096
        F_IN = 128
        H = 2
        DH = 64
        NEG = -1000000000.0
        h = jnp.einsum('nf,hfd->hnd', node_features, W)
        s_self = jnp.einsum('hnd,hd->hn', h, a_self)
        s_neigh = jnp.einsum('hnd,hd->hn', h, a_neigh)
        scores = s_self[:, :, None] + s_neigh[:, None, :]
        scores = scores + (1.0 - adj_matrix)[None] * NEG
        attn = jax.nn.softmax(scores, axis=-1)
        ctx = jnp.einsum('hij,hjd->hid', attn, h)
        out = jnp.transpose(ctx, (1, 0, 2)).reshape(node_features.shape[0], -1)
        out = out + bias
        return jax.nn.elu(out)

    def _L3_gnn_ref(x, mask, W, a_src, a_tgt):
        import jax, jax.numpy as jnp
        import numpy as np
        N, F_IN, F_OUT, H = (4096, 128, 128, 4)
        NEG = -1000000000.0
        proj = jnp.einsum('nf,hfo->hno', x, W)
        s_src = jnp.einsum('hno,ho->hn', proj, a_src)
        s_tgt = jnp.einsum('hno,ho->hn', proj, a_tgt)
        scores = jax.nn.leaky_relu(s_src[:, :, None] + s_tgt[:, None, :], negative_slope=0.2)
        attn = jax.nn.softmax(mask[None, :, :] + scores, axis=1)
        vals = jnp.einsum('hij,hjo->hio', attn, proj)
        vals = vals + x[None, :, :]
        vals = jax.nn.elu(vals)
        return vals.mean(axis=0)
    h = jnp.maximum(_layernorm(x, axis=-1), 0.0)
    x = x + _L0_gnn_ref(h, adj, L0_gnn_W1, L0_gnn_b1, L0_gnn_W2, L0_gnn_b2)
    h = jnp.maximum(_layernorm(x, axis=-1), 0.0)
    x = x + _L1_gnn_ref(h, adj, L1_gnn_beta)
    h = jnp.maximum(_layernorm(x, axis=-1), 0.0)
    x = x + _L2_gnn_ref(h, adj, L2_gnn_W, L2_gnn_a_self, L2_gnn_a_neigh, L2_gnn_bias)
    h = jnp.maximum(_layernorm(x, axis=-1), 0.0)
    x = x + _L3_gnn_ref(h, adj, L3_gnn_W, L3_gnn_a_src, L3_gnn_a_tgt)
    return x

_drawn_inputs = setup_inputs


def setup_inputs(seed=0):
    import zlib

    import numpy as np

    out = dict(_drawn_inputs(seed))
    spreads = {'L0_gnn_b1': (0.0, 2.0), 'L0_gnn_b2': (0.0, 2.0), 'L2_gnn_bias': (0.0, 2.0)}
    factors = {'L2_gnn_W': 31.217,
     'L3_gnn_W': 8.0,
     'L3_gnn_a_src': 8.0,
     'L3_gnn_a_tgt': 64.0,
     'L2_gnn_a_self': 54.083,
     'L2_gnn_a_neigh': 6.358}
    for name, (base, spread) in spreads.items():
        noise = np.random.default_rng([zlib.crc32(name.encode()), seed]).standard_normal(out[name].shape)
        drawn = base * np.exp(spread * noise) if base else spread * noise
        out[name] = jnp.asarray(drawn.astype(out[name].dtype))
    for name, factor in factors.items():
        out[name] = (out[name] * factor).astype(out[name].dtype)
    return out
```

```python
from contextlib import ExitStack

import numpy as np

import concourse.bass as bass
import concourse.mybir as mybir

F32 = mybir.dt.float32
ALU = mybir.AluOpType
ACT = mybir.ActivationFunctionType
X_AXIS = mybir.AxisListType.X

P = 128
N = 4096
D = 128
HID = 256
NT = N // P
BANK = 512
TPB = BANK // P
NCH = N // BANK
H2, DH2 = 2, 64
H3 = 4
LN_EPS = 1e-5
MIN_NORM = 1e-7
NEG = 1e9
SLOPE = 0.2
_Z0 = float(np.float32(1.0) + np.float32(MIN_NORM))
THETA_MIN = float(np.log(_Z0 + np.sqrt(_Z0 * _Z0 - 1.0)))


TINY_NORM = 1e-18
LOG_EPS = float(np.log(1e-7))
LOWEST = float(np.finfo(np.float32).min)


class Shared:
    pass


def ts(i, n):
    return slice(i * n, (i + 1) * n)


class Link:

    def __init__(self, eng, sem):
        self.eng, self.sem, self.n = eng, sem, 0

    def __call__(self, ins):
        self.n += 1
        ins.then_inc(self.sem, 1)
        self.eng.wait_ge(self.sem, self.n)


def over_rows(col, n=NT):
    return col.unsqueeze(2).to_broadcast([P, n, D])


def row_tiles(dram):
    return dram.rearrange("(t p) d -> p t d", p=P)



def layer_norm_dve(nc, dve, link, s, rows, h, sq, mean, var):
    link(nc.vector.tensor_reduce(mean[:, :], rows[:, :, :], X_AXIS, ALU.add))
    link(nc.vector.tensor_scalar(mean[:, :], mean[:, :], 1.0 / D, None, ALU.mult))
    nc.vector.tensor_tensor(h[:, :, :], rows[:, :, :], over_rows(mean[:, :]),
                            ALU.subtract).then_inc(s["centered"], 1)
    dve.wait_ge(s["squared"], 1)
    link(nc.vector.tensor_reduce(var[:, :], sq[:, :, :], X_AXIS, ALU.add))
    nc.vector.tensor_scalar(var[:, :], var[:, :], 1.0 / D, LN_EPS, ALU.mult, ALU.add).then_inc(s["var"], 1)
    dve.wait_ge(s["std"], 1)
    link(nc.vector.reciprocal(var[:, :], var[:, :]))
    dve.wait_ge(s["centered"], 1)
    link(nc.vector.tensor_tensor(h[:, :, :], h[:, :, :], over_rows(var[:, :]), ALU.mult))
    link(nc.vector.tensor_scalar(h[:, :, :], h[:, :, :], 0.0, None, ALU.max))


def layer_norm_act(nc, act, s, h, sq, var):
    act.wait_ge(s["centered"], 1)
    nc.scalar.activation(sq[:, :, :], h[:, :, :], ACT.Square).then_inc(s["squared"], 1)
    act.wait_ge(s["var"], 1)
    nc.scalar.activation(var[:, :], var[:, :], ACT.Sqrt).then_inc(s["std"], 1)


def transpose_rows_pe(nc, pe, rows, banks, identity, done, taken):
    for c in range(NCH):
        if c >= len(banks):
            pe.wait_ge(taken, c - len(banks) + 1)
        for s in range(TPB):
            last = nc.tensor.transpose(banks[c % len(banks)][:, ts(s, P)], rows(c * TPB + s), identity)
        last.then_inc(done, 1)


def transpose_rows_act(nc, act, out, banks, done, taken):
    for c in range(NCH):
        act.wait_ge(done, c + 1)
        nc.scalar.copy(out(c), banks[c % len(banks)][:, :]).then_inc(taken, 1)


def next_semaphore(nc):
    with nc.semaphore("unused") as sem:
        return sem.num


def clear_semaphores(nc, first, end):
    with nc.Block() as block:
        @block.gpsimd
        def _(pool):
            pool.sem_clear(range(first, end))


def sems(nc, mem, phase, names):
    return {n: mem.enter_context(nc.semaphore(f"{phase}_{n}")) for n in names.split()}



def layer0_features(nc, g, x_dram):
    with ExitStack() as mem:
        x = mem.enter_context(nc.sbuf_tensor("l0_x", [P, NT, D], F32))
        sq = mem.enter_context(nc.sbuf_tensor("l0_sq", [P, NT, D], F32))
        mean, var, inv = (mem.enter_context(nc.sbuf_tensor(f"l0_{n}", [P, NT], F32)) for n in ("mean", "var", "inv"))
        s = sems(nc, mem, "l0", "x_in ident zeroed centered squared var std tangent_sq norm2 norm chain")
        h = g.rows
        block = mem.enter_context(nc.Block())

        @block.sync
        def _(sp):
            sp.dma_start(x[:, :, :], row_tiles(x_dram)).then_inc(s["x_in"], 16)

        @block.gpsimd
        def _(pool):
            nc.gpsimd.memset(g.ones[:, :], 1.0).then_inc(s["ident"], 1)
            nc.gpsimd.memset(g.identity[:, :], 0.0).then_inc(s["zeroed"], 1)
            pool.wait_ge(s["zeroed"], 1)
            nc.gpsimd.affine_select(out=g.identity[:, :], in_=g.identity[:, :], compare_op=ALU.not_equal,
                                    fill=1.0, base=0, pattern=[[-1, P]], channel_multiplier=1).then_inc(s["ident"], 1)

        @block.vector
        def _(dve):
            link = Link(dve, s["chain"])
            dve.wait_ge(s["x_in"], 16)
            layer_norm_dve(nc, dve, link, s, x, h, sq, mean, var)
            nc.vector.memset(h[:, :, 0:1], 0.0).then_inc(s["tangent_sq"], 1)
            dve.wait_ge(s["squared"], 2)
            nc.vector.tensor_reduce(var[:, :], sq[:, :, :], X_AXIS, ALU.add).then_inc(s["norm2"], 1)
            dve.wait_ge(s["norm"], 1)
            link(nc.vector.tensor_scalar(var[:, :], var[:, :], MIN_NORM, None, ALU.max))
            link(nc.vector.reciprocal(inv[:, :], var[:, :]))
            link(nc.vector.tensor_scalar(var[:, :], var[:, :], THETA_MIN, None, ALU.max))
            link(nc.vector.tensor_tensor(var[:, :], var[:, :], inv[:, :], ALU.mult))
            link(nc.vector.tensor_tensor(h[:, :, :], h[:, :, :], over_rows(var[:, :]), ALU.mult))

        @block.scalar
        def _(act):
            layer_norm_act(nc, act, s, h, sq, var)
            act.wait_ge(s["tangent_sq"], 1)
            nc.scalar.activation(sq[:, :, :], h[:, :, :], ACT.Square).then_inc(s["squared"], 1)
            act.wait_ge(s["norm2"], 1)
            nc.scalar.activation(var[:, :], var[:, :], ACT.Sqrt).then_inc(s["norm"], 1)


def layer0_aggregate(nc, g, adj, adj_t):
    GR = BANK // P
    NG = NT // GR
    CHT = 8
    NLOAD = NT // CHT
    STT = 4
    NST = NT // STT
    SLOTS = 4
    BANKS = 4
    with ExitStack() as mem:
        blk = [mem.enter_context(nc.sbuf_tensor(f"a_adj{c}", [P, GR, CHT * P], F32)) for c in range(NLOAD)]
        out = [mem.enter_context(nc.sbuf_tensor(f"a_out{c}", [P, STT, BANK], F32)) for c in range(SLOTS)]
        tp = [mem.enter_context(nc.psum_tensor(f"a_tp{b}", [P, BANK], F32)) for b in range(BANKS)]
        acc = mem.enter_context(nc.psum_tensor("a_acc", [P, BANK], F32))
        s = sems(nc, mem, "a", "transposed copied_act copied_dve multiplied summed taken")
        loaded = [mem.enter_context(nc.semaphore(f"a_loaded{c}")) for c in range(NLOAD)]
        stored = [mem.enter_context(nc.semaphore(f"a_stored{c}")) for c in range(SLOTS)]
        block = mem.enter_context(nc.Block())
        adj_v = adj.rearrange("(gr s p) j -> gr p s j", s=GR, p=P)
        adj_t_v = adj_t.rearrange("(q t p) i -> q p t i", t=STT, p=P)

        def columns(grp):
            if isinstance(grp, int):
                return slice(grp * BANK, (grp + 1) * BANK)
            return bass.ds(grp * BANK, BANK)

        @block.sync
        def _(sp):
            def load(grp, c):
                src = adj_v[grp] if isinstance(grp, int) else adj_v[bass.ds(grp, 1)].rearrange("o p s j -> (o p) s j")
                sp.dma_start(blk[c][:, :, :], src[:, :, ts(c, CHT * P)]).then_inc(loaded[c], 16)

            def stores(grp, c):
                for q in (2 * c, 2 * c + 1):
                    sp.wait_ge(s["multiplied"], grp * NT + (q + 1) * STT)
                    sp.dma_start(adj_t_v[q, :, :, columns(grp)], out[q % SLOTS][:, :, :]).then_inc(stored[q % SLOTS], 16)

            for c in range(NLOAD):
                load(0, c)
            with sp.Fori(0, NG - 1) as grp:
                for c in range(NLOAD):
                    stores(grp, c)
                    load(grp + 1, c)
            for c in range(NLOAD):
                stores(NG - 1, c)
            for c in range(SLOTS):
                sp.wait_ge(stored[c], 16 * NG * NST // SLOTS)

        @block.tensor
        def _(pe):
            def copied(grp, jt, ahead):
                return grp * (NT // 2) + (jt - ahead) // 2 + 1

            def group(grp, first):
                for jt in range(NT + 1):
                    if jt < NT:
                        if jt % CHT == 0:
                            pe.wait_ge(loaded[jt // CHT], grp * 16 + 16)
                        if not (first and jt < BANKS):
                            pe.wait_ge((s["copied_act"], s["copied_dve"])[jt % 2], copied(grp, jt, BANKS))
                        for r in range(GR):
                            last = nc.tensor.transpose(tp[jt % BANKS][:, ts(r, P)],
                                                       blk[jt // CHT][:, r, ts(jt % CHT, P)], g.identity[:, :])
                        last.then_inc(s["transposed"], 1)
                    if jt > 0:
                        m = jt - 1
                        pe.wait_ge((s["copied_act"], s["copied_dve"])[m % 2], copied(grp, m, 0))
                        if m == 0 and not first:
                            pe.wait_ge(s["taken"], grp)
                        mm = nc.tensor.matmul(acc[:, :], g.rows[:, m, :], out[(m // STT) % SLOTS][:, m % STT, :],
                                              start=(m == 0), stop=(m == NT - 1))
                        mm.then_inc(s["multiplied"], 1)

            group(0, True)
            with pe.Fori(1, NG) as grp:
                group(grp, False)

        def copies(eng, copy, odd, copied_sem):
            def group(grp, first):
                for jt in range(odd, NT, 2):
                    q = jt // STT
                    if jt % STT == odd and not (first and q < SLOTS):
                        eng.wait_ge(stored[q % SLOTS], (grp * (NST // SLOTS) + q // SLOTS) * 16)
                    eng.wait_ge(s["transposed"], grp * NT + jt + 1)
                    copy(out[q % SLOTS][:, jt % STT, :], tp[jt % BANKS][:, :]).then_inc(copied_sem, 1)
                if not odd:
                    eng.wait_ge(s["multiplied"], grp * NT + NT)
                    copy(g.agg_t[:, columns(grp)], acc[:, :]).then_inc(s["taken"], 1)

            group(0, True)
            with eng.Fori(1, NG) as grp:
                group(grp, False)

        @block.scalar
        def _(act):
            copies(act, nc.scalar.copy, 0, s["copied_act"])

        @block.vector
        def _(dve):
            copies(dve, nc.vector.tensor_copy, 1, s["copied_dve"])


def layer0_combine(nc, g, w1, b1, w2, b2, x_dram, x1_dram):
    with ExitStack() as mem:
        agg = mem.enter_context(nc.sbuf_tensor("c_agg", [P, NT, D], F32))
        sq = mem.enter_context(nc.sbuf_tensor("c_sq", [P, NT, D], F32))
        x = mem.enter_context(nc.sbuf_tensor("c_x", [P, NT, D], F32))
        w1_sb = mem.enter_context(nc.sbuf_tensor("c_w1", [P, HID], F32))
        w2_sb = mem.enter_context(nc.sbuf_tensor("c_w2", [P, HID // P, D], F32))
        b1_sb = mem.enter_context(nc.sbuf_tensor("c_b1", [P, HID // P], F32))
        b2_sb = mem.enter_context(nc.sbuf_tensor("c_b2", [P, 1, D], F32))
        hid = [mem.enter_context(nc.sbuf_tensor(f"c_hid{m}", [P, BANK], F32)) for m in range(HID // P)]
        n, inv, e, cosh = (mem.enter_context(nc.sbuf_tensor(f"c_{k}", [P, NT], F32)) for k in ("n", "inv", "e", "cosh"))
        tp = [mem.enter_context(nc.psum_tensor(f"c_tp{b}", [P, BANK], F32)) for b in range(2)]
        pre = [mem.enter_context(nc.psum_tensor(f"c_pre{m}", [P, BANK], F32)) for m in range(HID // P)]
        mlp = mem.enter_context(nc.psum_tensor("c_mlp", [P, BANK], F32))
        s = sems(nc, mem, "c", "weights x_in x_out t1 t1_out t2 t2_out chain v squared norm2 norm e combined "
                               "out_ready pre hid mlp added biased")
        agg_t = g.agg_t
        block = mem.enter_context(nc.Block())

        @block.sync
        def _(sp):
            sp.dma_start(w1_sb[:, :], w1).then_inc(s["weights"], 16)
            sp.dma_start(w2_sb[:, :, :], w2.rearrange("(m p) d -> p m d", p=P)).then_inc(s["weights"], 16)
            with nc.allow_non_contiguous_dma("two columns of biases"):
                sp.dma_start(b1_sb[:, :], b1.rearrange("(m p) -> p m", p=P)).then_inc(s["weights"], 16)
            sp.dma_start(b2_sb[:, 0, :], b2.partition_broadcast(P)).then_inc(s["weights"], 16)
            sp.dma_start(x[:, :, :], row_tiles(x_dram)).then_inc(s["x_in"], 16)
            sp.wait_ge(s["added"], NCH)
            sp.dma_start(row_tiles(x1_dram), x[:, :, :]).then_inc(s["x_out"], 16)
            sp.wait_ge(s["x_out"], 16)

        @block.tensor
        def _(pe):
            transpose_rows_pe(nc, pe, lambda t: agg_t[:, ts(t, P)], tp, g.identity[:, :], s["t1"], s["t1_out"])
            pe.wait_ge(s["out_ready"], 1)
            pe.wait_ge(s["t1_out"], NCH)
            transpose_rows_pe(nc, pe, lambda t: agg[:, t, :], tp, g.identity[:, :], s["t2"], s["t2_out"])
            pe.wait_ge(s["weights"], 64)
            pe.wait_ge(s["t2_out"], NCH)

            def chunk(c, first):
                if not first:
                    pe.wait_ge(s["hid"], c * (HID // P))
                for m in range(HID // P):
                    cols = slice(0, BANK) if first else bass.ds(c * BANK, BANK)
                    nc.tensor.matmul(pre[m][:, :], w1_sb[:, ts(m, P)], agg_t[:, cols],
                                     start=True, stop=True).then_inc(s["pre"], 1)
                if not first:
                    pe.wait_ge(s["added"], c)
                pe.wait_ge(s["hid"], (c + 1) * (HID // P))
                for r in range(TPB):
                    for m in range(HID // P):
                        last = nc.tensor.matmul(mlp[:, ts(r, D)], hid[m][:, ts(r, P)], w2_sb[:, m, :],
                                                start=(m == 0), stop=(m == HID // P - 1))
                last.then_inc(s["mlp"], 1)

            chunk(0, True)
            with pe.Fori(1, NCH) as c:
                chunk(c, False)

        @block.scalar
        def _(act):
            transpose_rows_act(nc, act, lambda c: agg[:, ts(c, TPB), :].rearrange("p t d -> p (t d)"), tp, s["t1"], s["t1_out"])
            for k in range(2):
                act.wait_ge(s["v"], k) if k else act.wait_ge(s["t1_out"], NCH)
                nc.scalar.activation(sq[:, :, :], agg[:, :, :], ACT.Square).then_inc(s["squared"], 1)
                act.wait_ge(s["norm2"], k + 1)
                nc.scalar.activation(n[:, :], n[:, :], ACT.Sqrt).then_inc(s["norm"], 1)
            act.wait_ge(s["v"], 2)
            nc.scalar.activation(e[:, :], n[:, :], ACT.Exp).then_inc(s["e"], 1)
            transpose_rows_act(nc, act, lambda c: agg_t[:, ts(c, BANK)], tp, s["t2"], s["t2_out"])
            act.wait_ge(s["weights"], 64)

            def chunk(c, first):
                for m in range(HID // P):
                    act.wait_ge(s["pre"], c * (HID // P) + m + 1)
                    if not first and m == 0:
                        act.wait_ge(s["mlp"], c)
                    nc.scalar.activation(hid[m][:, :], pre[m][:, :], ACT.Relu, bias=b1_sb[:, m:m + 1]).then_inc(s["hid"], 1)

            chunk(0, True)
            with act.Fori(1, NCH) as c:
                chunk(c, False)

        @block.vector
        def _(dve):
            link = Link(dve, s["chain"])
            dve.wait_ge(s["weights"], 64)
            dve.wait_ge(s["x_in"], 16)
            nc.vector.tensor_tensor(x[:, :, :], x[:, :, :], b2_sb[:, :, :].to_broadcast([P, NT, D]),
                                    ALU.add).then_inc(s["biased"], 1)
            dve.wait_ge(s["squared"], 1)
            nc.vector.tensor_reduce(n[:, :], sq[:, :, :], X_AXIS, ALU.add).then_inc(s["norm2"], 1)
            dve.wait_ge(s["norm"], 1)
            link(nc.vector.tensor_scalar(n[:, :], n[:, :], MIN_NORM, None, ALU.max))
            link(nc.vector.reciprocal(inv[:, :], n[:, :]))
            link(nc.vector.tensor_scalar(n[:, :], n[:, :], THETA_MIN, None, ALU.max))
            link(nc.vector.tensor_tensor(n[:, :], n[:, :], inv[:, :], ALU.mult))
            link(nc.vector.tensor_tensor(agg[:, :, :], agg[:, :, :], over_rows(n[:, :]), ALU.mult))
            nc.vector.tensor_tensor(agg[:, :, :], agg[:, :, :], g.rows[:, :, :], ALU.add).then_inc(s["v"], 1)
            dve.wait_ge(s["squared"], 2)
            nc.vector.tensor_reduce(n[:, :], sq[:, :, :], X_AXIS, ALU.add).then_inc(s["norm2"], 1)
            dve.wait_ge(s["norm"], 2)
            nc.vector.tensor_scalar(n[:, :], n[:, :], MIN_NORM, None, ALU.max).then_inc(s["v"], 1)
            dve.wait_ge(s["v"], 2)
            link(nc.vector.reciprocal(inv[:, :], n[:, :]))
            dve.wait_ge(s["e"], 1)
            link(nc.vector.reciprocal(n[:, :], e[:, :]))
            link(nc.vector.tensor_tensor(cosh[:, :], e[:, :], n[:, :], ALU.add))
            link(nc.vector.tensor_scalar(cosh[:, :], cosh[:, :], 0.5, None, ALU.mult))
            link(nc.vector.tensor_tensor(e[:, :], e[:, :], n[:, :], ALU.subtract))
            link(nc.vector.scalar_tensor_tensor(e[:, :], e[:, :], 0.5, inv[:, :], ALU.mult, ALU.mult))
            link(nc.vector.tensor_tensor(agg[:, :, :], agg[:, :, :], over_rows(e[:, :]), ALU.mult))
            nc.vector.tensor_copy(agg[:, :, 0:1], cosh[:, :].unsqueeze(2)).then_inc(s["out_ready"], 1)
            dve.wait_ge(s["biased"], 1)

            def chunk(c):
                dve.wait_ge(s["mlp"], c + 1)
                tiles = slice(0, TPB) if isinstance(c, int) else bass.ds(c * TPB, TPB)
                part = x[:, tiles, :].rearrange("p t d -> p (t d)")
                nc.vector.tensor_tensor(part, mlp[:, :], part, ALU.add).then_inc(s["added"], 1)

            chunk(0)
            with dve.Fori(1, NCH) as c:
                chunk(c)



def layer1_features(nc, g, x_dram, beta):
    with ExitStack() as mem:
        x = mem.enter_context(nc.sbuf_tensor("f1_x", [P, NT, D], F32))
        sq = mem.enter_context(nc.sbuf_tensor("f1_sq", [P, NT, D], F32))
        mean, var, n = (mem.enter_context(nc.sbuf_tensor(f"f1_{k}", [P, NT], F32)) for k in ("mean", "var", "n"))
        tp = [mem.enter_context(nc.psum_tensor(f"f1_tp{b}", [P, BANK], F32)) for b in range(4)]
        s = sems(nc, mem, "f1", "x_in beta_in centered squared var std chain rows norm2 norm clamped log unit diag "
                                "transposed copied spread spread_out")
        h = g.rows
        block = mem.enter_context(nc.Block())

        @block.sync
        def _(sp):
            sp.dma_start(x[:, :, :], row_tiles(x_dram)).then_inc(s["x_in"], 16)
            sp.dma_start(g.half_beta[:, :], beta.partition_broadcast(P)).then_inc(s["beta_in"], 16)

        @block.vector
        def _(dve):
            link = Link(dve, s["chain"])
            dve.wait_ge(s["beta_in"], 16)
            link(nc.vector.tensor_scalar(g.half_beta[:, :], g.half_beta[:, :], 0.5, None, ALU.mult))
            dve.wait_ge(s["x_in"], 16)
            layer_norm_dve(nc, dve, link, s, x, h, sq, mean, var)
            nc.vector.tensor_copy(mean[:, 0:1], var[:, 0:1]).then_inc(s["rows"], 1)
            dve.wait_ge(s["squared"], 2)
            nc.vector.tensor_reduce(n[:, :], sq[:, :, :], X_AXIS, ALU.add).then_inc(s["norm2"], 1)
            dve.wait_ge(s["norm"], 1)
            nc.vector.tensor_scalar(n[:, :], n[:, :], TINY_NORM, None, ALU.max).then_inc(s["clamped"], 1)
            dve.wait_ge(s["clamped"], 1)
            link(nc.vector.reciprocal(var[:, :], n[:, :]))
            nc.vector.tensor_tensor(sq[:, :, :], h[:, :, :], over_rows(var[:, :]), ALU.mult).then_inc(s["unit"], 1)
            dve.wait_ge(s["log"], 1)
            link(nc.vector.tensor_scalar(g.half_log[:, :], mean[:, :], -LOG_EPS, 0.5, ALU.add, ALU.mult))
            nc.vector.tensor_tensor(x[:, :, :], g.identity[:, :].unsqueeze(1).to_broadcast([P, NT, D]),
                                    over_rows(mean[:, :]), ALU.mult).then_inc(s["diag"], 1)

        @block.scalar
        def _(act):
            layer_norm_act(nc, act, s, h, sq, var)
            act.wait_ge(s["rows"], 1)
            nc.scalar.activation(sq[:, :, :], h[:, :, :], ACT.Square).then_inc(s["squared"], 1)
            act.wait_ge(s["norm2"], 1)
            nc.scalar.activation(n[:, :], n[:, :], ACT.Sqrt).then_inc(s["norm"], 1)
            act.wait_ge(s["clamped"], 1)
            nc.scalar.activation(mean[:, :], n[:, :], ACT.Ln).then_inc(s["log"], 1)
            transpose_rows_act(nc, act, lambda c: g.unit_t[:, ts(c, BANK)], tp, s["transposed"], s["copied"])
            transpose_rows_act(nc, act, lambda c: g.log_row[:, ts(c, BANK)], tp, s["spread"], s["spread_out"])

        @block.tensor
        def _(pe):
            pe.wait_ge(s["unit"], 1)
            transpose_rows_pe(nc, pe, lambda t: sq[:, t, :], tp, g.identity[:, :], s["transposed"], s["copied"])
            pe.wait_ge(s["diag"], 1)
            pe.wait_ge(s["copied"], NCH)
            for c in range(NCH):
                if c >= len(tp):
                    pe.wait_ge(s["spread_out"], c - len(tp) + 1)
                nc.tensor.matmul(tp[c % len(tp)][:, :], g.ones[:, :], x[:, ts(c, TPB), :].rearrange("p t d -> p (t d)"),
                                 start=True, stop=True).then_inc(s["spread"], 1)


def layer2_features(nc, g, x_dram, w, a_self, a_neigh):
    with ExitStack() as mem:
        x = mem.enter_context(nc.sbuf_tensor("f2_x", [P, NT, D], F32))
        sq = mem.enter_context(nc.sbuf_tensor("f2_sq", [P, NT, D], F32))
        h = mem.enter_context(nc.sbuf_tensor("f2_h", [P, NT, D], F32))
        h_t = mem.enter_context(nc.sbuf_tensor("f2_ht", [P, N], F32))
        mean, var = (mem.enter_context(nc.sbuf_tensor(f"f2_{k}", [P, NT], F32)) for k in ("mean", "var"))
        w_sb = mem.enter_context(nc.sbuf_tensor("f2_w", [P, D + H2], F32))
        a_sb = mem.enter_context(nc.sbuf_tensor("f2_a", [P, 2, D], F32))
        wa = mem.enter_context(nc.sbuf_tensor("f2_wa", [P, 2, D], F32))
        w_neigh = mem.enter_context(nc.sbuf_tensor("f2_wn", [P, H2], F32))
        w_neigh_all = mem.enter_context(nc.sbuf_tensor("f2_wna", [P, H2, P], F32))
        tp = [mem.enter_context(nc.psum_tensor(f"f2_tp{b}", [P, BANK], F32)) for b in range(4)]
        s = sems(nc, mem, "f2", "x_in w_in centered squared var std chain rows weights transposed copied projected "
                                "projected_out spread spread_out")
        block = mem.enter_context(nc.Block())

        @block.sync
        def _(sp):
            sp.dma_start(x[:, :, :], row_tiles(x_dram)).then_inc(s["x_in"], 16)
            sp.dma_start(w_sb[:, 0:D].rearrange("p (h d) -> p h d", h=H2), w.rearrange("h f d -> f h d")).then_inc(s["w_in"], 16)
            sp.dma_start(a_sb[:, 0, :], a_self.rearrange("h d -> (h d)").partition_broadcast(P)).then_inc(s["w_in"], 16)
            sp.dma_start(a_sb[:, 1, :], a_neigh.rearrange("h d -> (h d)").partition_broadcast(P)).then_inc(s["w_in"], 16)

        @block.vector
        def _(dve):
            link = Link(dve, s["chain"])
            dve.wait_ge(s["w_in"], 48)
            for k, dst in ((0, w_sb[:, D:D + H2]), (1, w_neigh[:, :])):
                link(nc.vector.tensor_tensor(wa[:, k, :], w_sb[:, 0:D], a_sb[:, k, :], ALU.mult))
                link(nc.vector.tensor_reduce(dst, wa[:, k, :].rearrange("p (h d) -> p h d", h=H2), X_AXIS, ALU.add))
            for k in range(H2):
                nc.vector.tensor_scalar(w_neigh_all[:, k, :], g.ones[:, :], w_neigh[:, k:k + 1], None,
                                        ALU.mult).then_inc(s["weights"], 1)
            dve.wait_ge(s["x_in"], 16)
            layer_norm_dve(nc, dve, link, s, x, h, sq, mean, var)
            nc.vector.tensor_copy(mean[:, 0:1], var[:, 0:1]).then_inc(s["rows"], 1)

        @block.scalar
        def _(act):
            layer_norm_act(nc, act, s, h, sq, var)
            transpose_rows_act(nc, act, lambda c: h_t[:, ts(c, BANK)], tp, s["transposed"], s["copied"])
            for t in range(NT):
                act.wait_ge(s["projected"], t + 1)
                nc.scalar.copy(g.rows[:, t, :], tp[t % 4][:, 0:D])
                nc.scalar.copy(g.self_col[:, t, :], tp[t % 4][:, D:D + H2]).then_inc(s["projected_out"], 1)
            transpose_rows_act(nc, act, lambda c: g.neigh_row[:, c // NCH, ts(c % NCH, BANK)], tp, s["spread"], s["spread_out"])
            for c in range(NCH, H2 * NCH):
                act.wait_ge(s["spread"], c + 1)
                nc.scalar.copy(g.neigh_row[:, c // NCH, ts(c % NCH, BANK)], tp[c % 4][:, :]).then_inc(s["spread_out"], 1)

        @block.tensor
        def _(pe):
            pe.wait_ge(s["rows"], 1)
            transpose_rows_pe(nc, pe, lambda t: h[:, t, :], tp, g.identity[:, :], s["transposed"], s["copied"])
            pe.wait_ge(s["copied"], NCH)
            pe.wait_ge(s["weights"], H2)
            for t in range(NT):
                if t >= 4:
                    pe.wait_ge(s["projected_out"], t - 3)
                nc.tensor.matmul(tp[t % 4][:, 0:D + H2], h_t[:, ts(t, P)], w_sb[:, :], start=True, stop=True).then_inc(s["projected"], 1)
            pe.wait_ge(s["projected_out"], NT)
            for c in range(H2 * NCH):
                if c >= 4:
                    pe.wait_ge(s["spread_out"], c - 3)
                nc.tensor.matmul(tp[c % 4][:, :], w_neigh_all[:, c // NCH, :], h_t[:, ts(c % NCH, BANK)],
                                 start=True, stop=True).then_inc(s["spread"], 1)


def masked_attention(nc, g, layer, adj, x_dram, x_next_dram, bias=None):
    heads = 1 if layer == 1 else H2
    UN = 4
    GT = UN // heads
    NG = NT // GT
    TPN = 2 if layer == 1 else 4
    TB = NT // TPB
    SCH = 2 * BANK
    NS = N // SCH
    with ExitStack() as mem:
        adj_sb = [mem.enter_context(nc.sbuf_tensor(f"m{layer}_adj{b}", [P, N], F32)) for b in range(2)]
        part = mem.enter_context(nc.sbuf_tensor(f"m{layer}_part", [P, N], F32))
        score = [mem.enter_context(nc.sbuf_tensor(f"m{layer}_score{b}", [P, N], F32)) for b in range(2)]
        probs = mem.enter_context(nc.sbuf_tensor(f"m{layer}_probs", [P, NT, BANK], F32))
        out_t = mem.enter_context(nc.sbuf_tensor(f"m{layer}_out_t", [P, GT * P], F32))
        xg = mem.enter_context(nc.sbuf_tensor(f"m{layer}_x", [P, GT, D], F32))
        top, neg_top, total, inv = (mem.enter_context(nc.sbuf_tensor(f"m{layer}_{k}", [P, UN], F32))
                                    for k in ("top", "neg_top", "total", "inv"))
        spare = mem.enter_context(nc.sbuf_tensor(f"m{layer}_spare", [P, 1], F32))
        tp = [mem.enter_context(nc.psum_tensor(f"m{layer}_tp{b}", [P, TPB, P], F32)) for b in range(TPN)]
        ps_out = mem.enter_context(nc.psum_tensor(f"m{layer}_ps_out", [P, BANK], F32))
        ps_rows = mem.enter_context(nc.psum_tensor(f"m{layer}_ps_rows", [P, BANK], F32))
        if layer == 1:
            lhs = [mem.enter_context(nc.sbuf_tensor(f"m1_lhs{b}", [P, P], F32)) for b in range(2)]
            ps_s = [mem.enter_context(nc.psum_tensor(f"m1_ps_s{b}", [P, SCH], F32)) for b in range(2)]
        else:
            val = mem.enter_context(nc.sbuf_tensor("m2_val", [P, GT, D], F32))
            low = mem.enter_context(nc.sbuf_tensor("m2_low", [P, GT, D], F32))
            bias_sb = mem.enter_context(nc.sbuf_tensor("m2_bias", [P, D], F32))
        s = sems(nc, mem, f"m{layer}", "gated masks masked neg_top exped transposed copied summed out_copied rows inv "
                 "rows_read x_in x_ready x_out " + ("lhs products part_ready" if layer == 1 else "bias_in valued lowered elu_exp"))
        adj_in = [mem.enter_context(nc.semaphore(f"m{layer}_adj_in{b}")) for b in range(2)]
        block = mem.enter_context(nc.Block())
        adj_v = adj.rearrange("(k p) j -> k p j", p=P)

        def row_tile(dram, k, n=1):
            tiles = row_tiles(dram)
            return tiles[:, k:k + n, :] if isinstance(k, int) else tiles[:, bass.ds(k, n), :]

        @block.sync
        def _(sp):
            def load(k, slot):
                src = adj_v[k] if isinstance(k, int) else adj_v[bass.ds(k, 1)].rearrange("o p j -> (o p) j")
                sp.dma_start(adj_sb[slot][:, :], src).then_inc(adj_in[slot], 16)

            def ahead(grp, r):
                sp.wait_ge(s["masked"], heads * (GT * grp + r + 1))
                load(GT * grp + r + 2, r % 2)

            if layer == 2:
                sp.dma_start(bias_sb[:, :], bias.partition_broadcast(P)).then_inc(s["bias_in"], 16)
            load(0, 0)
            load(1, 1)
            with sp.Fori(0, NG - 1) as grp:
                for r in range(GT):
                    ahead(grp, r)
            for r in range(GT - 2):
                ahead(NG - 1, r)

        @block.gpsimd
        def _(pool):
            def load(grp):
                pool.dma_start(xg[:, :, :], row_tile(x_dram, GT * grp, GT)).then_inc(s["x_in"], 16)

            def store(grp):
                pool.wait_ge(s["x_ready"], grp + 1)
                pool.dma_start(row_tile(x_next_dram, GT * grp, GT), xg[:, :, :]).then_inc(s["x_out"], 16)
                pool.wait_ge(s["x_out"], (grp + 1) * 16)

            load(0)
            with pool.Fori(0, NG - 1) as grp:
                store(grp)
                load(grp + 1)
            store(NG - 1)

        def transposes(pe, k, u, b, started):
            if b == 0:
                pe.wait_ge(s["exped"], k + 1)
            if started or b >= TPN:
                pe.wait_ge(s["copied"], k * TB + b - TPN + 1)
            for r in range(TPB):
                last = nc.tensor.transpose(tp[b % TPN][:, r, :], score[u % 2][:, ts(b * TPB + r, P)], g.identity[:, :])
            last.then_inc(s["transposed"], 1)

        def values(pe, grp):
            pe.wait_ge(s["copied"], (grp + 1) * UN * TB)
            width = BANK // heads
            for jt in range(NT):
                for h in range(heads):
                    rows = slice(h * (D // heads), (h + 1) * (D // heads))
                    last = nc.tensor.matmul(ps_out[rows, 0:width], g.rows[:, jt, rows], probs[:, jt, ts(h, width)],
                                            start=(jt == 0), stop=(jt == NT - 1))
            last.then_inc(s["summed"], 1)

        def rows_back(pe, grp):
            pe.wait_ge(s["out_copied"], grp + 1)
            pe.wait_ge(s["rows_read"], grp + 1)
            for r in range(GT):
                last = nc.tensor.transpose(ps_rows[:, ts(r, P)], out_t[:, ts(r, P)], g.identity[:, :])
            last.then_inc(s["rows"], 1)

        @block.tensor
        def _(pe):
            def unit(grp, u, first):
                k = grp * UN + u
                behind = not (first and u == 0)
                if layer == 1:
                    pe.wait_ge(s["lhs"], k + 1)
                for c in range(NS):
                    if layer == 1:
                        if behind or c >= 2:
                            pe.wait_ge(s["gated"], k * NS + c - 1)
                        for q in range(2):
                            last = nc.tensor.matmul(ps_s[c % 2][:, ts(q, BANK)], lhs[u % 2][:, :],
                                                    g.unit_t[:, ts(2 * c + q, BANK)], start=True, stop=True)
                        last.then_inc(s["products"], 1)
                    if behind:
                        for b in range(c * TB // NS, (c + 1) * TB // NS):
                            transposes(pe, k - 1, u - 1, b, not (first and u == 1))
                if u == 0 and not first:
                    values(pe, grp - 1)
                if u == 1 and not first:
                    rows_back(pe, grp - 1)

            for u in range(UN):
                unit(0, u, True)
            with pe.Fori(1, NG) as grp:
                for u in range(UN):
                    unit(grp, u, False)
            for b in range(TB):
                transposes(pe, NG * UN - 1, UN - 1, b, True)
            values(pe, NG - 1)
            rows_back(pe, NG - 1)

        @block.scalar
        def _(act):
            def softmax(k, u, first_group):
                act.wait_ge(s["neg_top"], k + 1)
                if u == 0 and not first_group:
                    act.wait_ge(s["inv"], k // UN if isinstance(k, int) else k >> 2)
                nc.scalar.activation(score[u % 2][:, :], score[u % 2][:, :], ACT.Exp, bias=neg_top[:, u:u + 1],
                                     accum_out=total[:, u:u + 1]).then_inc(s["exped"], 1)

            def copies(k, u, first_group):
                col = (u % heads) * GT + u // heads
                for b in range(TB):
                    act.wait_ge(s["transposed"], k * TB + b + 1)
                    nc.scalar.copy(probs[:, ts(b, TPB), ts(col, P)], tp[b % TPN][:, :, :]).then_inc(s["copied"], 1)

            def take_out(grp):
                act.wait_ge(s["summed"], grp + 1)
                nc.scalar.copy(out_t[:, :], ps_out[:, 0:GT * P]).then_inc(s["out_copied"], 1)

            def elu_exp(grp):
                act.wait_ge(s["lowered"], grp + 1)
                nc.scalar.activation(low[:, :, :], low[:, :, :], ACT.Exp).then_inc(s["elu_exp"], 1)

            def unit(grp, u, first):
                k = grp * UN + u
                if layer == 1:
                    tile = ts(k, P) if first else bass.ds(k * P, P)
                    row = slice(k, k + 1) if first else bass.ds(k, 1)
                    if not (first and u < 2):
                        act.wait_ge(s["products"], (k - 1) * NS)
                    nc.scalar.activation(lhs[u % 2][:, :], g.unit_t[:, tile], ACT.Identity,
                                         scale=g.half_beta[:, :]).then_inc(s["lhs"], 1)
                    if not (first and u == 0):
                        act.wait_ge(s["masked"], k)
                    nc.scalar.activation(part[:, :], g.log_row[:, :], ACT.Tanh, scale=0.5,
                                         bias=g.half_log[:, row]).then_inc(s["part_ready"], 1)
                if not (first and u == 0):
                    softmax(k - 1, (u - 1) % UN, first or (u == 0 and first))
                    if u == 1 and not first:
                        take_out(grp - 1)
                    copies(k - 1, (u - 1) % UN, first)
                if layer == 2 and u == 3 and not first:
                    elu_exp(grp - 1)

            for u in range(UN):
                unit(0, u, True)
            with act.Fori(1, NG) as grp:
                for u in range(UN):
                    unit(grp, u, False)
            softmax(NG * UN - 1, UN - 1, False)
            copies(NG * UN - 1, UN - 1, False)
            take_out(NG - 1)
            if layer == 2:
                elu_exp(NG - 1)

        @block.vector
        def _(dve):
            def invert(grp):
                dve.wait_ge(s["exped"], (grp + 1) * UN)
                nc.vector.reciprocal(inv[:, :], total[:, :]).then_inc(s["inv"], 1)

            def finish(grp):
                dve.wait_ge(s["rows"], grp + 1)
                dve.wait_ge(s["x_in"], (grp + 1) * 16)
                dve.wait_ge(s["inv"], grp + 1)
                if layer == 1:
                    for r in range(GT):
                        last = nc.vector.scalar_tensor_tensor(xg[:, r, :], ps_rows[:, ts(r, P)], inv[:, r:r + 1],
                                                              xg[:, r, :], ALU.mult, ALU.add)
                        if r == GT - 1:
                            last.then_inc(s["x_ready"], 1)
                    dve.wait_ge(s["x_ready"], grp + 1)
                    nc.vector.tensor_copy(inv[:, 0:1], inv[:, 0:1]).then_inc(s["rows_read"], 1)
                else:
                    for r in range(GT):
                        for h in range(heads):
                            cols = slice(h * DH2, (h + 1) * DH2)
                            u = r * heads + h
                            last = nc.vector.scalar_tensor_tensor(
                                val[:, r, cols], ps_rows[:, r * P + h * DH2:r * P + (h + 1) * DH2],
                                inv[:, u:u + 1], bias_sb[:, cols], ALU.mult, ALU.add)
                    last.then_inc(s["rows_read"], 1)
                    dve.wait_ge(s["rows_read"], grp + 2)
                    nc.vector.tensor_scalar(low[:, :, :], val[:, :, :], 0.0, None, ALU.min).then_inc(s["lowered"], 1)

            def finish_elu(grp):
                dve.wait_ge(s["elu_exp"], grp + 1)
                nc.vector.scalar_tensor_tensor(val[:, :, :], val[:, :, :], 0.0, low[:, :, :],
                                               ALU.max, ALU.add).then_inc(s["valued"], 1)
                dve.wait_ge(s["valued"], grp + 1)
                nc.vector.scalar_tensor_tensor(xg[:, :, :], val[:, :, :], -1.0, xg[:, :, :],
                                               ALU.add, ALU.add).then_inc(s["x_ready"], 1)

            def unit(grp, u, first):
                k = grp * UN + u
                r, h = u // heads, u % heads
                mask = adj_sb[r % 2]
                if h == 0:
                    dve.wait_ge(adj_in[r % 2], (grp * (GT // 2) + r // 2 + 1) * 16)
                    nc.vector.tensor_scalar(mask[:, :], mask[:, :], 1.0, NEG, ALU.subtract, ALU.mult).then_inc(s["masks"], 1)
                if u == 1 and not first:
                    invert(grp - 1)
                if layer == 1:
                    dve.wait_ge(s["part_ready"], k + 1)
                    for c in range(NS):
                        dve.wait_ge(s["products"], k * NS + c + 1)
                        nc.vector.scalar_tensor_tensor(part[:, ts(c, SCH)], part[:, ts(c, SCH)], 1.0, ps_s[c % 2][:, :],
                                                       ALU.add, ALU.mult).then_inc(s["gated"], 1)
                    dve.wait_ge(s["gated"], (k + 1) * NS)
                else:
                    col = GT * grp + r
                    this = slice(col, col + 1) if first else bass.ds(col, 1)
                    nc.vector.tensor_scalar(part[:, :], g.neigh_row[:, h, :],
                                            g.self_col[:, this, h], None, ALU.add).then_inc(s["gated"], 1)
                    dve.wait_ge(s["gated"], k + 1)
                dve.wait_ge(s["masks"], GT * grp + r + 1)
                if not (first and u < 2):
                    dve.wait_ge(s["transposed"], (k - 1) * TB)
                nc.vector.memset(spare[:, :], 0.0)
                nc.vector.tensor_tensor_reduce(out=score[u % 2][:, :], in0=part[:, :], in1=mask[:, :], scale=1.0,
                                               scalar=LOWEST, op0=ALU.add, op1=ALU.max,
                                               accum_out=top[:, u:u + 1]).then_inc(s["masked"], 1)
                dve.wait_ge(s["masked"], k + 1)
                nc.vector.tensor_scalar(neg_top[:, u:u + 1], top[:, u:u + 1], -1.0, None, ALU.mult).then_inc(s["neg_top"], 1)
                if u == 2 and not first:
                    finish(grp - 1)
                if layer == 2 and u == 3 and not first:
                    finish_elu(grp - 1)

            if layer == 2:
                dve.wait_ge(s["bias_in"], 16)
            dve.sem_inc(s["rows_read"], 1)
            for u in range(UN):
                unit(0, u, True)
            with dve.Fori(1, NG) as grp:
                for u in range(UN):
                    unit(grp, u, False)
            invert(NG - 1)
            finish(NG - 1)
            if layer == 2:
                finish_elu(NG - 1)



def layer3_features(nc, g, x_dram, w, a_src, a_tgt, proj_dram, src_dram):
    with ExitStack() as mem:
        x = mem.enter_context(nc.sbuf_tensor("f3_x", [P, NT, D], F32))
        sq = mem.enter_context(nc.sbuf_tensor("f3_sq", [P, NT, D], F32))
        h = mem.enter_context(nc.sbuf_tensor("f3_h", [P, NT, D], F32))
        mean, var = (mem.enter_context(nc.sbuf_tensor(f"f3_{k}", [P, NT], F32)) for k in ("mean", "var"))
        w_sb = mem.enter_context(nc.sbuf_tensor("f3_w", [P, H3, D], F32))
        a_sb = mem.enter_context(nc.sbuf_tensor("f3_a", [P, 2, H3, D], F32))
        wa = mem.enter_context(nc.sbuf_tensor("f3_wa", [P, 2, H3, D], F32))
        w_a = mem.enter_context(nc.sbuf_tensor("f3_w_a", [P, 2, H3], F32))
        proj = [mem.enter_context(nc.sbuf_tensor(f"f3_proj{b}", [P, H3 * D], F32)) for b in range(4)]
        src = mem.enter_context(nc.sbuf_tensor("f3_src", [H3, N], F32))
        tp = [mem.enter_context(nc.psum_tensor(f"f3_tp{b}", [P, BANK], F32)) for b in range(4)]
        ps_tgt = mem.enter_context(nc.psum_tensor("f3_ps_tgt", [P, NT, H3], F32))
        s = sems(nc, mem, "f3", "x_in w_in centered squared var std chain rows weights transposed copied projected "
                                "projected_out sources sources_out src_stored")
        stored = [mem.enter_context(nc.semaphore(f"f3_stored{b}")) for b in range(4)]
        block = mem.enter_context(nc.Block())

        @block.sync
        def _(sp):
            sp.dma_start(x[:, :, :], row_tiles(x_dram)).then_inc(s["x_in"], 16)
            sp.dma_start(w_sb[:, :, :], w.rearrange("h f o -> f h o")).then_inc(s["w_in"], 16)
            for k, a in ((0, a_src), (1, a_tgt)):
                sp.dma_start(a_sb[:, k, :, :].rearrange("p h o -> p (h o)"),
                             a.rearrange("h o -> (h o)").partition_broadcast(P)).then_inc(s["w_in"], 16)
            for t in range(NT):
                sp.wait_ge(s["projected_out"], t + 1)
                sp.dma_start(proj_dram[ts(t, P), :], proj[t % 4][:, :]).then_inc(stored[t % 4], 16)
            sp.wait_ge(s["sources_out"], NCH)
            sp.dma_start(src_dram, src[:, :]).then_inc(s["src_stored"], 16)
            sp.wait_ge(s["src_stored"], 16)
            for b in range(4):
                sp.wait_ge(stored[b], 16 * NT // 4)

        @block.vector
        def _(dve):
            link = Link(dve, s["chain"])
            dve.wait_ge(s["w_in"], 48)
            for k in range(2):
                link(nc.vector.tensor_tensor(wa[:, k, :, :], w_sb[:, :, :], a_sb[:, k, :, :], ALU.mult))
                nc.vector.tensor_reduce(w_a[:, k, :], wa[:, k, :, :], X_AXIS, ALU.add).then_inc(s["weights"], 1)
            dve.wait_ge(s["x_in"], 16)
            layer_norm_dve(nc, dve, link, s, x, h, sq, mean, var)
            nc.vector.tensor_copy(mean[:, 0:1], var[:, 0:1]).then_inc(s["rows"], 1)
            dve.wait_ge(s["projected"], NT)
            nc.vector.tensor_copy(g.tgt[:, :, :], ps_tgt[:, :, :].rearrange("p t h -> p h t"))
            nc.vector.tensor_scalar(g.tgt_sloped[:, :, :], ps_tgt[:, :, :].rearrange("p t h -> p h t"), SLOPE, None, ALU.mult)

        @block.scalar
        def _(act):
            layer_norm_act(nc, act, s, h, sq, var)
            transpose_rows_act(nc, act, lambda c: g.h_t[:, ts(c, BANK)], tp, s["transposed"], s["copied"])
            for c in range(NCH):
                act.wait_ge(s["sources"], c + 1)
                nc.scalar.copy(src[:, ts(c, BANK)], tp[c % 4][0:H3, :]).then_inc(s["sources_out"], 1)
            for t in range(NT):
                act.wait_ge(s["projected"], t + 1)
                if t >= 4:
                    act.wait_ge(stored[t % 4], 16 * (t // 4))
                nc.scalar.copy(proj[t % 4][:, :], tp[t % 4][:, :]).then_inc(s["projected_out"], 1)

        @block.tensor
        def _(pe):
            pe.wait_ge(s["rows"], 1)
            transpose_rows_pe(nc, pe, lambda t: h[:, t, :], tp, g.identity[:, :], s["transposed"], s["copied"])
            pe.wait_ge(s["copied"], NCH)
            pe.wait_ge(s["weights"], 2)
            for c in range(NCH):
                if c >= 4:
                    pe.wait_ge(s["sources_out"], c - 3)
                nc.tensor.matmul(tp[c % 4][0:H3, :], w_a[:, 0, :], g.h_t[:, ts(c, BANK)],
                                 start=True, stop=True).then_inc(s["sources"], 1)
            pe.wait_ge(s["sources_out"], NCH)
            for t in range(NT):
                if t >= 4:
                    pe.wait_ge(s["projected_out"], t - 3)
                nc.tensor.matmul(ps_tgt[:, t, :], g.h_t[:, ts(t, P)], w_a[:, 1, :], start=True, stop=True)
                nc.tensor.matmul(tp[t % 4][:, :], g.h_t[:, ts(t, P)], w_sb[:, :, :].rearrange("p h o -> p (h o)"),
                                 start=True, stop=True).then_inc(s["projected"], 1)


def layer3_attention(nc, g, adj_t, proj_dram, src_dram):
    UN = 4
    NG = NT // UN
    with ExitStack() as mem:
        src = mem.enter_context(nc.sbuf_tensor("e_src", [P, 2, N], F32))
        adj_sb = [mem.enter_context(nc.sbuf_tensor(f"e_adj{b}", [P, N], F32)) for b in range(2)]
        e = [mem.enter_context(nc.sbuf_tensor(f"e_e{b}", [P, N], F32)) for b in range(UN)]
        v = mem.enter_context(nc.sbuf_tensor("e_v", [P, 2, UN, D], F32))
        scaled = [mem.enter_context(nc.sbuf_tensor(f"e_scaled{b}", [P, D], F32)) for b in range(UN)]
        val = mem.enter_context(nc.sbuf_tensor("e_val", [P, N], F32))
        low = mem.enter_context(nc.sbuf_tensor("e_low", [P, N], F32))
        acc = g.acc
        top, neg_top, total, inv = (mem.enter_context(nc.sbuf_tensor(f"e_{k}", [P, UN], F32))
                                    for k in ("top", "neg_top", "total", "inv"))
        spare = mem.enter_context(nc.sbuf_tensor("e_spare", [P, 1], F32))
        ps = mem.enter_context(nc.psum_tensor("e_ps", [P, NCH, BANK], F32))
        s = sems(nc, mem, "e", "src_in v_in sloped leaky masked neg_top exped inv scaled multiplied taken lowered elu_exp "
                               "valued acc_ready")
        adj_in = [mem.enter_context(nc.semaphore(f"e_adj_in{b}")) for b in range(2)]
        block = mem.enter_context(nc.Block())
        adj_v = adj_t.rearrange("(k p) i -> k p i", p=P)
        proj_v = proj_dram.rearrange("(q t p) (h o) -> h q p t o", t=UN, p=P, h=H3)

        def heads_and_groups(eng, head):
            head(0, True)
            with eng.Fori(1, H3) as h:
                head(h, False)

        @block.sync
        def _(sp):
            def load(k, slot):
                src_ap = adj_v[k] if isinstance(k, int) else adj_v[bass.ds(k, 1)].rearrange("o p i -> (o p) i")
                sp.dma_start(adj_sb[slot][:, :], src_ap).then_inc(adj_in[slot], 16)

            def load_src(h, slot):
                row = src_dram[h:h + 1, :] if isinstance(h, int) else src_dram[bass.ds(h, 1), :]
                sp.dma_start(src[:, slot, :], row.rearrange("o n -> (o n)").partition_broadcast(P)).then_inc(s["src_in"], 16)

            load_src(0, 0)
            load(0, 0)
            load(1, 1)
            sp.wait_ge(s["src_in"], 16)
            load_src(1, 1)
            for k in range(2, NT):
                sp.wait_ge(s["masked"], k - 1)
                load(k, k % 2)

            def head(h, last):
                if not last:
                    sp.wait_ge(s["leaky"], h * NT)
                    sp.wait_ge(s["src_in"], (h + 1) * 16)
                    slots = src[:, bass.ds((h + 1) % 2, 1), :].rearrange("p o n -> p (o n)")
                    sp.dma_start(slots, src_dram[bass.ds(h + 1, 1), :].rearrange("o n -> (o n)").partition_broadcast(P)
                                 ).then_inc(s["src_in"], 16)
                with sp.Fori(0, NT // 2) as m:
                    for b in range(2):
                        sp.wait_ge(s["masked"], h * NT + m * 2 + b - 1)
                        load(m * 2 + b, b)

            with sp.Fori(1, H3 - 1) as h:
                head(h, False)
            head(H3 - 1, True)

        @block.gpsimd
        def _(pool):
            def load(h, q, slot):
                rows = proj_v[h, q] if isinstance(h, int) and isinstance(q, int) else \
                    proj_v[(slice(h, h + 1) if isinstance(h, int) else bass.ds(h, 1)),
                           (slice(q, q + 1) if isinstance(q, int) else bass.ds(q, 1))].rearrange("a b p t o -> (a b p) t o")
                pool.dma_start(v[:, slot, :, :], rows).then_inc(s["v_in"], 16)

            load(0, 0, 0)
            pool.wait_ge(s["v_in"], 16)
            load(0, 1, 1)

            def group(h, q):
                g_at = h * NG + q
                pool.wait_ge(s["scaled"], g_at * UN - UN)
                pool.wait_ge(s["v_in"], g_at * 16)
                rows = proj_v[(slice(h, h + 1) if isinstance(h, int) else bass.ds(h, 1)),
                              bass.ds(q, 1)].rearrange("a b p t o -> (a b p) t o")
                pool.dma_start(v[:, bass.ds(q % 2, 1), :, :].rearrange("p a t o -> p (a t) o"), rows).then_inc(s["v_in"], 16)

            with pool.Fori(2, NG) as q:
                group(0, q)
            with pool.Fori(1, H3) as h:
                with pool.Fori(0, NG) as q:
                    group(h, q)

        @block.tensor
        def _(pe):
            def group(h, q, first_head, first_group):
                for u in range(UN):
                    k = h * NT + q * UN + u
                    begin = first_group and u == 0
                    pe.wait_ge(s["scaled"], k + 1)
                    for c in range(NCH):
                        if begin and not first_head:
                            pe.wait_ge(s["taken"], (h - 1) * NCH + c + 1)
                        if first_group:
                            mm = nc.tensor.matmul(ps[:, c, :], scaled[u][:, :], e[u][:, ts(c, BANK)],
                                                  start=begin, stop=False, skip_group_check=True)
                        else:
                            mm = nc.tensor.matmul(ps[:, c, :], scaled[u][:, :], e[u][:, ts(c, BANK)],
                                                  start=False, stop=(u == UN - 1), skip_group_check=True)
                    mm.then_inc(s["multiplied"], 1)

            def head(h, first):
                group(h, 0, first, True)
                with pe.Fori(1, NG) as q:
                    group(h, q, first, False)

            heads_and_groups(pe, head)

        @block.scalar
        def _(act):
            def softmax(k, u):
                act.wait_ge(s["neg_top"], k + 1)
                nc.scalar.activation(e[u][:, :], e[u][:, :], ACT.Exp, bias=neg_top[:, u:u + 1],
                                     accum_out=total[:, u:u + 1]).then_inc(s["exped"], 1)

            def group(h, q, first_head, first_group):
                for u in range(UN):
                    k = h * NT + q * UN + u
                    start = first_head and first_group
                    if first_group and u == 0:
                        act.wait_ge(s["src_in"], (h + 1) * 16)
                    if not start:
                        act.wait_ge(s["multiplied"], k - UN + 1)
                    col = g.tgt_sloped[:, :, :].rearrange("p h t -> p (h t)")
                    col = col[:, k:k + 1] if start else col[:, bass.ds(k, 1)]
                    row = src[:, 0, :] if first_head else src[:, bass.ds(h % 2, 1), :].rearrange("p o n -> p (o n)")
                    nc.scalar.activation(e[u][:, :], row, ACT.Identity, scale=SLOPE, bias=col).then_inc(s["sloped"], 1)
                    if not (start and u == 0):
                        softmax(k - 1, (u - 1) % UN)
                    if first_group and u == UN - 1 and not first_head:
                        elu_exp(h - 1)

            def elu_exp(h):
                act.wait_ge(s["lowered"], h + 1)
                nc.scalar.activation(low[:, :], low[:, :], ACT.Exp).then_inc(s["elu_exp"], 1)

            def head(h, first):
                group(h, 0, first, True)
                with act.Fori(1, NG) as q:
                    group(h, q, first, False)

            heads_and_groups(act, head)
            softmax(H3 * NT - 1, UN - 1)
            elu_exp(H3 - 1)

        @block.vector
        def _(dve):
            def scale(h, q, k, u):
                dve.wait_ge(s["exped"], k + 1)
                nc.vector.reciprocal(inv[:, u:u + 1], total[:, u:u + 1]).then_inc(s["inv"], 1)
                dve.wait_ge(s["v_in"], (h * NG + q + 1) * 16)
                dve.wait_ge(s["inv"], k + 1)
                rows = v[:, q % 2, u, :] if isinstance(q, int) else \
                    v[:, bass.ds(q % 2, 1), u, :].rearrange("p o d -> p (o d)")
                nc.vector.tensor_scalar(scaled[u][:, :], rows, inv[:, u:u + 1], None, ALU.mult).then_inc(s["scaled"], 1)

            def take(h):
                dve.wait_ge(s["multiplied"], (h + 1) * NT)
                for c in range(NCH):
                    nc.vector.tensor_tensor(val[:, ts(c, BANK)], ps[:, c, :], g.h_t[:, ts(c, BANK)],
                                            ALU.add).then_inc(s["taken"], 1)

            def lower(h):
                dve.wait_ge(s["taken"], (h + 1) * NCH)
                nc.vector.tensor_scalar(low[:, :], val[:, :], 0.0, None, ALU.min).then_inc(s["lowered"], 1)

            def add_elu(h):
                dve.wait_ge(s["elu_exp"], h + 1)
                nc.vector.scalar_tensor_tensor(val[:, :], val[:, :], 0.0, low[:, :], ALU.max, ALU.add).then_inc(s["valued"], 1)
                dve.wait_ge(s["valued"], h + 1)
                dve.wait_ge(s["acc_ready"], h + 1)
                nc.vector.scalar_tensor_tensor(acc[:, :], val[:, :], -1.0, acc[:, :], ALU.add, ALU.add).then_inc(s["acc_ready"], 1)

            def group(h, q, first_head, first_group):
                for u in range(UN):
                    k = h * NT + q * UN + u
                    dve.wait_ge(adj_in[u % 2], (k // 2 + 1) * 16 if isinstance(k, int) else
                                (h * (NT // 2) + q * (UN // 2) + u // 2 + 1) * 16)
                    dve.wait_ge(s["sloped"], k + 1)
                    start = first_head and first_group
                    col = g.tgt[:, :, :].rearrange("p h t -> p (h t)")
                    col = col[:, k:k + 1] if start else col[:, bass.ds(k, 1)]
                    row = src[:, 0, :] if first_head else src[:, bass.ds(h % 2, 1), :].rearrange("p o n -> p (o n)")
                    nc.vector.scalar_tensor_tensor(e[u][:, :], row, col, e[u][:, :], ALU.add, ALU.max).then_inc(s["leaky"], 1)
                    dve.wait_ge(s["leaky"], k + 1)
                    nc.vector.memset(spare[:, :], 0.0)
                    nc.vector.tensor_tensor_reduce(out=e[u][:, :], in0=e[u][:, :], in1=adj_sb[u % 2][:, :], scale=1.0,
                                                   scalar=LOWEST, op0=ALU.add, op1=ALU.max,
                                                   accum_out=top[:, u:u + 1]).then_inc(s["masked"], 1)
                    dve.wait_ge(s["masked"], k + 1)
                    nc.vector.tensor_scalar(neg_top[:, u:u + 1], top[:, u:u + 1], -1.0, None, ALU.mult).then_inc(s["neg_top"], 1)
                    boundary = first_group and not first_head
                    if boundary and u == 1:
                        take(h - 1)
                    if boundary and u == 2:
                        lower(h - 1)
                    if not (first_head and first_group and u == 0):
                        if u > 0:
                            scale(h, q, k - 1, u - 1)
                        elif first_group:
                            scale(h - 1, NG - 1, k - 1, UN - 1)
                        else:
                            scale(h, q - 1, k - 1, UN - 1)
                if first_group and not first_head:
                    add_elu(h - 1)

            def head(h, first):
                group(h, 0, first, True)
                with dve.Fori(1, NG) as q:
                    group(h, q, first, False)

            nc.vector.memset(acc[:, :], 0.0).then_inc(s["acc_ready"], 1)
            heads_and_groups(dve, head)
            scale(H3 - 1, NG - 1, H3 * NT - 1, UN - 1)
            take(H3 - 1)
            lower(H3 - 1)
            add_elu(H3 - 1)


def layer3_output(nc, g, x_dram, out):
    with ExitStack() as mem:
        x = mem.enter_context(nc.sbuf_tensor("o_x", [P, NT, D], F32))
        tp = [mem.enter_context(nc.psum_tensor(f"o_tp{b}", [P, BANK], F32)) for b in range(4)]
        s = sems(nc, mem, "o", "x_in transposed added x_out")
        block = mem.enter_context(nc.Block())

        @block.sync
        def _(sp):
            sp.dma_start(x[:, :, :], row_tiles(x_dram)).then_inc(s["x_in"], 16)
            for c in range(NCH):
                sp.wait_ge(s["added"], c + 1)
                sp.dma_start(row_tiles(out)[:, ts(c, TPB), :], x[:, ts(c, TPB), :]).then_inc(s["x_out"], 16)
            sp.wait_ge(s["x_out"], 16 * NCH)

        @block.tensor
        def _(pe):
            transpose_rows_pe(nc, pe, lambda t: g.acc[:, ts(t, P)], tp, g.identity[:, :], s["transposed"], s["added"])

        @block.vector
        def _(dve):
            dve.wait_ge(s["x_in"], 16)
            for c in range(NCH):
                dve.wait_ge(s["transposed"], c + 1)
                part = x[:, ts(c, TPB), :].rearrange("p t d -> p (t d)")
                nc.vector.scalar_tensor_tensor(part, tp[c % 4][:, :], 1.0 / H3, part, ALU.mult, ALU.add).then_inc(s["added"], 1)


def build(nc, x, adj, w, out):
    adj_t = nc.dram_tensor("adj_t", [N, N], F32, kind="Internal").ap()
    proj = nc.dram_tensor("proj", [N, H3 * D], F32, kind="Internal").ap()
    src = nc.dram_tensor("src", [H3, N], F32, kind="Internal").ap()
    x1, x2, x3 = (nc.dram_tensor(f"x{k}", [N, D], F32, kind="Internal").ap() for k in (1, 2, 3))
    first_sem = next_semaphore(nc)
    with ExitStack() as mem:
        g = Shared()
        g.identity = mem.enter_context(nc.sbuf_tensor("identity", [P, P], F32))
        g.ones = mem.enter_context(nc.sbuf_tensor("ones", [P, P], F32))
        with nc.sbuf_tensor("rows", [P, NT, D], F32) as rows:
            g.rows = rows
            layer0_features(nc, g, x)
            with nc.sbuf_tensor("agg_t", [P, N], F32) as agg_t:
                g.agg_t = agg_t
                layer0_aggregate(nc, g, adj, adj_t)
                layer0_combine(nc, g, w["L0_gnn_W1"], w["L0_gnn_b1"], w["L0_gnn_W2"], w["L0_gnn_b2"], x, x1)
            with ExitStack() as m1:
                g.unit_t = m1.enter_context(nc.sbuf_tensor("unit_t", [P, N], F32))
                g.log_row = m1.enter_context(nc.sbuf_tensor("log_row", [P, N], F32))
                g.half_log = m1.enter_context(nc.sbuf_tensor("half_log", [P, NT], F32))
                g.half_beta = m1.enter_context(nc.sbuf_tensor("half_beta", [P, 1], F32))
                layer1_features(nc, g, x1, w["L1_gnn_beta"])
                masked_attention(nc, g, 1, adj, x1, x2)
            clear_semaphores(nc, first_sem, next_semaphore(nc))
            with ExitStack() as m2:
                g.neigh_row = m2.enter_context(nc.sbuf_tensor("neigh_row", [P, H2, N], F32))
                g.self_col = m2.enter_context(nc.sbuf_tensor("self_col", [P, NT, H2], F32))
                layer2_features(nc, g, x2, w["L2_gnn_W"], w["L2_gnn_a_self"], w["L2_gnn_a_neigh"])
                masked_attention(nc, g, 2, adj, x2, x3, bias=w["L2_gnn_bias"])
        g.h_t = mem.enter_context(nc.sbuf_tensor("h_t", [P, N], F32))
        g.tgt = mem.enter_context(nc.sbuf_tensor("tgt", [P, H3, NT], F32))
        g.tgt_sloped = mem.enter_context(nc.sbuf_tensor("tgt_sloped", [P, H3, NT], F32))
        g.acc = mem.enter_context(nc.sbuf_tensor("acc", [P, N], F32))
        layer3_features(nc, g, x3, w["L3_gnn_W"], w["L3_gnn_a_src"], w["L3_gnn_a_tgt"], proj, src)
        layer3_attention(nc, g, adj_t, proj, src)
        layer3_output(nc, g, x3, out)


_INS = ['x', 'adj', 'L0_gnn_W1', 'L0_gnn_b1', 'L0_gnn_W2', 'L0_gnn_b2', 'L1_gnn_beta', 'L2_gnn_W', 'L2_gnn_a_self',
        'L2_gnn_a_neigh', 'L2_gnn_bias', 'L3_gnn_W', 'L3_gnn_a_src', 'L3_gnn_a_tgt']


def kernel(**inputs):
    import numpy as _np
    import concourse.bacc as _bacc
    from concourse import mybir as _mybir
    from concourse.bass_utils import run_bass_kernel_spmd as _run

    nc = _bacc.Bacc("TRN2", target_bir_lowering=False, num_devices=1)
    arrays, args = {}, {}
    for name in _INS:
        a = _np.ascontiguousarray(inputs[name])
        arrays[f"in_{name}_dram"] = a
        args[name] = nc.dram_tensor(f"in_{name}_dram", a.shape, _mybir.dt.from_np(a.dtype), kind="ExternalInput").ap()
    out = nc.dram_tensor("out_0_dram", (N, D), _mybir.dt.float32, kind="ExternalOutput").ap()
    build(nc, args["x"], args["adj"], args, out)
    r = _run(nc, [arrays], core_ids=[0])
    return r.results[0]["out_0_dram"]
```

```python
from contextlib import ExitStack

import numpy as np

import concourse.bass as bass
import concourse.mybir as mybir

F32 = mybir.dt.float32
ALU = mybir.AluOpType
ACT = mybir.ActivationFunctionType
X_AXIS = mybir.AxisListType.X

P = 128
N = 4096
D = 128
HID = 256
NT = N // P
BANK = 512
TPB = BANK // P
NCH = N // BANK
H2, DH2 = 2, 64
H3 = 4
LN_EPS = 1e-5
MIN_NORM = 1e-7
NEG = 1e9
SLOPE = 0.2
_Z0 = float(np.float32(1.0) + np.float32(MIN_NORM))
THETA_MIN = float(np.log(_Z0 + np.sqrt(_Z0 * _Z0 - 1.0)))


TINY_NORM = 1e-18
LOG_EPS = float(np.log(1e-7))
HIGHEST = float(np.finfo(np.float32).max)


class Shared:
    pass


def ts(i, n):
    return slice(i * n, (i + 1) * n)


class Link:

    def __init__(self, eng, sem):
        self.eng, self.sem, self.n = eng, sem, 0

    def __call__(self, ins):
        self.n += 1
        ins.then_inc(self.sem, 1)
        self.eng.wait_ge(self.sem, self.n)


def over_rows(col, n=NT):
    return col.unsqueeze(2).to_broadcast([P, n, D])


def row_tiles(dram):
    return dram.rearrange("(t p) d -> p t d", p=P)



def layer_norm_dve(nc, dve, link, s, rows, h, sq, mean, var):
    link(nc.vector.tensor_reduce(mean[:, :], rows[:, :, :], X_AXIS, ALU.add))
    link(nc.vector.tensor_scalar(mean[:, :], mean[:, :], 1.0 / D, None, ALU.mult))
    nc.vector.tensor_tensor(h[:, :, :], rows[:, :, :], over_rows(mean[:, :]),
                            ALU.subtract).then_inc(s["centered"], 1)
    dve.wait_ge(s["squared"], 1)
    link(nc.vector.tensor_reduce(var[:, :], sq[:, :, :], X_AXIS, ALU.add))
    nc.vector.tensor_scalar(var[:, :], var[:, :], 1.0 / D, LN_EPS, ALU.mult, ALU.add).then_inc(s["var"], 1)
    dve.wait_ge(s["std"], 1)
    link(nc.vector.reciprocal(var[:, :], var[:, :]))
    dve.wait_ge(s["centered"], 1)
    link(nc.vector.tensor_tensor(h[:, :, :], h[:, :, :], over_rows(var[:, :]), ALU.mult))
    link(nc.vector.tensor_scalar(h[:, :, :], h[:, :, :], 0.0, None, ALU.max))


def layer_norm_act(nc, act, s, h, sq, var):
    act.wait_ge(s["centered"], 1)
    nc.scalar.activation(sq[:, :, :], h[:, :, :], ACT.Square).then_inc(s["squared"], 1)
    act.wait_ge(s["var"], 1)
    nc.scalar.activation(var[:, :], var[:, :], ACT.Sqrt).then_inc(s["std"], 1)


def transpose_rows_pe(nc, pe, rows, banks, identity, done, taken):
    for c in range(NCH):
        if c >= len(banks):
            pe.wait_ge(taken, c - len(banks) + 1)
        for s in range(TPB):
            last = nc.tensor.transpose(banks[c % len(banks)][:, ts(s, P)], rows(c * TPB + s), identity)
        last.then_inc(done, 1)


def transpose_rows_act(nc, act, out, banks, done, taken):
    for c in range(NCH):
        act.wait_ge(done, c + 1)
        nc.scalar.copy(out(c), banks[c % len(banks)][:, :]).then_inc(taken, 1)


def next_semaphore(nc):
    with nc.semaphore("unused") as sem:
        return sem.num


def clear_semaphores(nc, first, end):
    with nc.Block() as block:
        @block.gpsimd
        def _(pool):
            pool.sem_clear(range(first, end))


def sems(nc, mem, phase, names):
    return {n: mem.enter_context(nc.semaphore(f"{phase}_{n}")) for n in names.split()}



def layer0_features(nc, g, x_dram):
    with ExitStack() as mem:
        x = mem.enter_context(nc.sbuf_tensor("l0_x", [P, NT, D], F32))
        sq = mem.enter_context(nc.sbuf_tensor("l0_sq", [P, NT, D], F32))
        mean, var, inv = (mem.enter_context(nc.sbuf_tensor(f"l0_{n}", [P, NT], F32)) for n in ("mean", "var", "inv"))
        s = sems(nc, mem, "l0", "x_in ident zeroed centered squared var std tangent_sq norm2 norm chain")
        h = g.rows
        block = mem.enter_context(nc.Block())

        @block.sync
        def _(sp):
            sp.dma_start(x[:, :, :], row_tiles(x_dram)).then_inc(s["x_in"], 16)

        @block.gpsimd
        def _(pool):
            nc.gpsimd.memset(g.ones[:, :], 1.0).then_inc(s["ident"], 1)
            nc.gpsimd.memset(g.identity[:, :], 0.0).then_inc(s["zeroed"], 1)
            pool.wait_ge(s["zeroed"], 1)
            nc.gpsimd.affine_select(out=g.identity[:, :], in_=g.identity[:, :], compare_op=ALU.not_equal,
                                    fill=1.0, base=0, pattern=[[-1, P]], channel_multiplier=1).then_inc(s["ident"], 1)

        @block.vector
        def _(dve):
            link = Link(dve, s["chain"])
            dve.wait_ge(s["x_in"], 16)
            layer_norm_dve(nc, dve, link, s, x, h, sq, mean, var)
            nc.vector.memset(h[:, :, 0:1], 0.0).then_inc(s["tangent_sq"], 1)
            dve.wait_ge(s["squared"], 2)
            nc.vector.tensor_reduce(var[:, :], sq[:, :, :], X_AXIS, ALU.add).then_inc(s["norm2"], 1)
            dve.wait_ge(s["norm"], 1)
            link(nc.vector.tensor_scalar(var[:, :], var[:, :], MIN_NORM, None, ALU.max))
            link(nc.vector.reciprocal(inv[:, :], var[:, :]))
            link(nc.vector.tensor_scalar(var[:, :], var[:, :], THETA_MIN, None, ALU.max))
            link(nc.vector.tensor_tensor(var[:, :], var[:, :], inv[:, :], ALU.mult))
            link(nc.vector.tensor_tensor(h[:, :, :], h[:, :, :], over_rows(var[:, :]), ALU.mult))

        @block.scalar
        def _(act):
            layer_norm_act(nc, act, s, h, sq, var)
            act.wait_ge(s["tangent_sq"], 1)
            nc.scalar.activation(sq[:, :, :], h[:, :, :], ACT.Square).then_inc(s["squared"], 1)
            act.wait_ge(s["norm2"], 1)
            nc.scalar.activation(var[:, :], var[:, :], ACT.Sqrt).then_inc(s["norm"], 1)


def layer0_aggregate(nc, g, adj, adj_t):
    GR = BANK // P
    NG = NT // GR
    CHT = 8
    NLOAD = NT // CHT
    STT = 4
    NST = NT // STT
    SLOTS = 4
    BANKS = 4
    with ExitStack() as mem:
        blk = [mem.enter_context(nc.sbuf_tensor(f"a_adj{c}", [P, GR, CHT * P], F32)) for c in range(NLOAD)]
        out = [mem.enter_context(nc.sbuf_tensor(f"a_out{c}", [P, STT, BANK], F32)) for c in range(SLOTS)]
        tp = [mem.enter_context(nc.psum_tensor(f"a_tp{b}", [P, BANK], F32)) for b in range(BANKS)]
        acc = mem.enter_context(nc.psum_tensor("a_acc", [P, BANK], F32))
        s = sems(nc, mem, "a", "transposed copied_act copied_dve multiplied summed taken")
        loaded = [mem.enter_context(nc.semaphore(f"a_loaded{c}")) for c in range(NLOAD)]
        stored = [mem.enter_context(nc.semaphore(f"a_stored{c}")) for c in range(SLOTS)]
        block = mem.enter_context(nc.Block())
        adj_v = adj.rearrange("(gr s p) j -> gr p s j", s=GR, p=P)
        adj_t_v = adj_t.rearrange("(q t p) i -> q p t i", t=STT, p=P)

        def columns(grp):
            if isinstance(grp, int):
                return slice(grp * BANK, (grp + 1) * BANK)
            return bass.ds(grp * BANK, BANK)

        @block.sync
        def _(sp):
            def load(grp, c):
                src = adj_v[grp] if isinstance(grp, int) else adj_v[bass.ds(grp, 1)].rearrange("o p s j -> (o p) s j")
                sp.dma_start(blk[c][:, :, :], src[:, :, ts(c, CHT * P)]).then_inc(loaded[c], 16)

            def stores(grp, c):
                for q in (2 * c, 2 * c + 1):
                    sp.wait_ge(s["multiplied"], grp * NT + (q + 1) * STT)
                    sp.dma_start(adj_t_v[q, :, :, columns(grp)], out[q % SLOTS][:, :, :]).then_inc(stored[q % SLOTS], 16)

            for c in range(NLOAD):
                load(0, c)
            with sp.Fori(0, NG - 1) as grp:
                for c in range(NLOAD):
                    stores(grp, c)
                    load(grp + 1, c)
            for c in range(NLOAD):
                stores(NG - 1, c)
            for c in range(SLOTS):
                sp.wait_ge(stored[c], 16 * NG * NST // SLOTS)

        @block.tensor
        def _(pe):
            def copied(grp, jt, ahead):
                return grp * (NT // 2) + (jt - ahead) // 2 + 1

            def group(grp, first):
                for jt in range(NT + 1):
                    if jt < NT:
                        if jt % CHT == 0:
                            pe.wait_ge(loaded[jt // CHT], grp * 16 + 16)
                        if not (first and jt < BANKS):
                            pe.wait_ge((s["copied_act"], s["copied_dve"])[jt % 2], copied(grp, jt, BANKS))
                        for r in range(GR):
                            last = nc.tensor.transpose(tp[jt % BANKS][:, ts(r, P)],
                                                       blk[jt // CHT][:, r, ts(jt % CHT, P)], g.identity[:, :])
                        last.then_inc(s["transposed"], 1)
                    if jt > 0:
                        m = jt - 1
                        pe.wait_ge((s["copied_act"], s["copied_dve"])[m % 2], copied(grp, m, 0))
                        if m == 0 and not first:
                            pe.wait_ge(s["taken"], grp)
                        mm = nc.tensor.matmul(acc[:, :], g.rows[:, m, :], out[(m // STT) % SLOTS][:, m % STT, :],
                                              start=(m == 0), stop=(m == NT - 1))
                        mm.then_inc(s["multiplied"], 1)

            group(0, True)
            with pe.Fori(1, NG) as grp:
                group(grp, False)

        def copies(eng, copy, odd, copied_sem):
            def group(grp, first):
                for jt in range(odd, NT, 2):
                    q = jt // STT
                    if jt % STT == odd and not (first and q < SLOTS):
                        eng.wait_ge(stored[q % SLOTS], (grp * (NST // SLOTS) + q // SLOTS) * 16)
                    eng.wait_ge(s["transposed"], grp * NT + jt + 1)
                    copy(out[q % SLOTS][:, jt % STT, :], tp[jt % BANKS][:, :]).then_inc(copied_sem, 1)
                if not odd:
                    eng.wait_ge(s["multiplied"], grp * NT + NT)
                    copy(g.agg_t[:, columns(grp)], acc[:, :]).then_inc(s["taken"], 1)

            group(0, True)
            with eng.Fori(1, NG) as grp:
                group(grp, False)

        @block.scalar
        def _(act):
            copies(act, nc.scalar.copy, 0, s["copied_act"])

        @block.vector
        def _(dve):
            copies(dve, nc.vector.tensor_copy, 1, s["copied_dve"])


def layer0_combine(nc, g, w1, b1, w2, b2, x_dram, x1_dram):
    with ExitStack() as mem:
        agg = mem.enter_context(nc.sbuf_tensor("c_agg", [P, NT, D], F32))
        sq = mem.enter_context(nc.sbuf_tensor("c_sq", [P, NT, D], F32))
        x = mem.enter_context(nc.sbuf_tensor("c_x", [P, NT, D], F32))
        w1_sb = mem.enter_context(nc.sbuf_tensor("c_w1", [P, HID], F32))
        w2_sb = mem.enter_context(nc.sbuf_tensor("c_w2", [P, HID // P, D], F32))
        b1_sb = mem.enter_context(nc.sbuf_tensor("c_b1", [P, HID // P], F32))
        b2_sb = mem.enter_context(nc.sbuf_tensor("c_b2", [P, 1, D], F32))
        hid = [mem.enter_context(nc.sbuf_tensor(f"c_hid{m}", [P, BANK], F32)) for m in range(HID // P)]
        n, inv, e, cosh = (mem.enter_context(nc.sbuf_tensor(f"c_{k}", [P, NT], F32)) for k in ("n", "inv", "e", "cosh"))
        tp = [mem.enter_context(nc.psum_tensor(f"c_tp{b}", [P, BANK], F32)) for b in range(2)]
        pre = [mem.enter_context(nc.psum_tensor(f"c_pre{m}", [P, BANK], F32)) for m in range(HID // P)]
        mlp = mem.enter_context(nc.psum_tensor("c_mlp", [P, BANK], F32))
        s = sems(nc, mem, "c", "weights x_in x_out t1 t1_out t2 t2_out chain v squared norm2 norm e combined "
                               "out_ready pre hid mlp added biased")
        agg_t = g.agg_t
        block = mem.enter_context(nc.Block())

        @block.sync
        def _(sp):
            sp.dma_start(w1_sb[:, :], w1).then_inc(s["weights"], 16)
            sp.dma_start(w2_sb[:, :, :], w2.rearrange("(m p) d -> p m d", p=P)).then_inc(s["weights"], 16)
            with nc.allow_non_contiguous_dma("two columns of biases"):
                sp.dma_start(b1_sb[:, :], b1.rearrange("(m p) -> p m", p=P)).then_inc(s["weights"], 16)
            sp.dma_start(b2_sb[:, 0, :], b2.partition_broadcast(P)).then_inc(s["weights"], 16)
            sp.dma_start(x[:, :, :], row_tiles(x_dram)).then_inc(s["x_in"], 16)
            sp.wait_ge(s["added"], NCH)
            sp.dma_start(row_tiles(x1_dram), x[:, :, :]).then_inc(s["x_out"], 16)
            sp.wait_ge(s["x_out"], 16)

        @block.tensor
        def _(pe):
            transpose_rows_pe(nc, pe, lambda t: agg_t[:, ts(t, P)], tp, g.identity[:, :], s["t1"], s["t1_out"])
            pe.wait_ge(s["out_ready"], 1)
            pe.wait_ge(s["t1_out"], NCH)
            transpose_rows_pe(nc, pe, lambda t: agg[:, t, :], tp, g.identity[:, :], s["t2"], s["t2_out"])
            pe.wait_ge(s["weights"], 64)
            pe.wait_ge(s["t2_out"], NCH)

            def chunk(c, first):
                if not first:
                    pe.wait_ge(s["hid"], c * (HID // P))
                for m in range(HID // P):
                    cols = slice(0, BANK) if first else bass.ds(c * BANK, BANK)
                    nc.tensor.matmul(pre[m][:, :], w1_sb[:, ts(m, P)], agg_t[:, cols],
                                     start=True, stop=True).then_inc(s["pre"], 1)
                if not first:
                    pe.wait_ge(s["added"], c)
                pe.wait_ge(s["hid"], (c + 1) * (HID // P))
                for r in range(TPB):
                    for m in range(HID // P):
                        last = nc.tensor.matmul(mlp[:, ts(r, D)], hid[m][:, ts(r, P)], w2_sb[:, m, :],
                                                start=(m == 0), stop=(m == HID // P - 1))
                last.then_inc(s["mlp"], 1)

            chunk(0, True)
            with pe.Fori(1, NCH) as c:
                chunk(c, False)

        @block.scalar
        def _(act):
            transpose_rows_act(nc, act, lambda c: agg[:, ts(c, TPB), :].rearrange("p t d -> p (t d)"), tp, s["t1"], s["t1_out"])
            for k in range(2):
                act.wait_ge(s["v"], k) if k else act.wait_ge(s["t1_out"], NCH)
                nc.scalar.activation(sq[:, :, :], agg[:, :, :], ACT.Square).then_inc(s["squared"], 1)
                act.wait_ge(s["norm2"], k + 1)
                nc.scalar.activation(n[:, :], n[:, :], ACT.Sqrt).then_inc(s["norm"], 1)
            act.wait_ge(s["v"], 2)
            nc.scalar.activation(e[:, :], n[:, :], ACT.Exp).then_inc(s["e"], 1)
            transpose_rows_act(nc, act, lambda c: agg_t[:, ts(c, BANK)], tp, s["t2"], s["t2_out"])
            act.wait_ge(s["weights"], 64)

            def chunk(c, first):
                for m in range(HID // P):
                    act.wait_ge(s["pre"], c * (HID // P) + m + 1)
                    if not first and m == 0:
                        act.wait_ge(s["mlp"], c)
                    nc.scalar.activation(hid[m][:, :], pre[m][:, :], ACT.Relu, bias=b1_sb[:, m:m + 1]).then_inc(s["hid"], 1)

            chunk(0, True)
            with act.Fori(1, NCH) as c:
                chunk(c, False)

        @block.vector
        def _(dve):
            link = Link(dve, s["chain"])
            dve.wait_ge(s["weights"], 64)
            dve.wait_ge(s["x_in"], 16)
            nc.vector.tensor_tensor(x[:, :, :], x[:, :, :], b2_sb[:, :, :].to_broadcast([P, NT, D]),
                                    ALU.add).then_inc(s["biased"], 1)
            dve.wait_ge(s["squared"], 1)
            nc.vector.tensor_reduce(n[:, :], sq[:, :, :], X_AXIS, ALU.add).then_inc(s["norm2"], 1)
            dve.wait_ge(s["norm"], 1)
            link(nc.vector.tensor_scalar(n[:, :], n[:, :], MIN_NORM, None, ALU.max))
            link(nc.vector.reciprocal(inv[:, :], n[:, :]))
            link(nc.vector.tensor_scalar(n[:, :], n[:, :], THETA_MIN, None, ALU.max))
            link(nc.vector.tensor_tensor(n[:, :], n[:, :], inv[:, :], ALU.mult))
            link(nc.vector.tensor_tensor(agg[:, :, :], agg[:, :, :], over_rows(n[:, :]), ALU.mult))
            nc.vector.tensor_tensor(agg[:, :, :], agg[:, :, :], g.rows[:, :, :], ALU.add).then_inc(s["v"], 1)
            dve.wait_ge(s["squared"], 2)
            nc.vector.tensor_reduce(n[:, :], sq[:, :, :], X_AXIS, ALU.add).then_inc(s["norm2"], 1)
            dve.wait_ge(s["norm"], 2)
            nc.vector.tensor_scalar(n[:, :], n[:, :], MIN_NORM, None, ALU.max).then_inc(s["v"], 1)
            dve.wait_ge(s["v"], 2)
            link(nc.vector.reciprocal(inv[:, :], n[:, :]))
            dve.wait_ge(s["e"], 1)
            link(nc.vector.reciprocal(n[:, :], e[:, :]))
            link(nc.vector.tensor_tensor(cosh[:, :], e[:, :], n[:, :], ALU.add))
            link(nc.vector.tensor_scalar(cosh[:, :], cosh[:, :], 0.5, None, ALU.mult))
            link(nc.vector.tensor_tensor(e[:, :], e[:, :], n[:, :], ALU.subtract))
            link(nc.vector.scalar_tensor_tensor(e[:, :], e[:, :], 0.5, inv[:, :], ALU.mult, ALU.mult))
            link(nc.vector.tensor_tensor(agg[:, :, :], agg[:, :, :], over_rows(e[:, :]), ALU.mult))
            nc.vector.tensor_copy(agg[:, :, 0:1], cosh[:, :].unsqueeze(2)).then_inc(s["out_ready"], 1)
            dve.wait_ge(s["biased"], 1)

            def chunk(c):
                dve.wait_ge(s["mlp"], c + 1)
                tiles = slice(0, TPB) if isinstance(c, int) else bass.ds(c * TPB, TPB)
                part = x[:, tiles, :].rearrange("p t d -> p (t d)")
                nc.vector.tensor_tensor(part, mlp[:, :], part, ALU.add).then_inc(s["added"], 1)

            chunk(0)
            with dve.Fori(1, NCH) as c:
                chunk(c)



def layer1_features(nc, g, x_dram, beta):
    with ExitStack() as mem:
        x = mem.enter_context(nc.sbuf_tensor("f1_x", [P, NT, D], F32))
        sq = mem.enter_context(nc.sbuf_tensor("f1_sq", [P, NT, D], F32))
        mean, var, n = (mem.enter_context(nc.sbuf_tensor(f"f1_{k}", [P, NT], F32)) for k in ("mean", "var", "n"))
        tp = [mem.enter_context(nc.psum_tensor(f"f1_tp{b}", [P, BANK], F32)) for b in range(4)]
        s = sems(nc, mem, "f1", "x_in beta_in centered squared var std chain rows norm2 norm clamped log unit diag "
                                "transposed copied spread spread_out")
        h = g.rows
        block = mem.enter_context(nc.Block())

        @block.sync
        def _(sp):
            sp.dma_start(x[:, :, :], row_tiles(x_dram)).then_inc(s["x_in"], 16)
            sp.dma_start(g.half_beta[:, :], beta.partition_broadcast(P)).then_inc(s["beta_in"], 16)

        @block.vector
        def _(dve):
            link = Link(dve, s["chain"])
            dve.wait_ge(s["beta_in"], 16)
            link(nc.vector.tensor_scalar(g.half_beta[:, :], g.half_beta[:, :], 0.5, None, ALU.mult))
            dve.wait_ge(s["x_in"], 16)
            layer_norm_dve(nc, dve, link, s, x, h, sq, mean, var)
            nc.vector.tensor_copy(mean[:, 0:1], var[:, 0:1]).then_inc(s["rows"], 1)
            dve.wait_ge(s["squared"], 2)
            nc.vector.tensor_reduce(n[:, :], sq[:, :, :], X_AXIS, ALU.add).then_inc(s["norm2"], 1)
            dve.wait_ge(s["norm"], 1)
            nc.vector.tensor_scalar(n[:, :], n[:, :], TINY_NORM, None, ALU.max).then_inc(s["clamped"], 1)
            dve.wait_ge(s["clamped"], 1)
            link(nc.vector.reciprocal(var[:, :], n[:, :]))
            nc.vector.tensor_tensor(sq[:, :, :], h[:, :, :], over_rows(var[:, :]), ALU.mult).then_inc(s["unit"], 1)
            dve.wait_ge(s["log"], 1)
            link(nc.vector.tensor_scalar(g.half_log[:, :], mean[:, :], -LOG_EPS, 0.5, ALU.add, ALU.mult))
            nc.vector.tensor_tensor(x[:, :, :], g.identity[:, :].unsqueeze(1).to_broadcast([P, NT, D]),
                                    over_rows(mean[:, :]), ALU.mult).then_inc(s["diag"], 1)

        @block.scalar
        def _(act):
            layer_norm_act(nc, act, s, h, sq, var)
            act.wait_ge(s["rows"], 1)
            nc.scalar.activation(sq[:, :, :], h[:, :, :], ACT.Square).then_inc(s["squared"], 1)
            act.wait_ge(s["norm2"], 1)
            nc.scalar.activation(n[:, :], n[:, :], ACT.Sqrt).then_inc(s["norm"], 1)
            act.wait_ge(s["clamped"], 1)
            nc.scalar.activation(mean[:, :], n[:, :], ACT.Ln).then_inc(s["log"], 1)
            transpose_rows_act(nc, act, lambda c: g.unit_t[:, ts(c, BANK)], tp, s["transposed"], s["copied"])
            transpose_rows_act(nc, act, lambda c: g.log_row[:, ts(c, BANK)], tp, s["spread"], s["spread_out"])

        @block.tensor
        def _(pe):
            pe.wait_ge(s["unit"], 1)
            transpose_rows_pe(nc, pe, lambda t: sq[:, t, :], tp, g.identity[:, :], s["transposed"], s["copied"])
            pe.wait_ge(s["diag"], 1)
            pe.wait_ge(s["copied"], NCH)
            for c in range(NCH):
                if c >= len(tp):
                    pe.wait_ge(s["spread_out"], c - len(tp) + 1)
                nc.tensor.matmul(tp[c % len(tp)][:, :], g.ones[:, :], x[:, ts(c, TPB), :].rearrange("p t d -> p (t d)"),
                                 start=True, stop=True).then_inc(s["spread"], 1)


def layer2_features(nc, g, x_dram, w, a_self, a_neigh):
    with ExitStack() as mem:
        x = mem.enter_context(nc.sbuf_tensor("f2_x", [P, NT, D], F32))
        sq = mem.enter_context(nc.sbuf_tensor("f2_sq", [P, NT, D], F32))
        h = mem.enter_context(nc.sbuf_tensor("f2_h", [P, NT, D], F32))
        h_t = mem.enter_context(nc.sbuf_tensor("f2_ht", [P, N], F32))
        mean, var = (mem.enter_context(nc.sbuf_tensor(f"f2_{k}", [P, NT], F32)) for k in ("mean", "var"))
        w_sb = mem.enter_context(nc.sbuf_tensor("f2_w", [P, D + H2], F32))
        a_sb = mem.enter_context(nc.sbuf_tensor("f2_a", [P, 2, D], F32))
        wa = mem.enter_context(nc.sbuf_tensor("f2_wa", [P, 2, D], F32))
        w_neigh = mem.enter_context(nc.sbuf_tensor("f2_wn", [P, H2], F32))
        w_neigh_all = mem.enter_context(nc.sbuf_tensor("f2_wna", [P, H2, P], F32))
        tp = [mem.enter_context(nc.psum_tensor(f"f2_tp{b}", [P, BANK], F32)) for b in range(4)]
        s = sems(nc, mem, "f2", "x_in w_in centered squared var std chain rows weights transposed copied projected "
                                "projected_out spread spread_out")
        block = mem.enter_context(nc.Block())

        @block.sync
        def _(sp):
            sp.dma_start(x[:, :, :], row_tiles(x_dram)).then_inc(s["x_in"], 16)
            sp.dma_start(w_sb[:, 0:D].rearrange("p (h d) -> p h d", h=H2), w.rearrange("h f d -> f h d")).then_inc(s["w_in"], 16)
            sp.dma_start(a_sb[:, 0, :], a_self.rearrange("h d -> (h d)").partition_broadcast(P)).then_inc(s["w_in"], 16)
            sp.dma_start(a_sb[:, 1, :], a_neigh.rearrange("h d -> (h d)").partition_broadcast(P)).then_inc(s["w_in"], 16)

        @block.vector
        def _(dve):
            link = Link(dve, s["chain"])
            dve.wait_ge(s["w_in"], 48)
            for k, dst in ((0, w_sb[:, D:D + H2]), (1, w_neigh[:, :])):
                link(nc.vector.tensor_tensor(wa[:, k, :], w_sb[:, 0:D], a_sb[:, k, :], ALU.mult))
                link(nc.vector.tensor_reduce(dst, wa[:, k, :].rearrange("p (h d) -> p h d", h=H2), X_AXIS, ALU.add))
            for k in range(H2):
                nc.vector.tensor_scalar(w_neigh_all[:, k, :], g.ones[:, :], w_neigh[:, k:k + 1], None,
                                        ALU.mult).then_inc(s["weights"], 1)
            dve.wait_ge(s["x_in"], 16)
            layer_norm_dve(nc, dve, link, s, x, h, sq, mean, var)
            nc.vector.tensor_copy(mean[:, 0:1], var[:, 0:1]).then_inc(s["rows"], 1)

        @block.scalar
        def _(act):
            layer_norm_act(nc, act, s, h, sq, var)
            transpose_rows_act(nc, act, lambda c: h_t[:, ts(c, BANK)], tp, s["transposed"], s["copied"])
            for t in range(NT):
                act.wait_ge(s["projected"], t + 1)
                nc.scalar.copy(g.rows[:, t, :], tp[t % 4][:, 0:D])
                nc.scalar.copy(g.self_col[:, t, :], tp[t % 4][:, D:D + H2]).then_inc(s["projected_out"], 1)
            transpose_rows_act(nc, act, lambda c: g.neigh_row[:, c // NCH, ts(c % NCH, BANK)], tp, s["spread"], s["spread_out"])
            for c in range(NCH, H2 * NCH):
                act.wait_ge(s["spread"], c + 1)
                nc.scalar.copy(g.neigh_row[:, c // NCH, ts(c % NCH, BANK)], tp[c % 4][:, :]).then_inc(s["spread_out"], 1)

        @block.tensor
        def _(pe):
            pe.wait_ge(s["rows"], 1)
            transpose_rows_pe(nc, pe, lambda t: h[:, t, :], tp, g.identity[:, :], s["transposed"], s["copied"])
            pe.wait_ge(s["copied"], NCH)
            pe.wait_ge(s["weights"], H2)
            for t in range(NT):
                if t >= 4:
                    pe.wait_ge(s["projected_out"], t - 3)
                nc.tensor.matmul(tp[t % 4][:, 0:D + H2], h_t[:, ts(t, P)], w_sb[:, :], start=True, stop=True).then_inc(s["projected"], 1)
            pe.wait_ge(s["projected_out"], NT)
            for c in range(H2 * NCH):
                if c >= 4:
                    pe.wait_ge(s["spread_out"], c - 3)
                nc.tensor.matmul(tp[c % 4][:, :], w_neigh_all[:, c // NCH, :], h_t[:, ts(c % NCH, BANK)],
                                 start=True, stop=True).then_inc(s["spread"], 1)


def masked_attention(nc, g, layer, adj, x_dram, x_next_dram, bias=None):
    heads = 1 if layer == 1 else H2
    UN = 4
    RT = UN // heads
    NR = NT // RT
    NU = NR * UN
    PW = 2 * P
    TPN = 2 if layer == 1 else 4
    TB = NT // TPB
    EX = 1 if layer == 1 else 2
    SCH = 2 * BANK
    NS = N // SCH
    LAG = 7
    with ExitStack() as mem:
        def sb(name, shape):
            return mem.enter_context(nc.sbuf_tensor(f"m{layer}_{name}", shape, F32))

        def psum(name, shape):
            return mem.enter_context(nc.psum_tensor(f"m{layer}_{name}", shape, F32))

        adj_sb = [sb(f"adj{b}", [P, N]) for b in range(2)]
        part = sb("part", [P, N])
        score = [sb(f"score{b}", [P, N]) for b in range(2)]
        probs = [sb(f"probs{b}", [P, NT, PW]) for b in range(2)]
        out_t = sb("out_t", [P, RT * P])
        xg = sb("x", [P, RT, D])
        neg_top, total = sb("neg_top", [P, UN]), sb("total", [P, EX, UN])
        inv = sb("inv", [P, 2, UN])
        spare = sb("spare", [P, 1])
        tp = [psum(f"tp{b}", [P, TPB, P]) for b in range(TPN)]
        ps_out = psum("ps_out", [P, BANK])
        ps_rows = psum("ps_rows", [P, BANK])
        if layer == 1:
            lhs = [sb(f"lhs{b}", [P, P]) for b in range(2)]
            ps_s = [psum(f"ps_s{b}", [P, SCH]) for b in range(2)]
        else:
            sums = sb("sums", [P, UN])
            val, low, bias_sb = sb("val", [P, RT, D]), sb("low", [P, RT, D]), sb("bias", [P, D])
        s = sems(nc, mem, f"m{layer}", "gated masks masked exped transposed copied summed out_copied rows inv "
                 "rows_read x_in x_ready x_out " + ("lhs products part_ready" if layer == 1 else "bias_in valued lowered elu_exp summed_up"))
        adj_in = [mem.enter_context(nc.semaphore(f"m{layer}_adj_in{b}")) for b in range(2)]
        block = mem.enter_context(nc.Block())
        adj_v = adj.rearrange("(k p) j -> k p j", p=P)

        def out_part(tensor, pair):
            if layer == 1:
                return tensor[:, ts(pair, PW)]
            return tensor[ts(pair, DH2), 0:PW]

        def live(k, below):
            return not isinstance(k, int) or 0 <= k < below

        def rounds(eng, slot):
            for k in range(2 * UN):
                slot(k, k // UN, k % UN)
            with eng.Fori(2, NR - 1) as r:
                for u in range(UN):
                    slot(r * UN + u, r, u)
            for k in range(NU - UN, NU + LAG + 1):
                slot(k, k // UN, k % UN)

        def row_tile(dram, k, n=1):
            tiles = row_tiles(dram)
            return tiles[:, k:k + n, :] if isinstance(k, int) else tiles[:, bass.ds(k, n), :]

        @block.sync
        def _(sp):
            def load(k, slot):
                src = adj_v[k] if isinstance(k, int) else adj_v[bass.ds(k, 1)].rearrange("o p j -> (o p) j")
                sp.dma_start(adj_sb[slot][:, :], src).then_inc(adj_in[slot], 16)

            if layer == 2:
                sp.dma_start(bias_sb[:, :], bias.partition_broadcast(P)).then_inc(s["bias_in"], 16)
            load(0, 0)
            load(1, 1)
            with sp.Fori(1, NT // 2) as m:
                for b in range(2):
                    sp.wait_ge(s["masked"], m * 2 + b - 1 if layer == 1 else m * UN + b - 1)
                    load(m * 2 + b, b)

        @block.gpsimd
        def _(pool):
            def load(r):
                pool.dma_start(xg[:, :, :], row_tile(x_dram, RT * r, RT)).then_inc(s["x_in"], 16)

            def store(r):
                pool.wait_ge(s["x_ready"], r + 1)
                pool.dma_start(row_tile(x_next_dram, RT * r, RT), xg[:, :, :]).then_inc(s["x_out"], 16)
                pool.wait_ge(s["x_out"], (r + 1) * 16)

            load(0)
            with pool.Fori(0, NR - 1) as r:
                store(r)
                load(r + 1)
            store(NR - 1)

        @block.tensor
        def _(pe):
            def products(k, u, c):
                if not live(k, NU):
                    return
                if c == 0:
                    pe.wait_ge(s["lhs"], k + 1)
                if not (isinstance(k, int) and k == 0 and c < 2):
                    pe.wait_ge(s["gated"], k * NS + c - 1)
                for q in range(2):
                    last = nc.tensor.matmul(ps_s[c % 2][:, ts(q, BANK)], lhs[u % 2][:, :],
                                            g.unit_t[:, ts(2 * c + q, BANK)], start=True, stop=True)
                last.then_inc(s["products"], 1)

            def transposes(k, u, b):
                if not live(k, NU):
                    return
                if b * EX % TB == 0:
                    pe.wait_ge(s["exped"], k * EX + b * EX // TB + 1)
                if not (isinstance(k, int) and k == 0 and b < TPN):
                    pe.wait_ge(s["copied"], k * TB + b - TPN + 1)
                for r in range(TPB):
                    last = nc.tensor.transpose(tp[b % TPN][:, r, :], score[u % 2][:, ts(b * TPB + r, P)], g.identity[:, :])
                last.then_inc(s["transposed"], 1)

            def values(k, r, u, first, n):
                half = (u + 1) % 2
                last_unit = k - 2 - half
                pair = (u - 2 - half) // 2 % 2
                if not live(last_unit, NU):
                    return
                if half == 0 and first == 0:
                    pe.wait_ge(s["copied"], (last_unit + 1) * TB)
                    back = 1 if layer == 1 else 2
                    if live(last_unit - 2 * back, NU):
                        pe.wait_ge(s["out_copied"], 2 * r + (u == 3) - back)
                for jt in range(half * NT // 2 + first, half * NT // 2 + first + n):
                    cols = slice(0, D) if layer == 1 else ts(pair, DH2)
                    mm = nc.tensor.matmul(out_part(ps_out, pair), g.rows[:, jt, cols], probs[pair][:, jt, :],
                                          start=(jt == 0), stop=(jt == NT - 1))
                if half == 1 and first + n == NT // 2:
                    mm.then_inc(s["summed"], 1)

            def rows_back(r):
                if not live(r, NR):
                    return
                pe.wait_ge(s["out_copied"], 2 * r + 2)
                pe.wait_ge(s["rows_read"], r + 1)
                for t in range(RT):
                    last = nc.tensor.transpose(ps_rows[:, ts(t, P)], out_t[:, ts(t, P)], g.identity[:, :])
                last.then_inc(s["rows"], 1)

            def slot(k, r, u):
                if u == 0:
                    rows_back(r - 2)
                if layer == 1:
                    products(k, u, 2)
                    products(k, u, 3)
                    values(k, r, u, 0, 8)
                    for b in range(TB // 2):
                        transposes(k - 1, (u - 1) % UN, b)
                    products(k + 1, (u + 1) % UN, 0)
                    products(k + 1, (u + 1) % UN, 1)
                    values(k, r, u, 8, 8)
                    for b in range(TB // 2, TB):
                        transposes(k - 1, (u - 1) % UN, b)
                else:
                    values(k, r, u, 0, 10)
                    for b in range(TB // 2):
                        transposes(k - 1, (u - 1) % UN, b)
                    values(k, r, u, 10, 6)
                    for b in range(TB // 2, TB):
                        transposes(k - 1, (u - 1) % UN, b)

            if layer == 1:
                products(0, 0, 0)
                products(0, 0, 1)
            rounds(pe, slot)

        @block.scalar
        def _(act):
            def left_rows(k, u):
                if not live(k, NU):
                    return
                tile = ts(k, P) if isinstance(k, int) else bass.ds(k * P, P)
                if not (isinstance(k, int) and k < 2):
                    act.wait_ge(s["products"], (k - 1) * NS)
                nc.scalar.activation(lhs[u % 2][:, :], g.unit_t[:, tile], ACT.Identity,
                                     scale=g.half_beta[:, :]).then_inc(s["lhs"], 1)

            def gate(k):
                if not live(k, NU):
                    return
                row = slice(k, k + 1) if isinstance(k, int) else bass.ds(k, 1)
                if not (isinstance(k, int) and k == 0):
                    act.wait_ge(s["masked"], k)
                nc.scalar.activation(part[:, :], g.log_row[:, :], ACT.Tanh, scale=0.5,
                                     bias=g.half_log[:, row]).then_inc(s["part_ready"], 1)

            def softmax(k, u, r):
                if not live(k, NU):
                    return
                act.wait_ge(s["masked"], k + 1)
                if u == 0 and not (isinstance(r, int) and r == 0):
                    act.wait_ge(s["inv"], r)
                for x in range(EX):
                    cols = score[u % 2][:, ts(x, N // EX)]
                    nc.scalar.activation(cols, cols, ACT.Exp, scale=-1.0,
                                         bias=neg_top[:, u:u + 1], accum_out=total[:, x, u:u + 1]).then_inc(s["exped"], 1)

            def copies(k, r, u, first, n):
                if not live(k, NU):
                    return
                if u % 2 == 0 and first == 0 and live(k - UN, NU):
                    act.wait_ge(s["summed"], 2 * r + u // 2 - 1)
                for b in range(first, first + n):
                    act.wait_ge(s["transposed"], k * TB + b + 1)
                    nc.scalar.copy(probs[u // 2][:, ts(b, TPB), ts(u % 2, P)], tp[b % TPN][:, :, :]).then_inc(s["copied"], 1)

            def take_out(k, r, u):
                last_unit = k - 4
                if u % 2 == 0 or not live(last_unit, NU):
                    return
                pair, of_round = u // 2, r - 1
                count = of_round * 2 + pair + 1
                act.wait_ge(s["summed"], count)
                if pair == 0 and not (isinstance(of_round, int) and of_round == 0):
                    act.wait_ge(s["rows"], of_round)
                nc.scalar.copy(out_part(out_t, pair), out_part(ps_out, pair)).then_inc(s["out_copied"], 1)

            def elu_exp(r):
                if live(r, NR):
                    act.wait_ge(s["lowered"], r + 1)
                    nc.scalar.activation(low[:, :, :], low[:, :, :], ACT.Exp).then_inc(s["elu_exp"], 1)

            def slot(k, r, u):
                take_out(k, r, u)
                softmax(k - 1, (u - 1) % UN, r if u else r - 1)
                copies(k - 1, r if u else r - 1, (u - 1) % UN, 0, TB // 2)
                if layer == 1:
                    gate(k + 1)
                    left_rows(k + 2, u + 2)
                copies(k - 1, r if u else r - 1, (u - 1) % UN, TB // 2, TB // 2)
                if layer == 2 and u == 3:
                    elu_exp(r - 2)

            if layer == 1:
                left_rows(0, 0)
                left_rows(1, 1)
                gate(0)
            rounds(act, slot)

        @block.vector
        def _(dve):
            def inverse(r, cols):
                both = inv[:, :, cols]
                return both[:, r % 2, :] if isinstance(r, int) else both[:, bass.ds(r % 2, 1), :].rearrange("p o u -> p (o u)")

            def invert(r):
                if live(r, NR):
                    dve.wait_ge(s["exped"], (r + 1) * UN * EX)
                    if EX == 2:
                        nc.vector.tensor_tensor(sums[:, :], total[:, 0, :], total[:, 1, :],
                                                ALU.add).then_inc(s["summed_up"], 1)
                        dve.wait_ge(s["summed_up"], r + 1)
                        nc.vector.reciprocal(inverse(r, slice(0, UN)), sums[:, :]).then_inc(s["inv"], 1)
                    else:
                        nc.vector.reciprocal(inverse(r, slice(0, UN)), total[:, 0, :]).then_inc(s["inv"], 1)

            def finish(r):
                if not live(r, NR):
                    return
                dve.wait_ge(s["x_in"], (r + 1) * 16)
                dve.wait_ge(s["inv"], r + 1)
                dve.wait_ge(s["rows"], r + 1)
                for t in range(RT):
                    for h in range(heads):
                        cols = slice(h * D // heads, (h + 1) * D // heads)
                        u = h * RT + t
                        rows = ps_rows[:, t * P + cols.start:t * P + cols.stop]
                        if layer == 1:
                            last = nc.vector.scalar_tensor_tensor(xg[:, t, cols], rows, inverse(r, slice(u, u + 1)), xg[:, t, cols],
                                                                  ALU.mult, ALU.add)
                        else:
                            last = nc.vector.scalar_tensor_tensor(val[:, t, cols], rows, inverse(r, slice(u, u + 1)), bias_sb[:, cols],
                                                                  ALU.mult, ALU.add)
                last.then_inc(s["rows_read"], 1)
                dve.wait_ge(s["rows_read"], r + 2)
                if layer == 1:
                    nc.vector.memset(spare[:, :], 0.0).then_inc(s["x_ready"], 1)
                else:
                    nc.vector.tensor_scalar(low[:, :, :], val[:, :, :], 0.0, None, ALU.min).then_inc(s["lowered"], 1)

            def finish_elu(r):
                if not live(r, NR):
                    return
                dve.wait_ge(s["elu_exp"], r + 1)
                nc.vector.scalar_tensor_tensor(val[:, :, :], val[:, :, :], 0.0, low[:, :, :],
                                               ALU.max, ALU.add).then_inc(s["valued"], 1)
                dve.wait_ge(s["valued"], r + 1)
                nc.vector.scalar_tensor_tensor(xg[:, :, :], val[:, :, :], -1.0, xg[:, :, :],
                                               ALU.add, ALU.add).then_inc(s["x_ready"], 1)

            def scores(k, r, u):
                if not live(k, NU):
                    return
                mask = adj_sb[u % 2]
                if layer == 1 or u < 2:
                    dve.wait_ge(adj_in[u % 2], (r * 2 + u // 2 + 1) * 16 if layer == 1 else (r + 1) * 16)
                    nc.vector.tensor_scalar(mask[:, :], mask[:, :], 1.0, NEG, ALU.subtract, ALU.mult).then_inc(s["masks"], 1)
                if layer == 1:
                    dve.wait_ge(s["part_ready"], k + 1)
                    for c in range(NS):
                        dve.wait_ge(s["products"], k * NS + c + 1)
                        nc.vector.scalar_tensor_tensor(part[:, ts(c, SCH)], part[:, ts(c, SCH)], 1.0, ps_s[c % 2][:, :],
                                                       ALU.add, ALU.mult).then_inc(s["gated"], 1)
                    dve.wait_ge(s["gated"], (k + 1) * NS)
                    dve.wait_ge(s["masks"], k + 1)
                else:
                    h, col = u // 2, RT * r + u % 2
                    this = slice(col, col + 1) if isinstance(col, int) else bass.ds(col, 1)
                    if not (isinstance(k, int) and k == 0):
                        dve.wait_ge(s["masked"], k)
                    nc.vector.tensor_scalar(part[:, :], g.neigh_row[:, h, :],
                                            g.self_col[:, this, h], None, ALU.add).then_inc(s["gated"], 1)
                    dve.wait_ge(s["gated"], k + 1)
                    dve.wait_ge(s["masks"], RT * r + u % 2 + 1)
                if not (isinstance(k, int) and k < 2):
                    dve.wait_ge(s["transposed"], (k - 1) * TB)
                nc.vector.memset(spare[:, :], 0.0)
                nc.vector.tensor_tensor_reduce(out=score[u % 2][:, :], in0=part[:, :], in1=mask[:, :], scale=-1.0,
                                               scalar=HIGHEST, op0=ALU.add, op1=ALU.min,
                                               accum_out=neg_top[:, u:u + 1]).then_inc(s["masked"], 1)

            def slot(k, r, u):
                if u == 1:
                    invert(r - 1)
                scores(k, r, u)
                if u == 2:
                    finish(r - 2)
                if layer == 2 and u == 3:
                    finish_elu(r - 2)

            if layer == 2:
                dve.wait_ge(s["bias_in"], 16)
            dve.sem_inc(s["rows_read"], 1)
            rounds(dve, slot)



def layer3_features(nc, g, x_dram, w, a_src, a_tgt, proj_dram, src_dram):
    with ExitStack() as mem:
        x = mem.enter_context(nc.sbuf_tensor("f3_x", [P, NT, D], F32))
        sq = mem.enter_context(nc.sbuf_tensor("f3_sq", [P, NT, D], F32))
        h = mem.enter_context(nc.sbuf_tensor("f3_h", [P, NT, D], F32))
        mean, var = (mem.enter_context(nc.sbuf_tensor(f"f3_{k}", [P, NT], F32)) for k in ("mean", "var"))
        w_sb = mem.enter_context(nc.sbuf_tensor("f3_w", [P, H3, D], F32))
        a_sb = mem.enter_context(nc.sbuf_tensor("f3_a", [P, 2, H3, D], F32))
        wa = mem.enter_context(nc.sbuf_tensor("f3_wa", [P, 2, H3, D], F32))
        w_a = mem.enter_context(nc.sbuf_tensor("f3_w_a", [P, 2, H3], F32))
        proj = [mem.enter_context(nc.sbuf_tensor(f"f3_proj{b}", [P, H3 * D], F32)) for b in range(4)]
        src = mem.enter_context(nc.sbuf_tensor("f3_src", [H3, N], F32))
        tp = [mem.enter_context(nc.psum_tensor(f"f3_tp{b}", [P, BANK], F32)) for b in range(4)]
        ps_tgt = mem.enter_context(nc.psum_tensor("f3_ps_tgt", [P, NT, H3], F32))
        s = sems(nc, mem, "f3", "x_in w_in centered squared var std chain rows weights transposed copied projected "
                                "projected_out sources sources_out src_stored")
        stored = [mem.enter_context(nc.semaphore(f"f3_stored{b}")) for b in range(4)]
        block = mem.enter_context(nc.Block())

        @block.sync
        def _(sp):
            sp.dma_start(x[:, :, :], row_tiles(x_dram)).then_inc(s["x_in"], 16)
            sp.dma_start(w_sb[:, :, :], w.rearrange("h f o -> f h o")).then_inc(s["w_in"], 16)
            for k, a in ((0, a_src), (1, a_tgt)):
                sp.dma_start(a_sb[:, k, :, :].rearrange("p h o -> p (h o)"),
                             a.rearrange("h o -> (h o)").partition_broadcast(P)).then_inc(s["w_in"], 16)
            for t in range(NT):
                sp.wait_ge(s["projected_out"], t + 1)
                sp.dma_start(proj_dram[ts(t, P), :], proj[t % 4][:, :]).then_inc(stored[t % 4], 16)
            sp.wait_ge(s["sources_out"], NCH)
            sp.dma_start(src_dram, src[:, :]).then_inc(s["src_stored"], 16)
            sp.wait_ge(s["src_stored"], 16)
            for b in range(4):
                sp.wait_ge(stored[b], 16 * NT // 4)

        @block.vector
        def _(dve):
            link = Link(dve, s["chain"])
            dve.wait_ge(s["w_in"], 48)
            for k in range(2):
                link(nc.vector.tensor_tensor(wa[:, k, :, :], w_sb[:, :, :], a_sb[:, k, :, :], ALU.mult))
                nc.vector.tensor_reduce(w_a[:, k, :], wa[:, k, :, :], X_AXIS, ALU.add).then_inc(s["weights"], 1)
            dve.wait_ge(s["x_in"], 16)
            layer_norm_dve(nc, dve, link, s, x, h, sq, mean, var)
            nc.vector.tensor_copy(mean[:, 0:1], var[:, 0:1]).then_inc(s["rows"], 1)
            dve.wait_ge(s["projected"], NT)
            nc.vector.tensor_copy(g.tgt[:, :, :], ps_tgt[:, :, :].rearrange("p t h -> p h t"))
            nc.vector.tensor_scalar(g.tgt_sloped[:, :, :], ps_tgt[:, :, :].rearrange("p t h -> p h t"), SLOPE, None, ALU.mult)

        @block.scalar
        def _(act):
            layer_norm_act(nc, act, s, h, sq, var)
            transpose_rows_act(nc, act, lambda c: g.h_t[:, ts(c, BANK)], tp, s["transposed"], s["copied"])
            for c in range(NCH):
                act.wait_ge(s["sources"], c + 1)
                nc.scalar.copy(src[:, ts(c, BANK)], tp[c % 4][0:H3, :]).then_inc(s["sources_out"], 1)
            for t in range(NT):
                act.wait_ge(s["projected"], t + 1)
                if t >= 4:
                    act.wait_ge(stored[t % 4], 16 * (t // 4))
                nc.scalar.copy(proj[t % 4][:, :], tp[t % 4][:, :]).then_inc(s["projected_out"], 1)

        @block.tensor
        def _(pe):
            pe.wait_ge(s["rows"], 1)
            transpose_rows_pe(nc, pe, lambda t: h[:, t, :], tp, g.identity[:, :], s["transposed"], s["copied"])
            pe.wait_ge(s["copied"], NCH)
            pe.wait_ge(s["weights"], 2)
            for c in range(NCH):
                if c >= 4:
                    pe.wait_ge(s["sources_out"], c - 3)
                nc.tensor.matmul(tp[c % 4][0:H3, :], w_a[:, 0, :], g.h_t[:, ts(c, BANK)],
                                 start=True, stop=True).then_inc(s["sources"], 1)
            pe.wait_ge(s["sources_out"], NCH)
            for t in range(NT):
                if t >= 4:
                    pe.wait_ge(s["projected_out"], t - 3)
                nc.tensor.matmul(ps_tgt[:, t, :], g.h_t[:, ts(t, P)], w_a[:, 1, :], start=True, stop=True)
                nc.tensor.matmul(tp[t % 4][:, :], g.h_t[:, ts(t, P)], w_sb[:, :, :].rearrange("p h o -> p (h o)"),
                                 start=True, stop=True).then_inc(s["projected"], 1)


def layer3_attention(nc, g, adj_t, proj_dram, src_dram):
    UN = 4
    NG = NT // UN
    with ExitStack() as mem:
        src = mem.enter_context(nc.sbuf_tensor("e_src", [P, 2, N], F32))
        adj_sb = [mem.enter_context(nc.sbuf_tensor(f"e_adj{b}", [P, N], F32)) for b in range(2)]
        e = [mem.enter_context(nc.sbuf_tensor(f"e_e{b}", [P, N], F32)) for b in range(UN)]
        v = mem.enter_context(nc.sbuf_tensor("e_v", [P, 2, UN, D], F32))
        scaled = [mem.enter_context(nc.sbuf_tensor(f"e_scaled{b}", [P, D], F32)) for b in range(UN)]
        val = mem.enter_context(nc.sbuf_tensor("e_val", [P, N], F32))
        low = mem.enter_context(nc.sbuf_tensor("e_low", [P, N], F32))
        acc = g.acc
        neg_top, total, inv = (mem.enter_context(nc.sbuf_tensor(f"e_{k}", [P, UN], F32))
                                    for k in ("neg_top", "total", "inv"))
        spare = mem.enter_context(nc.sbuf_tensor("e_spare", [P, 1], F32))
        ps = mem.enter_context(nc.psum_tensor("e_ps", [P, NCH, BANK], F32))
        s = sems(nc, mem, "e", "src_in v_in sloped leaky masked exped inv scaled multiplied taken lowered elu_exp "
                               "valued acc_ready")
        adj_in = [mem.enter_context(nc.semaphore(f"e_adj_in{b}")) for b in range(2)]
        block = mem.enter_context(nc.Block())
        adj_v = adj_t.rearrange("(k p) i -> k p i", p=P)
        proj_v = proj_dram.rearrange("(q t p) (h o) -> h q p t o", t=UN, p=P, h=H3)

        def heads_and_groups(eng, head):
            head(0, True)
            with eng.Fori(1, H3) as h:
                head(h, False)

        @block.sync
        def _(sp):
            def load(k, slot):
                src_ap = adj_v[k] if isinstance(k, int) else adj_v[bass.ds(k, 1)].rearrange("o p i -> (o p) i")
                sp.dma_start(adj_sb[slot][:, :], src_ap).then_inc(adj_in[slot], 16)

            def load_src(h, slot):
                row = src_dram[h:h + 1, :] if isinstance(h, int) else src_dram[bass.ds(h, 1), :]
                sp.dma_start(src[:, slot, :], row.rearrange("o n -> (o n)").partition_broadcast(P)).then_inc(s["src_in"], 16)

            load_src(0, 0)
            load(0, 0)
            load(1, 1)
            sp.wait_ge(s["src_in"], 16)
            load_src(1, 1)
            for k in range(2, NT):
                sp.wait_ge(s["masked"], k - 1)
                load(k, k % 2)

            def head(h, last):
                if not last:
                    sp.wait_ge(s["leaky"], h * NT)
                    sp.wait_ge(s["src_in"], (h + 1) * 16)
                    slots = src[:, bass.ds((h + 1) % 2, 1), :].rearrange("p o n -> p (o n)")
                    sp.dma_start(slots, src_dram[bass.ds(h + 1, 1), :].rearrange("o n -> (o n)").partition_broadcast(P)
                                 ).then_inc(s["src_in"], 16)
                with sp.Fori(0, NT // 2) as m:
                    for b in range(2):
                        sp.wait_ge(s["masked"], h * NT + m * 2 + b - 1)
                        load(m * 2 + b, b)

            with sp.Fori(1, H3 - 1) as h:
                head(h, False)
            head(H3 - 1, True)

        @block.gpsimd
        def _(pool):
            def load(h, q, slot):
                rows = proj_v[h, q] if isinstance(h, int) and isinstance(q, int) else \
                    proj_v[(slice(h, h + 1) if isinstance(h, int) else bass.ds(h, 1)),
                           (slice(q, q + 1) if isinstance(q, int) else bass.ds(q, 1))].rearrange("a b p t o -> (a b p) t o")
                pool.dma_start(v[:, slot, :, :], rows).then_inc(s["v_in"], 16)

            load(0, 0, 0)
            pool.wait_ge(s["v_in"], 16)
            load(0, 1, 1)

            def group(h, q):
                g_at = h * NG + q
                pool.wait_ge(s["scaled"], g_at * UN - UN)
                pool.wait_ge(s["v_in"], g_at * 16)
                rows = proj_v[(slice(h, h + 1) if isinstance(h, int) else bass.ds(h, 1)),
                              bass.ds(q, 1)].rearrange("a b p t o -> (a b p) t o")
                pool.dma_start(v[:, bass.ds(q % 2, 1), :, :].rearrange("p a t o -> p (a t) o"), rows).then_inc(s["v_in"], 16)

            with pool.Fori(2, NG) as q:
                group(0, q)
            with pool.Fori(1, H3) as h:
                with pool.Fori(0, NG) as q:
                    group(h, q)

        @block.tensor
        def _(pe):
            def group(h, q, first_head, first_group):
                for u in range(UN):
                    k = h * NT + q * UN + u
                    begin = first_group and u == 0
                    pe.wait_ge(s["scaled"], k + 1)
                    for c in range(NCH):
                        if begin and not first_head:
                            pe.wait_ge(s["taken"], (h - 1) * NCH + c + 1)
                        if first_group:
                            mm = nc.tensor.matmul(ps[:, c, :], scaled[u][:, :], e[u][:, ts(c, BANK)],
                                                  start=begin, stop=False, skip_group_check=True)
                        else:
                            mm = nc.tensor.matmul(ps[:, c, :], scaled[u][:, :], e[u][:, ts(c, BANK)],
                                                  start=False, stop=(u == UN - 1), skip_group_check=True)
                    mm.then_inc(s["multiplied"], 1)

            def head(h, first):
                group(h, 0, first, True)
                with pe.Fori(1, NG) as q:
                    group(h, q, first, False)

            heads_and_groups(pe, head)

        @block.scalar
        def _(act):
            def softmax(k, u):
                act.wait_ge(s["masked"], k + 1)
                nc.scalar.activation(e[u][:, :], e[u][:, :], ACT.Exp, scale=-1.0, bias=neg_top[:, u:u + 1],
                                     accum_out=total[:, u:u + 1]).then_inc(s["exped"], 1)

            def group(h, q, first_head, first_group):
                for u in range(UN):
                    k = h * NT + q * UN + u
                    start = first_head and first_group
                    if first_group and u == 0:
                        act.wait_ge(s["src_in"], (h + 1) * 16)
                    if not start:
                        act.wait_ge(s["multiplied"], k - UN + 1)
                    col = g.tgt_sloped[:, :, :].rearrange("p h t -> p (h t)")
                    col = col[:, k:k + 1] if start else col[:, bass.ds(k, 1)]
                    row = src[:, 0, :] if first_head else src[:, bass.ds(h % 2, 1), :].rearrange("p o n -> p (o n)")
                    nc.scalar.activation(e[u][:, :], row, ACT.Identity, scale=SLOPE, bias=col).then_inc(s["sloped"], 1)
                    if not (start and u == 0):
                        softmax(k - 1, (u - 1) % UN)
                    if first_group and u == UN - 1 and not first_head:
                        elu_exp(h - 1)

            def elu_exp(h):
                act.wait_ge(s["lowered"], h + 1)
                nc.scalar.activation(low[:, :], low[:, :], ACT.Exp).then_inc(s["elu_exp"], 1)

            def head(h, first):
                group(h, 0, first, True)
                with act.Fori(1, NG) as q:
                    group(h, q, first, False)

            heads_and_groups(act, head)
            softmax(H3 * NT - 1, UN - 1)
            elu_exp(H3 - 1)

        @block.vector
        def _(dve):
            def scale(h, q, k, u):
                dve.wait_ge(s["exped"], k + 1)
                nc.vector.reciprocal(inv[:, u:u + 1], total[:, u:u + 1]).then_inc(s["inv"], 1)
                dve.wait_ge(s["v_in"], (h * NG + q + 1) * 16)
                dve.wait_ge(s["inv"], k + 1)
                rows = v[:, q % 2, u, :] if isinstance(q, int) else \
                    v[:, bass.ds(q % 2, 1), u, :].rearrange("p o d -> p (o d)")
                nc.vector.tensor_scalar(scaled[u][:, :], rows, inv[:, u:u + 1], None, ALU.mult).then_inc(s["scaled"], 1)

            def take(h):
                dve.wait_ge(s["multiplied"], (h + 1) * NT)
                for c in range(NCH):
                    nc.vector.tensor_tensor(val[:, ts(c, BANK)], ps[:, c, :], g.h_t[:, ts(c, BANK)],
                                            ALU.add).then_inc(s["taken"], 1)

            def lower(h):
                dve.wait_ge(s["taken"], (h + 1) * NCH)
                nc.vector.tensor_scalar(low[:, :], val[:, :], 0.0, None, ALU.min).then_inc(s["lowered"], 1)

            def add_elu(h):
                dve.wait_ge(s["elu_exp"], h + 1)
                nc.vector.scalar_tensor_tensor(val[:, :], val[:, :], 0.0, low[:, :], ALU.max, ALU.add).then_inc(s["valued"], 1)
                dve.wait_ge(s["valued"], h + 1)
                dve.wait_ge(s["acc_ready"], h + 1)
                nc.vector.scalar_tensor_tensor(acc[:, :], val[:, :], -1.0, acc[:, :], ALU.add, ALU.add).then_inc(s["acc_ready"], 1)

            def group(h, q, first_head, first_group):
                for u in range(UN):
                    k = h * NT + q * UN + u
                    dve.wait_ge(adj_in[u % 2], (k // 2 + 1) * 16 if isinstance(k, int) else
                                (h * (NT // 2) + q * (UN // 2) + u // 2 + 1) * 16)
                    dve.wait_ge(s["sloped"], k + 1)
                    start = first_head and first_group
                    col = g.tgt[:, :, :].rearrange("p h t -> p (h t)")
                    col = col[:, k:k + 1] if start else col[:, bass.ds(k, 1)]
                    row = src[:, 0, :] if first_head else src[:, bass.ds(h % 2, 1), :].rearrange("p o n -> p (o n)")
                    nc.vector.scalar_tensor_tensor(e[u][:, :], row, col, e[u][:, :], ALU.add, ALU.max).then_inc(s["leaky"], 1)
                    dve.wait_ge(s["leaky"], k + 1)
                    boundary = first_group and not first_head
                    if boundary and u == 1:
                        take(h - 1)
                    if boundary and u == 2:
                        lower(h - 1)
                    if first_head and first_group and u == 0:
                        nc.vector.memset(spare[:, :], 0.0)
                    elif u > 0:
                        scale(h, q, k - 1, u - 1)
                    elif first_group:
                        scale(h - 1, NG - 1, k - 1, UN - 1)
                    else:
                        scale(h, q - 1, k - 1, UN - 1)
                    nc.vector.tensor_tensor_reduce(out=e[u][:, :], in0=e[u][:, :], in1=adj_sb[u % 2][:, :], scale=-1.0,
                                                   scalar=HIGHEST, op0=ALU.add, op1=ALU.min,
                                                   accum_out=neg_top[:, u:u + 1]).then_inc(s["masked"], 1)
                if first_group and not first_head:
                    add_elu(h - 1)

            def head(h, first):
                group(h, 0, first, True)
                with dve.Fori(1, NG) as q:
                    group(h, q, first, False)

            nc.vector.memset(acc[:, :], 0.0).then_inc(s["acc_ready"], 1)
            heads_and_groups(dve, head)
            scale(H3 - 1, NG - 1, H3 * NT - 1, UN - 1)
            take(H3 - 1)
            lower(H3 - 1)
            add_elu(H3 - 1)


def layer3_output(nc, g, x_dram, out):
    with ExitStack() as mem:
        x = mem.enter_context(nc.sbuf_tensor("o_x", [P, NT, D], F32))
        tp = [mem.enter_context(nc.psum_tensor(f"o_tp{b}", [P, BANK], F32)) for b in range(4)]
        s = sems(nc, mem, "o", "x_in transposed added x_out")
        block = mem.enter_context(nc.Block())

        @block.sync
        def _(sp):
            sp.dma_start(x[:, :, :], row_tiles(x_dram)).then_inc(s["x_in"], 16)
            for c in range(NCH):
                sp.wait_ge(s["added"], c + 1)
                sp.dma_start(row_tiles(out)[:, ts(c, TPB), :], x[:, ts(c, TPB), :]).then_inc(s["x_out"], 16)
            sp.wait_ge(s["x_out"], 16 * NCH)

        @block.tensor
        def _(pe):
            transpose_rows_pe(nc, pe, lambda t: g.acc[:, ts(t, P)], tp, g.identity[:, :], s["transposed"], s["added"])

        @block.vector
        def _(dve):
            dve.wait_ge(s["x_in"], 16)
            for c in range(NCH):
                dve.wait_ge(s["transposed"], c + 1)
                part = x[:, ts(c, TPB), :].rearrange("p t d -> p (t d)")
                nc.vector.scalar_tensor_tensor(part, tp[c % 4][:, :], 1.0 / H3, part, ALU.mult, ALU.add).then_inc(s["added"], 1)


def build(nc, x, adj, w, out):
    adj_t = nc.dram_tensor("adj_t", [N, N], F32, kind="Internal").ap()
    proj = nc.dram_tensor("proj", [N, H3 * D], F32, kind="Internal").ap()
    src = nc.dram_tensor("src", [H3, N], F32, kind="Internal").ap()
    x1, x2, x3 = (nc.dram_tensor(f"x{k}", [N, D], F32, kind="Internal").ap() for k in (1, 2, 3))
    first_sem = next_semaphore(nc)
    with ExitStack() as mem:
        g = Shared()
        g.identity = mem.enter_context(nc.sbuf_tensor("identity", [P, P], F32))
        g.ones = mem.enter_context(nc.sbuf_tensor("ones", [P, P], F32))
        with nc.sbuf_tensor("rows", [P, NT, D], F32) as rows:
            g.rows = rows
            layer0_features(nc, g, x)
            with nc.sbuf_tensor("agg_t", [P, N], F32) as agg_t:
                g.agg_t = agg_t
                layer0_aggregate(nc, g, adj, adj_t)
                layer0_combine(nc, g, w["L0_gnn_W1"], w["L0_gnn_b1"], w["L0_gnn_W2"], w["L0_gnn_b2"], x, x1)
            with ExitStack() as m1:
                g.unit_t = m1.enter_context(nc.sbuf_tensor("unit_t", [P, N], F32))
                g.log_row = m1.enter_context(nc.sbuf_tensor("log_row", [P, N], F32))
                g.half_log = m1.enter_context(nc.sbuf_tensor("half_log", [P, NT], F32))
                g.half_beta = m1.enter_context(nc.sbuf_tensor("half_beta", [P, 1], F32))
                layer1_features(nc, g, x1, w["L1_gnn_beta"])
                masked_attention(nc, g, 1, adj, x1, x2)
            clear_semaphores(nc, first_sem, next_semaphore(nc))
            with ExitStack() as m2:
                g.neigh_row = m2.enter_context(nc.sbuf_tensor("neigh_row", [P, H2, N], F32))
                g.self_col = m2.enter_context(nc.sbuf_tensor("self_col", [P, NT, H2], F32))
                layer2_features(nc, g, x2, w["L2_gnn_W"], w["L2_gnn_a_self"], w["L2_gnn_a_neigh"])
                masked_attention(nc, g, 2, adj, x2, x3, bias=w["L2_gnn_bias"])
        g.h_t = mem.enter_context(nc.sbuf_tensor("h_t", [P, N], F32))
        g.tgt = mem.enter_context(nc.sbuf_tensor("tgt", [P, H3, NT], F32))
        g.tgt_sloped = mem.enter_context(nc.sbuf_tensor("tgt_sloped", [P, H3, NT], F32))
        g.acc = mem.enter_context(nc.sbuf_tensor("acc", [P, N], F32))
        layer3_features(nc, g, x3, w["L3_gnn_W"], w["L3_gnn_a_src"], w["L3_gnn_a_tgt"], proj, src)
        layer3_attention(nc, g, adj_t, proj, src)
        layer3_output(nc, g, x3, out)


_INS = ['x', 'adj', 'L0_gnn_W1', 'L0_gnn_b1', 'L0_gnn_W2', 'L0_gnn_b2', 'L1_gnn_beta', 'L2_gnn_W', 'L2_gnn_a_self',
        'L2_gnn_a_neigh', 'L2_gnn_bias', 'L3_gnn_W', 'L3_gnn_a_src', 'L3_gnn_a_tgt']


def kernel(**inputs):
    import numpy as _np
    import concourse.bacc as _bacc
    from concourse import mybir as _mybir
    from concourse.bass_utils import run_bass_kernel_spmd as _run

    nc = _bacc.Bacc("TRN2", target_bir_lowering=False, num_devices=1)
    arrays, args = {}, {}
    for name in _INS:
        a = _np.ascontiguousarray(inputs[name])
        arrays[f"in_{name}_dram"] = a
        args[name] = nc.dram_tensor(f"in_{name}_dram", a.shape, _mybir.dt.from_np(a.dtype), kind="ExternalInput").ap()
    out = nc.dram_tensor("out_0_dram", (N, D), _mybir.dt.float32, kind="ExternalOutput").ap()
    build(nc, args["x"], args["adj"], args, out)
    r = _run(nc, [arrays], core_ids=[0])
    return r.results[0]["out_0_dram"]
```

```python
from contextlib import ExitStack

import numpy as np

import concourse.bass as bass
import concourse.mybir as mybir

F32 = mybir.dt.float32
F16 = mybir.dt.float16
I32 = mybir.dt.int32
ALU = mybir.AluOpType
ACT = mybir.ActivationFunctionType
X_AXIS = mybir.AxisListType.X

P = 128
N = 4096
D = 128
HID = 256
NT = N // P
BANK = 512
TPB = BANK // P
NCH = N // BANK
NQ = 4
QT = NT // NQ
H2, DH2 = 2, 64
H3 = 4
LN_EPS = 1e-5
MIN_NORM = 1e-7
NEG = 1e9
SLOPE = 0.2
_Z0 = float(np.float32(1.0) + np.float32(MIN_NORM))
THETA_MIN = float(np.log(_Z0 + np.sqrt(_Z0 * _Z0 - 1.0)))


TINY_NORM = 1e-18
LOG_EPS = float(np.log(1e-7))
UNIT = 64.0
EXPONENT_BITS = 0x7F800000
HIGHEST = float(np.finfo(np.float32).max)


class Shared:
    pass


def ts(i, n):
    return slice(i * n, (i + 1) * n)


class Link:

    def __init__(self, eng, sem):
        self.eng, self.sem, self.n = eng, sem, 0

    def __call__(self, ins):
        self.n += 1
        ins.then_inc(self.sem, 1)
        self.eng.wait_ge(self.sem, self.n)


def over_rows(col, n=NT):
    return col.unsqueeze(2).to_broadcast([P, n, D])


def row_tiles(dram):
    return dram.rearrange("(t p) d -> p t d", p=P)



def load_rows(nc, sp, rows, dram, s):
    for q in range(NQ):
        sp.dma_start(rows[:, ts(q, QT), :], row_tiles(dram)[:, ts(q, QT), :]).then_inc(s[f"x_in{q}"], 16)


def attention_tiles(nc, g, mem, layer):
    g.adj_sb = [mem.enter_context(nc.sbuf_tensor(f"adj_sb{layer}{b}", [P, N], F32)) for b in range(2)]
    g.adj_in = [mem.enter_context(nc.semaphore(f"adj_in{layer}{b}")) for b in range(2)]


def prefetch_tiles(sp, g, tiles):
    for b in range(2):
        sp.dma_start(g.adj_sb[b][:, :], tiles[b]).then_inc(g.adj_in[b], 16)


def center_dve(nc, link, s, q, rows, h, mean):
    t = ts(q, QT)
    link(nc.vector.tensor_reduce(mean[:, t], rows[:, t, :], X_AXIS, ALU.add))
    link(nc.vector.tensor_scalar(mean[:, t], mean[:, t], 1.0 / D, None, ALU.mult))
    nc.vector.tensor_tensor(h[:, t, :], rows[:, t, :], over_rows(mean[:, t], QT), ALU.subtract).then_inc(s["centered"], 1)


def sum_squares_dve(nc, dve, s, q, before, sq, total):
    dve.wait_ge(s["squared"], before + q + 1)
    return nc.vector.tensor_reduce(total[:, ts(q, QT)], sq[:, ts(q, QT), :], X_AXIS, ALU.add)


def scale_dve(nc, dve, link, s, h, var, loads=""):
    nc.vector.tensor_scalar(var[:, :], var[:, :], 1.0 / D, LN_EPS, ALU.mult, ALU.add).then_inc(s["var"], 1)
    dve.wait_ge(s["std"], 1)
    link(nc.vector.reciprocal(var[:, :], var[:, :]))
    for q in range(NQ):
        t = ts(q, QT)
        if loads:
            dve.wait_ge(s[loads.split()[q]], 16)
        nc.vector.scalar_tensor_tensor(h[:, t, :], h[:, t, :], 0.0, over_rows(var[:, t], QT),
                                       ALU.max, ALU.mult).then_inc(s["rows"], 1)


def layer_norm_dve(nc, dve, link, s, rows, h, sq, mean, var):
    for q in range(NQ):
        dve.wait_ge(s[f"x_in{q}"], 16)
        center_dve(nc, link, s, q, rows, h, mean)
    for q in range(NQ - 1):
        sum_squares_dve(nc, dve, s, q, 0, sq, var)
    link(sum_squares_dve(nc, dve, s, NQ - 1, 0, sq, var))
    dve.wait_ge(s["centered"], NQ)
    scale_dve(nc, dve, link, s, h, var)


def squares_act(nc, act, s, ready, h, sq):
    for q in range(NQ):
        act.wait_ge(s[ready], q + 1)
        nc.scalar.activation(sq[:, ts(q, QT), :], h[:, ts(q, QT), :], ACT.Square).then_inc(s["squared"], 1)


def root_act(nc, act, s, var):
    act.wait_ge(s["var"], 1)
    nc.scalar.activation(var[:, :], var[:, :], ACT.Sqrt).then_inc(s["std"], 1)


def layer_norm_act(nc, act, s, h, sq, var):
    squares_act(nc, act, s, "centered", h, sq)
    root_act(nc, act, s, var)


def transpose_rows_pe(nc, pe, rows, banks, identity, done, taken, ready=None):
    for c in range(NCH):
        if c >= len(banks):
            pe.wait_ge(taken, c - len(banks) + 1)
        if ready is not None and c % (NCH // NQ) == 0:
            pe.wait_ge(ready, c // (NCH // NQ) + 1)
        for s in range(TPB):
            last = nc.tensor.transpose(banks[c % len(banks)][:, ts(s, P)], rows(c * TPB + s), identity)
        last.then_inc(done, 1)


def transpose_rows_act(nc, act, out, banks, done, taken):
    for c in range(NCH):
        act.wait_ge(done, c + 1)
        nc.scalar.copy(out(c), banks[c % len(banks)][:, :]).then_inc(taken, 1)


def next_semaphore(nc):
    with nc.semaphore("unused") as sem:
        return sem.num


def clear_semaphores(nc, first, end):
    with nc.Block() as block:
        @block.gpsimd
        def _(pool):
            pool.sem_clear(range(first, end))


X_IN = "".join(f"x_in{q} " for q in range(NQ))


def sems(nc, mem, phase, names):
    return {n: mem.enter_context(nc.semaphore(f"{phase}_{n}")) for n in names.split()}



GR = BANK // P
CHT = 8


def load_blocks(sp, g, adj, grp, c):
    adj_v = adj.rearrange("(gr s p) j -> gr p s j", s=GR, p=P)
    src = adj_v[grp] if isinstance(grp, int) else adj_v[bass.ds(grp, 1)].rearrange("o p s j -> (o p) s j")
    sp.dma_start(g.blk[c][:, :, :], src[:, :, ts(c, CHT * P)]).then_inc(g.loaded[c], 16)


def layer0_features(nc, g, x_dram, adj):
    with ExitStack() as mem:
        x = mem.enter_context(nc.sbuf_tensor("l0_x", [P, NT, D], F32))
        sq = mem.enter_context(nc.sbuf_tensor("l0_sq", [P, NT, D], F32))
        mean, var, inv = (mem.enter_context(nc.sbuf_tensor(f"l0_{n}", [P, NT], F32)) for n in ("mean", "var", "inv"))
        s = sems(nc, mem, "l0", X_IN + "ident zeroed centered squared var std rows tangent norm2 norm chain")
        h = g.rows
        block = mem.enter_context(nc.Block())

        @block.sync
        def _(sp):
            load_rows(nc, sp, x, x_dram, s)
            for c in range(len(g.blk)):
                load_blocks(sp, g, adj, 0, c)

        @block.gpsimd
        def _(pool):
            nc.gpsimd.memset(g.ones[:, :], 1.0).then_inc(s["ident"], 1)
            nc.gpsimd.memset(g.identity[:, :], 0.0).then_inc(s["zeroed"], 1)
            pool.wait_ge(s["zeroed"], 1)
            nc.gpsimd.affine_select(out=g.identity[:, :], in_=g.identity[:, :], compare_op=ALU.not_equal,
                                    fill=1.0, base=0, pattern=[[-1, P]], channel_multiplier=1).then_inc(s["ident"], 1)

        @block.vector
        def _(dve):
            link = Link(dve, s["chain"])
            layer_norm_dve(nc, dve, link, s, x, h, sq, mean, var)
            dve.wait_ge(s["rows"], NQ)
            for q in range(NQ):
                nc.vector.memset(h[:, ts(q, QT), 0:1], 0.0).then_inc(s["tangent"], 1)
            for q in range(NQ):
                last = sum_squares_dve(nc, dve, s, q, NQ, sq, var)
            last.then_inc(s["norm2"], 1)
            dve.wait_ge(s["norm"], 1)
            link(nc.vector.tensor_scalar(var[:, :], var[:, :], MIN_NORM, None, ALU.max))
            link(nc.vector.reciprocal(inv[:, :], var[:, :]))
            link(nc.vector.tensor_scalar(var[:, :], var[:, :], THETA_MIN, None, ALU.max))
            link(nc.vector.tensor_tensor(var[:, :], var[:, :], inv[:, :], ALU.mult))
            link(nc.vector.tensor_tensor(h[:, :, :], h[:, :, :], over_rows(var[:, :]), ALU.mult))

        @block.scalar
        def _(act):
            layer_norm_act(nc, act, s, h, sq, var)
            squares_act(nc, act, s, "tangent", h, sq)
            act.wait_ge(s["norm2"], 1)
            nc.scalar.activation(var[:, :], var[:, :], ACT.Sqrt).then_inc(s["norm"], 1)


def layer0_aggregate(nc, g, adj, adj_t):
    NG = NT // GR
    NLOAD = NT // CHT
    STT = 4
    NST = NT // STT
    SLOTS = 4
    BANKS = 4
    with ExitStack() as mem:
        blk, loaded = g.blk, g.loaded
        out = [mem.enter_context(nc.sbuf_tensor(f"a_out{c}", [P, STT, BANK], F32)) for c in range(SLOTS)]
        tp = [mem.enter_context(nc.psum_tensor(f"a_tp{b}", [P, BANK], F32)) for b in range(BANKS)]
        acc = mem.enter_context(nc.psum_tensor("a_acc", [P, BANK], F32))
        s = sems(nc, mem, "a", "transposed copied_act copied_dve multiplied summed taken")
        stored = [mem.enter_context(nc.semaphore(f"a_stored{c}")) for c in range(SLOTS)]
        block = mem.enter_context(nc.Block())
        adj_t_v = adj_t.rearrange("(q t p) i -> q p t i", t=STT, p=P)

        def columns(grp):
            if isinstance(grp, int):
                return slice(grp * BANK, (grp + 1) * BANK)
            return bass.ds(grp * BANK, BANK)

        @block.sync
        def _(sp):
            def stores(grp, c):
                for q in (2 * c, 2 * c + 1):
                    sp.wait_ge(s["multiplied"], grp * NT + (q + 1) * STT)
                    sp.dma_start(adj_t_v[q, :, :, columns(grp)], out[q % SLOTS][:, :, :]).then_inc(stored[q % SLOTS], 16)

            with sp.Fori(0, NG - 1) as grp:
                for c in range(NLOAD):
                    stores(grp, c)
                    load_blocks(sp, g, adj, grp + 1, c)
            for c in range(NLOAD):
                stores(NG - 1, c)
            for c in range(SLOTS):
                sp.wait_ge(stored[c], 16 * NG * NST // SLOTS)

        @block.tensor
        def _(pe):
            def copied(grp, jt, ahead):
                return grp * (NT // 2) + (jt - ahead) // 2 + 1

            def group(grp, first):
                for jt in range(NT + 1):
                    if jt < NT:
                        if jt % CHT == 0:
                            pe.wait_ge(loaded[jt // CHT], grp * 16 + 16)
                        if not (first and jt < BANKS):
                            pe.wait_ge((s["copied_act"], s["copied_dve"])[jt % 2], copied(grp, jt, BANKS))
                        for r in range(GR):
                            last = nc.tensor.transpose(tp[jt % BANKS][:, ts(r, P)],
                                                       blk[jt // CHT][:, r, ts(jt % CHT, P)], g.identity[:, :])
                        last.then_inc(s["transposed"], 1)
                    if jt > 0:
                        m = jt - 1
                        pe.wait_ge((s["copied_act"], s["copied_dve"])[m % 2], copied(grp, m, 0))
                        if m == 0 and not first:
                            pe.wait_ge(s["taken"], grp)
                        mm = nc.tensor.matmul(acc[:, :], g.rows[:, m, :], out[(m // STT) % SLOTS][:, m % STT, :],
                                              start=(m == 0), stop=(m == NT - 1))
                        mm.then_inc(s["multiplied"], 1)

            group(0, True)
            with pe.Fori(1, NG) as grp:
                group(grp, False)

        def copies(eng, copy, odd, copied_sem):
            def group(grp, first):
                for jt in range(odd, NT, 2):
                    q = jt // STT
                    if jt % STT == odd and not (first and q < SLOTS):
                        eng.wait_ge(stored[q % SLOTS], (grp * (NST // SLOTS) + q // SLOTS) * 16)
                    eng.wait_ge(s["transposed"], grp * NT + jt + 1)
                    copy(out[q % SLOTS][:, jt % STT, :], tp[jt % BANKS][:, :]).then_inc(copied_sem, 1)
                if not odd:
                    eng.wait_ge(s["multiplied"], grp * NT + NT)
                    copy(g.agg_t[:, columns(grp)], acc[:, :]).then_inc(s["taken"], 1)

            group(0, True)
            with eng.Fori(1, NG) as grp:
                group(grp, False)

        @block.scalar
        def _(act):
            copies(act, nc.scalar.copy, 0, s["copied_act"])

        @block.vector
        def _(dve):
            copies(dve, nc.vector.tensor_copy, 1, s["copied_dve"])


def layer0_combine(nc, g, w1, b1, w2, b2, x_dram, x1_dram):
    HM = HID // P
    with ExitStack() as mem:
        agg = mem.enter_context(nc.sbuf_tensor("c_agg", [P, NT, D], F32))
        sq = mem.enter_context(nc.sbuf_tensor("c_sq", [P, NT, D], F32))
        x = mem.enter_context(nc.sbuf_tensor("c_x", [P, NT, D], F32))
        w1_sb = mem.enter_context(nc.sbuf_tensor("c_w1", [P, HID], F32))
        w2_sb = mem.enter_context(nc.sbuf_tensor("c_w2", [P, HM, D], F32))
        b1_sb = mem.enter_context(nc.sbuf_tensor("c_b1", [P, HM], F32))
        b2_sb = mem.enter_context(nc.sbuf_tensor("c_b2", [P, 1, D], F32))
        hid = [[mem.enter_context(nc.sbuf_tensor(f"c_hid{b}{m}", [P, BANK], F32)) for m in range(HM)] for b in range(2)]
        mean, n, inv, e, cosh = (mem.enter_context(nc.sbuf_tensor(f"c_{k}", [P, NT], F32)) for k in ("mean", "n", "inv", "e", "cosh"))
        banks = [mem.enter_context(nc.psum_tensor(f"c_bank{b}", [P, BANK], F32)) for b in range(2 * HM)]
        mlp = [mem.enter_context(nc.psum_tensor(f"c_mlp{b}", [P, BANK], F32)) for b in range(2)]
        s = sems(nc, mem, "c", "weights x_in x_out t1 t1_out t2 t2_out chain moved v clamped squared norm2 norm e "
                               "out_ready pre hid mlp added biased centered summed")
        agg_t = g.agg_t
        CPQ = NCH // NQ
        block = mem.enter_context(nc.Block())

        @block.sync
        def _(sp):
            sp.dma_start(x[:, :, :], row_tiles(x_dram)).then_inc(s["x_in"], 16)
            sp.dma_start(w1_sb[:, :], w1).then_inc(s["weights"], 16)
            sp.dma_start(w2_sb[:, :, :], w2.rearrange("(m p) d -> p m d", p=P)).then_inc(s["weights"], 16)
            with nc.allow_non_contiguous_dma("two columns of biases"):
                sp.dma_start(b1_sb[:, :], b1.rearrange("(m p) -> p m", p=P)).then_inc(s["weights"], 16)
            sp.dma_start(b2_sb[:, 0, :], b2.partition_broadcast(P)).then_inc(s["weights"], 16)
            for q in range(NQ):
                sp.wait_ge(s["added"], (q + 1) * CPQ)
                sp.dma_start(row_tiles(x1_dram)[:, ts(q, QT), :], x[:, ts(q, QT), :]).then_inc(s["x_out"], 16)
            sp.wait_ge(s["x_out"], 16 * NQ)

        @block.tensor
        def _(pe):
            transpose_rows_pe(nc, pe, lambda t: agg_t[:, ts(t, P)], banks, g.identity[:, :], s["t1"], s["t1_out"])
            pe.wait_ge(s["t1_out"], NCH)
            transpose_rows_pe(nc, pe, lambda t: agg[:, t, :], banks, g.identity[:, :], s["t2"], s["t2_out"], s["out_ready"])
            pe.wait_ge(s["weights"], 64)
            pe.wait_ge(s["t2_out"], NCH)

            def hidden(c):
                if c >= 2:
                    pe.wait_ge(s["hid"], (c - 1) * HM)
                for m in range(HM):
                    nc.tensor.matmul(banks[c % 2 * HM + m][:, :], w1_sb[:, ts(m, P)], agg_t[:, ts(c, BANK)],
                                     start=True, stop=True).then_inc(s["pre"], 1)

            def output(c):
                if c >= 2:
                    pe.wait_ge(s["added"], c - 1)
                pe.wait_ge(s["hid"], (c + 1) * HM)
                for r in range(TPB):
                    for m in range(HM):
                        last = nc.tensor.matmul(mlp[c % 2][:, ts(r, D)], hid[c % 2][m][:, ts(r, P)], w2_sb[:, m, :],
                                                start=(m == 0), stop=(m == HM - 1))
                last.then_inc(s["mlp"], 1)

            hidden(0)
            for c in range(NCH):
                if c + 1 < NCH:
                    hidden(c + 1)
                output(c)

        @block.scalar
        def _(act):
            for c in range(NCH):
                act.wait_ge(s["t1"], c + 1)
                nc.scalar.copy(agg[:, ts(c, TPB), :].rearrange("p t d -> p (t d)"), banks[c % len(banks)][:, :]).then_inc(s["t1_out"], 1)
                if c % CPQ == CPQ - 1:
                    q = c // CPQ
                    act.wait_ge(s["t1_out"], c + 1)
                    nc.scalar.activation(sq[:, ts(q, QT), :], agg[:, ts(q, QT), :], ACT.Square).then_inc(s["squared"], 1)
            act.wait_ge(s["norm2"], 1)
            nc.scalar.activation(n[:, :], n[:, :], ACT.Sqrt).then_inc(s["norm"], 1)
            squares_act(nc, act, s, "v", agg, sq)
            act.wait_ge(s["norm2"], 2)
            nc.scalar.activation(n[:, :], n[:, :], ACT.Sqrt).then_inc(s["norm"], 1)
            act.wait_ge(s["clamped"], 1)
            nc.scalar.activation(e[:, :], n[:, :], ACT.Exp).then_inc(s["e"], 1)
            transpose_rows_act(nc, act, lambda c: agg_t[:, ts(c, BANK)], banks, s["t2"], s["t2_out"])
            act.wait_ge(s["weights"], 64)

            def centered_squares(q):
                act.wait_ge(s["centered"], q + 1)
                nc.scalar.activation(sq[:, ts(q, QT), :], g.rows[:, ts(q, QT), :], ACT.Square).then_inc(s["squared"], 1)

            for c in range(NCH):
                for m in range(HM):
                    act.wait_ge(s["pre"], c * HM + m + 1)
                    if c >= 2 and m == 0:
                        act.wait_ge(s["mlp"], c - 1)
                    nc.scalar.activation(hid[c % 2][m][:, :], banks[c % 2 * HM + m][:, :], ACT.Relu,
                                         bias=b1_sb[:, m:m + 1]).then_inc(s["hid"], 1)
                if c >= 2 and c % CPQ == 0:
                    centered_squares(c // CPQ - 1)
            centered_squares(NQ - 1)

        @block.vector
        def _(dve):
            link = Link(dve, s["chain"])
            for q in range(NQ):
                last = sum_squares_dve(nc, dve, s, q, 0, sq, n)
            last.then_inc(s["norm2"], 1)
            dve.wait_ge(s["norm"], 1)
            link(nc.vector.tensor_scalar(n[:, :], n[:, :], MIN_NORM, None, ALU.max))
            link(nc.vector.reciprocal(inv[:, :], n[:, :]))
            link(nc.vector.tensor_scalar(n[:, :], n[:, :], THETA_MIN, None, ALU.max))
            link(nc.vector.tensor_tensor(n[:, :], n[:, :], inv[:, :], ALU.mult))
            for q in range(NQ):
                t = ts(q, QT)
                nc.vector.tensor_tensor(agg[:, t, :], agg[:, t, :], over_rows(n[:, t], QT), ALU.mult).then_inc(s["moved"], 1)
                dve.wait_ge(s["moved"], q + 1)
                nc.vector.tensor_tensor(agg[:, t, :], agg[:, t, :], g.rows[:, t, :], ALU.add).then_inc(s["v"], 1)
            for q in range(NQ):
                last = sum_squares_dve(nc, dve, s, q, NQ, sq, n)
            last.then_inc(s["norm2"], 1)
            dve.wait_ge(s["weights"], 64)
            dve.wait_ge(s["x_in"], 16)
            half = ts(0, NT // 2)
            nc.vector.tensor_tensor(x[:, half, :], x[:, half, :], b2_sb[:, :, :].to_broadcast([P, NT // 2, D]),
                                    ALU.add).then_inc(s["biased"], 1)
            dve.wait_ge(s["norm"], 2)
            nc.vector.tensor_scalar(n[:, :], n[:, :], MIN_NORM, None, ALU.max).then_inc(s["clamped"], 1)
            dve.wait_ge(s["clamped"], 1)
            link(nc.vector.reciprocal(inv[:, :], n[:, :]))
            dve.wait_ge(s["e"], 1)
            link(nc.vector.reciprocal(n[:, :], e[:, :]))
            link(nc.vector.tensor_tensor(cosh[:, :], e[:, :], n[:, :], ALU.add))
            link(nc.vector.tensor_scalar(cosh[:, :], cosh[:, :], 0.5, None, ALU.mult))
            link(nc.vector.tensor_tensor(e[:, :], e[:, :], n[:, :], ALU.subtract))
            link(nc.vector.scalar_tensor_tensor(e[:, :], e[:, :], 0.5, inv[:, :], ALU.mult, ALU.mult))
            for q in range(NQ):
                t = ts(q, QT)
                link(nc.vector.tensor_tensor(agg[:, t, :], agg[:, t, :], over_rows(e[:, t], QT), ALU.mult))
                nc.vector.tensor_copy(agg[:, t, 0:1], cosh[:, t].unsqueeze(2)).then_inc(s["out_ready"], 1)
            half = ts(1, NT // 2)
            nc.vector.tensor_tensor(x[:, half, :], x[:, half, :], b2_sb[:, :, :].to_broadcast([P, NT // 2, D]),
                                    ALU.add).then_inc(s["biased"], 1)
            dve.wait_ge(s["biased"], 2)
            dve.wait_ge(s["v"], NQ)
            for c in range(NCH):
                dve.wait_ge(s["mlp"], c + 1)
                part = x[:, ts(c, TPB), :].rearrange("p t d -> p (t d)")
                nc.vector.tensor_tensor(part, mlp[c % 2][:, :], part, ALU.add).then_inc(s["added"], 1)
                if c % CPQ == CPQ - 1:
                    q = c // CPQ
                    dve.wait_ge(s["added"], c + 1)
                    center_dve(nc, link, s, q, x, g.rows, mean)
                    if q:
                        sum_squares_dve(nc, dve, s, q - 1, 2 * NQ, sq, g.var)
            sum_squares_dve(nc, dve, s, NQ - 1, 2 * NQ, sq, g.var).then_inc(s["summed"], 1)
            dve.wait_ge(s["summed"], 1)



def layer1_features(nc, g, adj, beta, left_dram):
    with ExitStack() as mem:
        sq = mem.enter_context(nc.sbuf_tensor("f1_sq", [P, NT, D], F32))
        left = mem.enter_context(nc.sbuf_tensor("f1_left", [P, NT, 2, P], F16))
        n, log, inv = (mem.enter_context(nc.sbuf_tensor(f"f1_{k}", [P, NT], F32)) for k in ("n", "log", "inv"))
        half_beta, share, inv_step = (mem.enter_context(nc.sbuf_tensor(f"f1_{k}", [P, 1], F32))
                                      for k in ("half_beta", "share", "inv_step"))
        tp = [mem.enter_context(nc.psum_tensor(f"f1_tp{b}", [P, BANK], F32)) for b in range(4)]
        lp = [mem.enter_context(nc.psum_tensor(f"f1_lp{b}", [P, BANK], F32)) for b in range(4)]
        s = sems(nc, mem, "f1", "beta_in squared var std chain scaled rows norm2 norm clamped log unit "
                                "transposed high low spread spread_out left_out")
        h, var = g.rows, g.var
        block = mem.enter_context(nc.Block())

        @block.sync
        def _(sp):
            sp.dma_start(half_beta[:, :], beta.partition_broadcast(P)).then_inc(s["beta_in"], 16)
            prefetch_tiles(sp, g, adj.rearrange("(k p) j -> k p j", p=P))
            for q in range(NQ):
                sp.wait_ge(s["low"], (q + 1) * (NCH // NQ))
                sp.dma_start(left_dram[:, ts(q, QT), :, :], left[:, ts(q, QT), :, :]).then_inc(s["left_out"], 16)
            sp.wait_ge(s["left_out"], 16 * NQ)

        @block.vector
        def _(dve):
            link = Link(dve, s["chain"])
            scale_dve(nc, dve, link, s, h, var)
            for q in range(NQ):
                last = sum_squares_dve(nc, dve, s, q, 0, sq, n)
            last.then_inc(s["norm2"], 1)
            dve.wait_ge(s["beta_in"], 16)
            link(nc.vector.tensor_scalar(half_beta[:, :], half_beta[:, :], 0.5, None, ALU.mult))
            link(nc.vector.tensor_scalar(share[:, :].bitcast(I32), half_beta[:, :].bitcast(I32), EXPONENT_BITS, None, ALU.bitwise_and))
            link(nc.vector.tensor_scalar(g.step[:, :], share[:, :], 1.0, 1.0 / UNIT ** 2, ALU.max, ALU.mult))
            link(nc.vector.reciprocal(inv_step[:, :], g.step[:, :]))
            link(nc.vector.tensor_scalar(share[:, :], half_beta[:, :], inv_step[:, :], 1.0 / UNIT ** 2, ALU.mult, ALU.mult))
            link(nc.vector.tensor_scalar(g.mask_step[:, :], inv_step[:, :], NEG, None, ALU.mult))
            link(nc.vector.tensor_scalar(g.neg_step[:, :], g.step[:, :], -1.0, None, ALU.mult))
            dve.wait_ge(s["norm"], 1)
            nc.vector.tensor_scalar(n[:, :], n[:, :], TINY_NORM, None, ALU.max).then_inc(s["clamped"], 1)
            dve.wait_ge(s["clamped"], 1)
            link(nc.vector.reciprocal(inv[:, :], n[:, :]))
            link(nc.vector.tensor_scalar(inv[:, :], inv[:, :], UNIT, None, ALU.mult))
            dve.wait_ge(s["rows"], NQ)
            for q in range(NQ):
                t = ts(q, QT)
                nc.vector.tensor_tensor(sq[:, t, :], h[:, t, :], over_rows(inv[:, t], QT), ALU.mult).then_inc(s["unit"], 1)
            for c in range(NCH):
                dve.wait_ge(s["high"], 2 * c + 2)
                nc.vector.tensor_tensor(g.unit_lo[:, ts(c, BANK)], tp[c % 4][:, :], g.unit_hi[:, ts(c, BANK)], ALU.subtract)
                nc.vector.scalar_tensor_tensor(left[:, ts(c, TPB), 1, :], tp[c % 4][:, :].rearrange("p (t c) -> p t c", t=TPB),
                                               share[:, :], left[:, ts(c, TPB), 0, :], ALU.mult, ALU.subtract).then_inc(s["low"], 1)
            dve.wait_ge(s["log"], 1)
            link(nc.vector.tensor_scalar(g.half_log[:, :], log[:, :], -LOG_EPS, 0.5, ALU.add, ALU.mult))

        @block.scalar
        def _(act):
            root_act(nc, act, s, var)
            squares_act(nc, act, s, "rows", h, sq)
            act.wait_ge(s["norm2"], 1)
            nc.scalar.activation(n[:, :], n[:, :], ACT.Sqrt).then_inc(s["norm"], 1)
            act.wait_ge(s["clamped"], 1)
            nc.scalar.activation(log[:, :], n[:, :], ACT.Ln).then_inc(s["log"], 1)
            for c in range(NCH):
                act.wait_ge(s["transposed"], c + 1)
                nc.scalar.copy(g.unit_hi[:, ts(c, BANK)], tp[c % 4][:, :]).then_inc(s["high"], 1)
                nc.scalar.activation(left[:, ts(c, TPB), 0, :], tp[c % 4][:, :].rearrange("p (t c) -> p t c", t=TPB),
                                     ACT.Identity, scale=share[:, :]).then_inc(s["high"], 1)
            transpose_rows_act(nc, act, lambda c: g.log_row[:, ts(c, BANK)], lp, s["spread"], s["spread_out"])

        @block.tensor
        def _(pe):
            transpose_rows_pe(nc, pe, lambda t: sq[:, t, :], tp, g.identity[:, :], s["transposed"], s["low"], s["unit"])
            pe.wait_ge(s["log"], 1)
            for c in range(NCH):
                if c >= len(lp):
                    pe.wait_ge(s["spread_out"], c - len(lp) + 1)
                for r in range(TPB):
                    t = c * TPB + r
                    last = nc.tensor.matmul(lp[c % len(lp)][:, ts(r, P)], log[:, t:t + 1].to_broadcast([P, P]),
                                            g.identity[:, :], start=True, stop=True)
                last.then_inc(s["spread"], 1)


def layer2_features(nc, g, adj, centered_dram, w, a_self, a_neigh):
    with ExitStack() as mem:
        h = mem.enter_context(nc.sbuf_tensor("f2_h", [P, NT, D], F32))
        h_t = mem.enter_context(nc.sbuf_tensor("f2_ht", [P, N], F32))
        w_sb = mem.enter_context(nc.sbuf_tensor("f2_w", [P, D + H2], F32))
        TPP = 2
        pp = [mem.enter_context(nc.psum_tensor(f"f2_pp{b}", [P, TPP, D + H2], F32)) for b in range(4)]
        a_sb = mem.enter_context(nc.sbuf_tensor("f2_a", [P, 2, D], F32))
        wa = mem.enter_context(nc.sbuf_tensor("f2_wa", [P, 2, D], F32))
        w_neigh = mem.enter_context(nc.sbuf_tensor("f2_wn", [P, H2], F32))
        w_neigh_all = mem.enter_context(nc.sbuf_tensor("f2_wna", [P, H2, P], F32))
        tp = [mem.enter_context(nc.psum_tensor(f"f2_tp{b}", [P, BANK], F32)) for b in range(4)]
        s = sems(nc, mem, "f2", X_IN + "w_in var std chain rows weights transposed copied projected "
                                "projected_act projected_dve spread spread_act spread_dve")
        block = mem.enter_context(nc.Block())

        def projected_out(eng, copy, odd, out):
            for c in range(odd, NT // TPP, 2):
                eng.wait_ge(s["projected"], c + 1)
                copy(g.rows[:, ts(c, TPP), :], pp[c % 4][:, :, 0:D])
                copy(g.self_col[:, ts(c, TPP), :], pp[c % 4][:, :, D:D + H2]).then_inc(out, 1)

        def spread_out(eng, copy, odd, out):
            for c in range(odd, H2 * NCH, 2):
                eng.wait_ge(s["spread"], c + 1)
                copy(g.neigh_row[:, c // NCH, ts(c % NCH, BANK)], tp[c % 4][:, :]).then_inc(out, 1)

        @block.sync
        def _(sp):
            load_rows(nc, sp, h, centered_dram, s)
            sp.dma_start(w_sb[:, 0:D].rearrange("p (h d) -> p h d", h=H2), w.rearrange("h f d -> f h d")).then_inc(s["w_in"], 16)
            sp.dma_start(a_sb[:, 0, :], a_self.rearrange("h d -> (h d)").partition_broadcast(P)).then_inc(s["w_in"], 16)
            sp.dma_start(a_sb[:, 1, :], a_neigh.rearrange("h d -> (h d)").partition_broadcast(P)).then_inc(s["w_in"], 16)
            prefetch_tiles(sp, g, adj.rearrange("(k p) j -> k p j", p=P))

        @block.vector
        def _(dve):
            link = Link(dve, s["chain"])
            scale_dve(nc, dve, link, s, h, g.var, X_IN)
            dve.wait_ge(s["w_in"], 48)
            for k, dst in ((0, w_sb[:, D:D + H2]), (1, w_neigh[:, :])):
                link(nc.vector.tensor_tensor(wa[:, k, :], w_sb[:, 0:D], a_sb[:, k, :], ALU.mult))
                link(nc.vector.tensor_reduce(dst, wa[:, k, :].rearrange("p (h d) -> p h d", h=H2), X_AXIS, ALU.add))
            for k in range(H2):
                nc.vector.tensor_scalar(w_neigh_all[:, k, :], g.ones[:, :], w_neigh[:, k:k + 1], None,
                                        ALU.mult).then_inc(s["weights"], 1)
            projected_out(dve, nc.vector.tensor_copy, 1, s["projected_dve"])
            spread_out(dve, nc.vector.tensor_copy, 1, s["spread_dve"])

        @block.scalar
        def _(act):
            root_act(nc, act, s, g.var)
            transpose_rows_act(nc, act, lambda c: h_t[:, ts(c, BANK)], tp, s["transposed"], s["copied"])
            projected_out(act, nc.scalar.copy, 0, s["projected_act"])
            spread_out(act, nc.scalar.copy, 0, s["spread_act"])

        @block.tensor
        def _(pe):
            transpose_rows_pe(nc, pe, lambda t: h[:, t, :], tp, g.identity[:, :], s["transposed"], s["copied"], s["rows"])
            pe.wait_ge(s["weights"], H2)
            for c in range(NT // TPP):
                if c % (TPB // TPP) == 0:
                    pe.wait_ge(s["copied"], c * TPP // TPB + 1)
                if c >= 4:
                    pe.wait_ge((s["projected_act"], s["projected_dve"])[c % 2], (c - 4) // 2 + 1)
                for r in range(TPP):
                    t = c * TPP + r
                    last = nc.tensor.matmul(pp[c % 4][:, r, :], h_t[:, ts(t, P)], w_sb[:, :], start=True, stop=True)
                last.then_inc(s["projected"], 1)
            for c in range(H2 * NCH):
                if c >= 4:
                    pe.wait_ge((s["spread_act"], s["spread_dve"])[c % 2], (c - 4) // 2 + 1)
                nc.tensor.matmul(tp[c % 4][:, :], w_neigh_all[:, c // NCH, :], h_t[:, ts(c % NCH, BANK)],
                                 start=True, stop=True).then_inc(s["spread"], 1)


def masked_attention(nc, g, layer, adj, x_dram, x_next_dram, bias=None, left_dram=None, h_next_dram=None):
    heads = 1 if layer == 1 else H2
    UN = 4
    RT = UN // heads
    NR = NT // RT
    NU = NR * UN
    PW = 2 * P
    TPN = 2 if layer == 1 else 4
    TB = NT // TPB
    EX = 1 if layer == 1 else 2
    SCH = 2 * BANK
    NS = N // SCH
    NORM = 5
    LAG = 7
    with ExitStack() as mem:
        def sb(name, shape):
            return mem.enter_context(nc.sbuf_tensor(f"m{layer}_{name}", shape, F32))

        def psum(name, shape):
            return mem.enter_context(nc.psum_tensor(f"m{layer}_{name}", shape, F32))

        adj_sb, adj_in = g.adj_sb, g.adj_in
        part = sb("part", [P, N])
        score = [sb(f"score{b}", [P, N]) for b in range(2)]
        probs = [sb(f"probs{b}", [P, NT, PW]) for b in range(2)]
        out_t = sb("out_t", [P, RT * P])
        xg = sb("x", [P, 2, RT, D])
        neg_top, total = sb("neg_top", [P, UN]), sb("total", [P, EX, UN])
        inv = sb("inv", [P, 2, UN])
        spare = sb("spare", [P, 1])
        tp = [psum(f"tp{b}", [P, TPB, P]) for b in range(TPN)]
        ps_out = psum("ps_out", [P, BANK])
        ps_rows = psum("ps_rows", [P, BANK])
        if layer == 1:
            left = [mem.enter_context(nc.sbuf_tensor(f"m1_left{b}", [P, 2, P], F16)) for b in range(2)]
            top_step = sb("top_step", [P, UN])
            centered = sb("centered", [P, 2, RT, D])
            squares, mean, spare_norm = sb("squares", [P, RT, D]), sb("mean", [P, RT]), sb("spare_norm", [P, 2])
            left_in = [mem.enter_context(nc.semaphore(f"m1_left_in{b}")) for b in range(2)]
            ps_s = [psum(f"ps_s{b}", [P, SCH]) for b in range(2)]
        else:
            sums = sb("sums", [P, UN])
            val, low, bias_sb = sb("val", [P, RT, D]), sb("low", [P, RT, D]), sb("bias", [P, D])
        s = sems(nc, mem, f"m{layer}", "gated masks masked exped transposed copied summed out_copied rows inv "
                 "rows_read x_in x_ready x_out " + ("products part_ready topped normed centered_out" if layer == 1 else "bias_in valued lowered elu_exp summed_up"))
        block = mem.enter_context(nc.Block())
        adj_v = adj.rearrange("(k p) j -> k p j", p=P)

        def out_part(tensor, pair):
            if layer == 1:
                return tensor[:, ts(pair, PW)]
            return tensor[ts(pair, DH2), 0:PW]

        def of_round(tensor, r):
            return tensor[:, r % 2, :, :] if isinstance(r, int) else \
                tensor[:, bass.ds(r % 2, 1), :, :].rearrange("p o t d -> p (o t) d")

        def x_rows(r):
            return of_round(xg, r)

        def live(k, below):
            return not isinstance(k, int) or 0 <= k < below

        def rounds(eng, slot):
            for k in range(2 * UN):
                slot(k, k // UN, k % UN)
            with eng.Fori(2, NR - 1) as r:
                for u in range(UN):
                    slot(r * UN + u, r, u)
            for k in range(NU - UN, NU + LAG + 1):
                slot(k, k // UN, k % UN)

        def row_tile(dram, k, n=1):
            tiles = row_tiles(dram)
            return tiles[:, k:k + n, :] if isinstance(k, int) else tiles[:, bass.ds(k, n), :]

        @block.sync
        def _(sp):
            def load(k, slot):
                src = adj_v[k] if isinstance(k, int) else adj_v[bass.ds(k, 1)].rearrange("o p j -> (o p) j")
                sp.dma_start(adj_sb[slot][:, :], src).then_inc(adj_in[slot], 16)

            if layer == 2:
                sp.dma_start(bias_sb[:, :], bias.partition_broadcast(P)).then_inc(s["bias_in"], 16)
            def load_left(k, b):
                src = left_dram[:, k, :, :] if isinstance(k, int) else \
                    left_dram[:, bass.ds(k, 1), :, :].rearrange("p o v c -> p (o v) c")
                sp.dma_start(left[b][:, :, :], src).then_inc(left_in[b], 16)

            if layer == 1:
                load_left(0, 0)
                load_left(1, 1)
            with sp.Fori(1, NT // 2) as m:
                for b in range(2):
                    if layer == 1:
                        sp.wait_ge(s["products"], (m * 2 + b - 1) * NS)
                        load_left(m * 2 + b, b)
                    sp.wait_ge(s["masked"], m * 2 + b - 1 if layer == 1 else m * UN + b - 1)
                    load(m * 2 + b, b)

        @block.gpsimd
        def _(pool):
            def load(r):
                pool.dma_start(x_rows(r), row_tile(x_dram, RT * r, RT)).then_inc(s["x_in"], 16)

            def store(r):
                pool.wait_ge(s["x_ready"], r + 2)
                pool.dma_start(row_tile(x_next_dram, RT * r, RT), x_rows(r)).then_inc(s["x_out"], 16)
                if layer == 1:
                    pool.wait_ge(s["normed"], r * NORM + 4)
                    pool.dma_start(row_tile(h_next_dram, RT * r, RT), of_round(centered, r)).then_inc(s["centered_out"], 16)

            load(0)
            pool.wait_ge(s["x_in"], 16)
            load(1)
            with pool.Fori(0, NR - 2) as r:
                store(r)
                pool.wait_ge(s["x_out"], (r + 1) * 16)
                if layer == 1:
                    pool.wait_ge(s["centered_out"], (r + 1) * 16)
                pool.wait_ge(s["x_in"], (r + 2) * 16)
                load(r + 2)
            store(NR - 2)
            store(NR - 1)
            pool.wait_ge(s["x_out"], NR * 16)
            if layer == 1:
                pool.wait_ge(s["centered_out"], NR * 16)

        @block.tensor
        def _(pe):
            def products(k, r, u, c):
                if not live(k, NU):
                    return
                if c == 0:
                    pe.wait_ge(left_in[u % 2], (k // 2 + 1) * 16 if isinstance(k, int) else (r * 2 + u // 2 + 1) * 16)
                if not (isinstance(k, int) and k == 0 and c < 2):
                    pe.wait_ge(s["gated"], k * NS + c - 1)
                hi, lo = left[u % 2][:, 0, :], left[u % 2][:, 1, :]
                for part, (lhs, rhs) in enumerate(((hi, g.unit_hi), (hi, g.unit_lo), (lo, g.unit_hi))):
                    for q in range(2):
                        last = nc.tensor.matmul(ps_s[c % 2][:, ts(q, BANK)], lhs, rhs[:, ts(2 * c + q, BANK)],
                                                start=(part == 0), stop=(part == 2))
                last.then_inc(s["products"], 1)

            def transposes(k, u, b):
                if not live(k, NU):
                    return
                if b * EX % TB == 0:
                    pe.wait_ge(s["exped"], k * EX + b * EX // TB + 1)
                if not (isinstance(k, int) and k == 0 and b < TPN):
                    pe.wait_ge(s["copied"], k * TB + b - TPN + 1)
                for r in range(TPB):
                    last = nc.tensor.transpose(tp[b % TPN][:, r, :], score[u % 2][:, ts(b * TPB + r, P)], g.identity[:, :])
                last.then_inc(s["transposed"], 1)

            def values(k, r, u, first, n):
                half = (u + 1) % 2
                last_unit = k - 2 - half
                pair = (u - 2 - half) // 2 % 2
                if not live(last_unit, NU):
                    return
                if half == 0 and first == 0:
                    pe.wait_ge(s["copied"], (last_unit + 1) * TB)
                    back = 1 if layer == 1 else 2
                    if live(last_unit - 2 * back, NU):
                        pe.wait_ge(s["out_copied"], 2 * r + (u == 3) - back)
                for jt in range(half * NT // 2 + first, half * NT // 2 + first + n):
                    cols = slice(0, D) if layer == 1 else ts(pair, DH2)
                    mm = nc.tensor.matmul(out_part(ps_out, pair), g.rows[:, jt, cols], probs[pair][:, jt, :],
                                          start=(jt == 0), stop=(jt == NT - 1))
                if half == 1 and first + n == NT // 2:
                    mm.then_inc(s["summed"], 1)

            def rows_back(r):
                if not live(r, NR):
                    return
                pe.wait_ge(s["out_copied"], 2 * r + 2)
                pe.wait_ge(s["rows_read"], r + 1)
                for t in range(RT):
                    last = nc.tensor.transpose(ps_rows[:, ts(t, P)], out_t[:, ts(t, P)], g.identity[:, :])
                last.then_inc(s["rows"], 1)

            def slot(k, r, u):
                if u == 0:
                    rows_back(r - 2)
                if layer == 1:
                    products(k, r, u, 2)
                    products(k, r, u, 3)
                    values(k, r, u, 0, 8)
                    for b in range(TB // 2):
                        transposes(k - 1, (u - 1) % UN, b)
                    products(k + 1, r, u + 1, 0)
                    products(k + 1, r, u + 1, 1)
                    values(k, r, u, 8, 8)
                    for b in range(TB // 2, TB):
                        transposes(k - 1, (u - 1) % UN, b)
                else:
                    values(k, r, u, 0, 10)
                    for b in range(TB // 2):
                        transposes(k - 1, (u - 1) % UN, b)
                    values(k, r, u, 10, 6)
                    for b in range(TB // 2, TB):
                        transposes(k - 1, (u - 1) % UN, b)

            if layer == 1:
                products(0, 0, 0, 0)
                products(0, 0, 0, 1)
            rounds(pe, slot)

        @block.scalar
        def _(act):
            def gate(k):
                if not live(k, NU):
                    return
                row = slice(k, k + 1) if isinstance(k, int) else bass.ds(k, 1)
                if not (isinstance(k, int) and k == 0):
                    act.wait_ge(s["masked"], k)
                nc.scalar.activation(part[:, :], g.log_row[:, :], ACT.Tanh, scale=0.5,
                                     bias=g.half_log[:, row]).then_inc(s["part_ready"], 1)

            def softmax(k, u, r):
                if not live(k, NU):
                    return
                act.wait_ge(s["topped" if layer == 1 else "masked"], k + 1)
                if u == 0 and not (isinstance(r, int) and r == 0):
                    act.wait_ge(s["inv"], r)
                for x in range(EX):
                    cols = score[u % 2][:, ts(x, N // EX)]
                    nc.scalar.activation(cols, cols, ACT.Exp, scale=g.neg_step[:, :] if layer == 1 else -1.0,
                                         bias=(top_step if layer == 1 else neg_top)[:, u:u + 1], accum_out=total[:, x, u:u + 1]).then_inc(s["exped"], 1)

            def copies(k, r, u, first, n):
                if not live(k, NU):
                    return
                if u % 2 == 0 and first == 0 and live(k - UN, NU):
                    act.wait_ge(s["summed"], 2 * r + u // 2 - 1)
                for b in range(first, first + n):
                    act.wait_ge(s["transposed"], k * TB + b + 1)
                    nc.scalar.copy(probs[u // 2][:, ts(b, TPB), ts(u % 2, P)], tp[b % TPN][:, :, :]).then_inc(s["copied"], 1)

            def take_out(k, r, u):
                last_unit = k - 4
                if u % 2 == 0 or not live(last_unit, NU):
                    return
                pair, of_round = u // 2, r - 1
                count = of_round * 2 + pair + 1
                act.wait_ge(s["summed"], count)
                if pair == 0 and not (isinstance(of_round, int) and of_round == 0):
                    act.wait_ge(s["rows"], of_round)
                nc.scalar.copy(out_part(out_t, pair), out_part(ps_out, pair)).then_inc(s["out_copied"], 1)

            def elu_exp(r):
                if live(r, NR):
                    act.wait_ge(s["lowered"], r + 1)
                    nc.scalar.activation(low[:, :, :], low[:, :, :], ACT.Exp).then_inc(s["elu_exp"], 1)

            def slot(k, r, u):
                take_out(k, r, u)
                if layer == 2 and u == 3:
                    elu_exp(r - 2)
                softmax(k - 1, (u - 1) % UN, r if u else r - 1)
                copies(k - 1, r if u else r - 1, (u - 1) % UN, 0, TB // 2)
                if layer == 1:
                    gate(k + 1)
                copies(k - 1, r if u else r - 1, (u - 1) % UN, TB // 2, TB // 2)

            if layer == 1:
                gate(0)
            rounds(act, slot)

        @block.vector
        def _(dve):
            def inverse(r, cols):
                both = inv[:, :, cols]
                return both[:, r % 2, :] if isinstance(r, int) else both[:, bass.ds(r % 2, 1), :].rearrange("p o u -> p (o u)")

            def invert(r):
                if live(r, NR):
                    dve.wait_ge(s["exped"], (r + 1) * UN * EX)
                    if EX == 2:
                        nc.vector.tensor_tensor(sums[:, :], total[:, 0, :], total[:, 1, :],
                                                ALU.add).then_inc(s["summed_up"], 1)
                        dve.wait_ge(s["summed_up"], r + 1)
                        nc.vector.reciprocal(inverse(r, slice(0, UN)), sums[:, :]).then_inc(s["inv"], 1)
                    else:
                        nc.vector.reciprocal(inverse(r, slice(0, UN)), total[:, 0, :]).then_inc(s["inv"], 1)

            def finish(r):
                if not live(r, NR):
                    return
                dve.wait_ge(s["x_in"], (r + 1) * 16)
                dve.wait_ge(s["x_ready"], r + 1)
                dve.wait_ge(s["inv"], r + 1)
                dve.wait_ge(s["rows"], r + 1)
                for t in range(RT):
                    for h in range(heads):
                        cols = slice(h * D // heads, (h + 1) * D // heads)
                        u = h * RT + t
                        rows = ps_rows[:, t * P + cols.start:t * P + cols.stop]
                        if layer == 1:
                            x_tile = xg[:, r % 2, t, cols] if isinstance(r, int) else \
                                xg[:, bass.ds(r % 2, 1), t, cols].rearrange("p o d -> p (o d)")
                            last = nc.vector.scalar_tensor_tensor(x_tile, rows, inverse(r, slice(u, u + 1)), x_tile,
                                                                  ALU.mult, ALU.add)
                        else:
                            last = nc.vector.scalar_tensor_tensor(val[:, t, cols], rows, inverse(r, slice(u, u + 1)), bias_sb[:, cols],
                                                                  ALU.mult, ALU.add)
                last.then_inc(s["rows_read"], 1)
                dve.wait_ge(s["rows_read"], r + 2)
                if layer == 1:
                    nc.vector.memset(spare[:, :], 0.0).then_inc(s["x_ready"], 1)
                else:
                    nc.vector.tensor_scalar(low[:, :, :], val[:, :, :], 0.0, None, ALU.min).then_inc(s["lowered"], 1)

            def finish_elu(r):
                if not live(r, NR):
                    return
                dve.wait_ge(s["elu_exp"], r + 1)
                nc.vector.scalar_tensor_tensor(val[:, :, :], val[:, :, :], 0.0, low[:, :, :],
                                               ALU.max, ALU.add).then_inc(s["valued"], 1)
                dve.wait_ge(s["valued"], r + 1)
                nc.vector.scalar_tensor_tensor(x_rows(r), val[:, :, :], -1.0, x_rows(r),
                                               ALU.add, ALU.add).then_inc(s["x_ready"], 1)

            def scores(k, r, u):
                if not live(k, NU):
                    return
                mask = adj_sb[u % 2]
                if layer == 1 or u < 2:
                    dve.wait_ge(adj_in[u % 2], (r * 2 + u // 2 + 1) * 16 if layer == 1 else (r + 1) * 16)
                    nc.vector.tensor_scalar(mask[:, :], mask[:, :], 1.0, g.mask_step[:, :] if layer == 1 else NEG,
                                            ALU.subtract, ALU.mult).then_inc(s["masks"], 1)
                if layer == 1:
                    dve.wait_ge(s["part_ready"], k + 1)
                    for c in range(NS):
                        dve.wait_ge(s["products"], k * NS + c + 1)
                        nc.vector.scalar_tensor_tensor(part[:, ts(c, SCH)], part[:, ts(c, SCH)], 1.0, ps_s[c % 2][:, :],
                                                       ALU.add, ALU.mult).then_inc(s["gated"], 1)
                    dve.wait_ge(s["gated"], (k + 1) * NS)
                    dve.wait_ge(s["masks"], k + 1)
                else:
                    h, col = u // 2, RT * r + u % 2
                    this = slice(col, col + 1) if isinstance(col, int) else bass.ds(col, 1)
                    if not (isinstance(k, int) and k == 0):
                        dve.wait_ge(s["masked"], k)
                    nc.vector.tensor_scalar(part[:, :], g.neigh_row[:, h, :],
                                            g.self_col[:, this, h], None, ALU.add).then_inc(s["gated"], 1)
                    dve.wait_ge(s["gated"], k + 1)
                    dve.wait_ge(s["masks"], RT * r + u % 2 + 1)
                if not (isinstance(k, int) and k < 2):
                    dve.wait_ge(s["transposed"], (k - 1) * TB)
                nc.vector.memset(spare[:, :], 0.0)
                nc.vector.tensor_tensor_reduce(out=score[u % 2][:, :], in0=part[:, :], in1=mask[:, :], scale=-1.0,
                                               scalar=HIGHEST, op0=ALU.add, op1=ALU.min,
                                               accum_out=neg_top[:, u:u + 1]).then_inc(s["masked"], 1)
                if layer == 1:
                    dve.wait_ge(s["masked"], k + 1)
                    nc.vector.tensor_scalar(top_step[:, u:u + 1], neg_top[:, u:u + 1], g.step[:, :], None,
                                            ALU.mult).then_inc(s["topped"], 1)

            def norm(r):
                if not live(r, NR):
                    return
                dve.wait_ge(s["x_ready"], r + 2)
                dve.wait_ge(s["normed"], r * NORM + 1)
                nc.vector.memset(spare_norm[:, 0:1], 0.0)
                nc.vector.tensor_reduce(mean[:, :], x_rows(r), X_AXIS, ALU.add).then_inc(s["normed"], 1)
                dve.wait_ge(s["normed"], r * NORM + 2)
                nc.vector.tensor_scalar(mean[:, :], mean[:, :], 1.0 / D, None, ALU.mult).then_inc(s["normed"], 1)
                dve.wait_ge(s["normed"], r * NORM + 3)
                nc.vector.tensor_tensor(of_round(centered, r), x_rows(r), over_rows(mean[:, :], RT),
                                        ALU.subtract).then_inc(s["normed"], 1)
                dve.wait_ge(s["normed"], r * NORM + 4)
                nc.vector.tensor_tensor(squares[:, :, :], of_round(centered, r), of_round(centered, r),
                                        ALU.mult).then_inc(s["normed"], 1)
                dve.wait_ge(s["normed"], r * NORM + 5)
                nc.vector.memset(spare_norm[:, 1:2], 0.0)
                tiles = slice(RT * r, RT * r + RT) if isinstance(r, int) else bass.ds(r * RT, RT)
                nc.vector.tensor_reduce(g.var[:, tiles], squares[:, :, :], X_AXIS, ALU.add).then_inc(s["normed"], 1)

            def slot(k, r, u):
                if u == 1:
                    invert(r - 1)
                scores(k, r, u)
                if u == 2:
                    finish(r - 2)
                if layer == 2 and u == 3:
                    finish_elu(r - 2)
                if layer == 1 and u == 3:
                    norm(r - 2)

            if layer == 2:
                dve.wait_ge(s["bias_in"], 16)
            dve.sem_inc(s["rows_read"], 1)
            dve.sem_inc(s["x_ready"], 1)
            if layer == 1:
                dve.sem_inc(s["normed"], 1)
            rounds(dve, slot)



def layer3_features(nc, g, adj_t, x_dram, w, a_src, a_tgt, proj_dram, src_dram):
    BUFS = 6
    with ExitStack() as mem:
        x = mem.enter_context(nc.sbuf_tensor("f3_x", [P, NT, D], F32))
        sq = mem.enter_context(nc.sbuf_tensor("f3_sq", [P, NT, D], F32))
        h = mem.enter_context(nc.sbuf_tensor("f3_h", [P, NT, D], F32))
        mean, var = (mem.enter_context(nc.sbuf_tensor(f"f3_{k}", [P, NT], F32)) for k in ("mean", "var"))
        w_sb = mem.enter_context(nc.sbuf_tensor("f3_w", [P, H3, D], F32))
        a_sb = mem.enter_context(nc.sbuf_tensor("f3_a", [P, 2, H3, D], F32))
        wa = mem.enter_context(nc.sbuf_tensor("f3_wa", [P, 2, H3, D], F32))
        w_a = mem.enter_context(nc.sbuf_tensor("f3_w_a", [P, 2, H3], F32))
        proj = [mem.enter_context(nc.sbuf_tensor(f"f3_proj{b}", [P, H3 * D], F32)) for b in range(BUFS)]
        src_cols = mem.enter_context(nc.sbuf_tensor("f3_src_cols", [P, H3, NT], F32))
        src = mem.enter_context(nc.sbuf_tensor("f3_src", [H3 * NT, P], F32))
        tp = [mem.enter_context(nc.psum_tensor(f"f3_tp{b}", [P, BANK], F32)) for b in range(4)]
        ps_score = mem.enter_context(nc.psum_tensor("f3_ps_score", [P, NT, 2, H3], F32))
        ps_src = mem.enter_context(nc.psum_tensor("f3_ps_src", [H3 * NT, P], F32))
        s = sems(nc, mem, "f3", X_IN + "w_in centered squared var std chain rows weights transposed copied scored "
                                "src_cols src_rows src_copied projected out_act out_dve src_stored")
        stored = [mem.enter_context(nc.semaphore(f"f3_stored{b}")) for b in range(BUFS)]

        def projections_out(eng, copy, odd, out):
            for t in range(odd, NT, 2):
                eng.wait_ge(s["projected"], t + 1)
                if t >= BUFS:
                    eng.wait_ge(stored[t % BUFS], 16 * (t // BUFS))
                copy(proj[t % BUFS][:, :], tp[t % 4][:, :]).then_inc(out, 1)

        block = mem.enter_context(nc.Block())

        @block.sync
        def _(sp):
            load_rows(nc, sp, x, x_dram, s)
            sp.dma_start(w_sb[:, :, :], w.rearrange("h f o -> f h o")).then_inc(s["w_in"], 16)
            for k, a in ((0, a_src), (1, a_tgt)):
                sp.dma_start(a_sb[:, k, :, :].rearrange("p h o -> p (h o)"),
                             a.rearrange("h o -> (h o)").partition_broadcast(P)).then_inc(s["w_in"], 16)
            prefetch_tiles(sp, g, adj_t.rearrange("(k p) i -> k p i", p=P))
            sp.wait_ge(s["src_copied"], 1)
            sp.dma_start(src_dram.rearrange("h (t p) -> (h t) p", p=P), src[:, :]).then_inc(s["src_stored"], 16)
            for t in range(NT):
                sp.wait_ge((s["out_act"], s["out_dve"])[t % 2], t // 2 + 1)
                sp.dma_start(proj_dram[ts(t, P), :], proj[t % BUFS][:, :]).then_inc(stored[t % BUFS], 16)
                if t == BUFS - 1:
                    sp.wait_ge(s["src_stored"], 16)
                    sp.dma_start(g.src[:, 0, :], src_dram[0, :].partition_broadcast(P)).then_inc(g.src0_in, 16)
            for b in range(BUFS):
                sp.wait_ge(stored[b], 16 * len(range(b, NT, BUFS)))

        @block.vector
        def _(dve):
            link = Link(dve, s["chain"])
            layer_norm_dve(nc, dve, link, s, x, h, sq, mean, var)
            dve.wait_ge(s["w_in"], 48)
            for k in range(2):
                link(nc.vector.tensor_tensor(wa[:, k, :, :], w_sb[:, :, :], a_sb[:, k, :, :], ALU.mult))
                nc.vector.tensor_reduce(w_a[:, k, :], wa[:, k, :, :], X_AXIS, ALU.add).then_inc(s["weights"], 1)
            dve.wait_ge(s["scored"], 1)
            nc.vector.tensor_copy(src_cols[:, :, :], ps_score[:, :, 0, :].rearrange("p t h -> p h t")).then_inc(s["src_cols"], 1)
            targets = ps_score[:, :, 1, :].rearrange("p t h -> p h t")
            nc.vector.tensor_copy(g.tgt[:, :, :], targets)
            nc.vector.tensor_scalar(g.tgt_sloped[:, :, :], targets, SLOPE, None, ALU.mult)
            dve.wait_ge(s["src_rows"], 1)
            nc.vector.tensor_copy(src[:, :], ps_src[:, :]).then_inc(s["src_copied"], 1)
            projections_out(dve, nc.vector.tensor_copy, 1, s["out_dve"])

        @block.scalar
        def _(act):
            layer_norm_act(nc, act, s, h, sq, var)
            transpose_rows_act(nc, act, lambda c: g.h_t[:, ts(c, BANK)], tp, s["transposed"], s["copied"])
            projections_out(act, nc.scalar.copy, 0, s["out_act"])

        @block.tensor
        def _(pe):
            transpose_rows_pe(nc, pe, lambda t: h[:, t, :], tp, g.identity[:, :], s["transposed"], s["copied"], s["rows"])
            pe.wait_ge(s["weights"], 2)
            pe.wait_ge(s["copied"], NCH)
            for t in range(NT):
                last = nc.tensor.matmul(ps_score[:, t, :, :].rearrange("p k h -> p (k h)"), g.h_t[:, ts(t, P)],
                                        w_a[:, :, :].rearrange("p k h -> p (k h)"), start=True, stop=True)
            last.then_inc(s["scored"], 1)
            pe.wait_ge(s["src_cols"], 1)
            nc.tensor.transpose(ps_src[:, :], src_cols[:, :, :].rearrange("p h t -> p (h t)"), g.identity[:, :]).then_inc(s["src_rows"], 1)
            for t in range(NT):
                if t >= 4:
                    pe.wait_ge((s["out_act"], s["out_dve"])[t % 2], (t - 4) // 2 + 1)
                nc.tensor.matmul(tp[t % 4][:, :], g.h_t[:, ts(t, P)], w_sb[:, :, :].rearrange("p h o -> p (h o)"),
                                 start=True, stop=True).then_inc(s["projected"], 1)


def layer3_attention(nc, g, adj_t, proj_dram, src_dram, x_dram, out):
    UN = 4
    NG = NT // UN
    PIECE = N // (NT // 2)
    SRC_IN = 16 * NT // 2
    with ExitStack() as mem:
        src = g.src
        adj_sb, adj_in = g.adj_sb, g.adj_in
        e = [mem.enter_context(nc.sbuf_tensor(f"e_e{b}", [P, N], F32)) for b in range(UN)]
        v = mem.enter_context(nc.sbuf_tensor("e_v", [P, 2, UN, D], F32))
        scaled = [mem.enter_context(nc.sbuf_tensor(f"e_scaled{b}", [P, D], F32)) for b in range(UN)]
        x = mem.enter_context(nc.sbuf_tensor("e_x", [P, NT, D], F32))
        low = mem.enter_context(nc.sbuf_tensor("e_low", [P, N], F32))
        acc = mem.enter_context(nc.sbuf_tensor("e_acc", [P, N], F32))
        neg_top, total, inv = (mem.enter_context(nc.sbuf_tensor(f"e_{k}", [P, UN], F32))
                                    for k in ("neg_top", "total", "inv"))
        spare = mem.enter_context(nc.sbuf_tensor("e_spare", [P, 1], F32))
        ps = mem.enter_context(nc.psum_tensor("e_ps", [P, NCH, BANK], F32))
        s = sems(nc, mem, "e", "src_in v_in sloped leaky masked exped inv scaled multiplied taken lowered elu_exp "
                               "acc_ready x_in turned x_ready x_out")
        block = mem.enter_context(nc.Block())
        adj_v = adj_t.rearrange("(k p) i -> k p i", p=P)
        proj_v = proj_dram.rearrange("(q t p) (h o) -> h q p t o", t=UN, p=P, h=H3)

        def heads_and_groups(eng, head):
            head(0, True)
            with eng.Fori(1, H3) as h:
                head(h, False)

        @block.sync
        def _(sp):
            def load(k, slot):
                src_ap = adj_v[k] if isinstance(k, int) else adj_v[bass.ds(k, 1)].rearrange("o p i -> (o p) i")
                sp.dma_start(adj_sb[slot][:, :], src_ap).then_inc(adj_in[slot], 16)

            def src_piece(h, m):
                row = src_dram[h] if isinstance(h, int) else src_dram[bass.ds(h, 1), :].rearrange("o n -> (o n)")
                slot = h % 2
                to = src[:, slot, :] if isinstance(h, int) else src[:, bass.ds(slot, 1), :].rearrange("p o n -> p (o n)")
                cols = slice(m * PIECE, (m + 1) * PIECE) if isinstance(m, int) else bass.ds(m * PIECE, PIECE)
                sp.dma_start(to[:, cols], row[cols].partition_broadcast(P)).then_inc(s["src_in"], 16)

            src_piece(1, 0)
            with sp.Fori(1, NT // 2) as m:
                for b in range(2):
                    sp.wait_ge(s["masked"], m * 2 + b - 1)
                    load(m * 2 + b, b)
                src_piece(1, m)

            def head(h, last):
                with sp.Fori(0, NT // 2) as m:
                    for b in range(2):
                        sp.wait_ge(s["masked"], h * NT + m * 2 + b - 1)
                        load(m * 2 + b, b)
                    if not last:
                        sp.wait_ge(s["leaky"], h * NT + 1)
                        src_piece(h + 1, m)

            with sp.Fori(1, H3 - 1) as h:
                head(h, False)
            head(H3 - 1, True)
            for c in range(NCH):
                sp.wait_ge(s["x_ready"], c + 1)
                sp.dma_start(row_tiles(out)[:, ts(c, TPB), :], x[:, ts(c, TPB), :]).then_inc(s["x_out"], 16)
            sp.wait_ge(s["x_out"], 16 * NCH)

        @block.gpsimd
        def _(pool):
            def load(h, q, slot):
                rows = proj_v[h, q] if isinstance(h, int) and isinstance(q, int) else \
                    proj_v[(slice(h, h + 1) if isinstance(h, int) else bass.ds(h, 1)),
                           (slice(q, q + 1) if isinstance(q, int) else bass.ds(q, 1))].rearrange("a b p t o -> (a b p) t o")
                pool.dma_start(v[:, slot, :, :], rows).then_inc(s["v_in"], 16)

            load(0, 0, 0)
            pool.wait_ge(s["v_in"], 16)
            load(0, 1, 1)
            def group(h, q):
                g_at = h * NG + q
                pool.wait_ge(s["scaled"], g_at * UN - UN)
                pool.wait_ge(s["v_in"], g_at * 16)
                rows = proj_v[(slice(h, h + 1) if isinstance(h, int) else bass.ds(h, 1)),
                              bass.ds(q, 1)].rearrange("a b p t o -> (a b p) t o")
                pool.dma_start(v[:, bass.ds(q % 2, 1), :, :].rearrange("p a t o -> p (a t) o"), rows).then_inc(s["v_in"], 16)

            with pool.Fori(2, NG) as q:
                group(0, q)
            pool.dma_start(x[:, :, :], row_tiles(x_dram)).then_inc(s["x_in"], 16)
            with pool.Fori(1, H3) as h:
                with pool.Fori(0, NG) as q:
                    group(h, q)

        @block.tensor
        def _(pe):
            def group(h, q, first_head, first_group):
                for u in range(UN):
                    k = h * NT + q * UN + u
                    begin = first_group and u == 0
                    pe.wait_ge(s["scaled"], k + 1)
                    for c in range(NCH):
                        if begin and not first_head:
                            pe.wait_ge(s["taken"], (h - 1) * NCH + c + 1)
                        if first_group:
                            mm = nc.tensor.matmul(ps[:, c, :], scaled[u][:, :], e[u][:, ts(c, BANK)],
                                                  start=begin, stop=False, skip_group_check=True)
                        else:
                            mm = nc.tensor.matmul(ps[:, c, :], scaled[u][:, :], e[u][:, ts(c, BANK)],
                                                  start=False, stop=(u == UN - 1), skip_group_check=True)
                    mm.then_inc(s["multiplied"], 1)
                    if first_group and u in (1, 2):
                        for c in range((u - 1) * NCH // 2, u * NCH // 2):
                            nc.tensor.matmul(ps[:, c, :], g.identity[:, :], g.h_t[:, ts(c, BANK)],
                                             start=False, stop=False, skip_group_check=True)

            def head(h, first):
                group(h, 0, first, True)
                with pe.Fori(1, NG) as q:
                    group(h, q, first, False)

            heads_and_groups(pe, head)
            for c in range(NCH):
                pe.wait_ge(s["taken"], (H3 - 1) * NCH + c + 1)
                pe.wait_ge(s["acc_ready"], H3 + c + 1)
                for r in range(TPB):
                    last = nc.tensor.transpose(ps[:, c, ts(r, P)], acc[:, ts(c * TPB + r, P)], g.identity[:, :])
                last.then_inc(s["turned"], 1)

        @block.scalar
        def _(act):
            def scale(h, q, k, u):
                act.wait_ge(s["v_in"], (h * NG + q + 1) * 16)
                act.wait_ge(s["inv"], k + 1)
                rows = v[:, q % 2, u, :] if isinstance(q, int) else \
                    v[:, bass.ds(q % 2, 1), u, :].rearrange("p o d -> p (o d)")
                nc.scalar.activation(scaled[u][:, :], rows, ACT.Identity, scale=inv[:, u:u + 1]).then_inc(s["scaled"], 1)

            def softmax(k, u):
                act.wait_ge(s["masked"], k + 1)
                nc.scalar.activation(e[u][:, :], e[u][:, :], ACT.Exp, scale=-1.0, bias=neg_top[:, u:u + 1],
                                     accum_out=total[:, u:u + 1]).then_inc(s["exped"], 1)

            def group(h, q, first_head, first_group):
                for u in range(UN):
                    k = h * NT + q * UN + u
                    start = first_head and first_group
                    if first_group and u == 0:
                        if first_head:
                            act.wait_ge(g.src0_in, 16)
                        else:
                            act.wait_ge(s["src_in"], h * SRC_IN)
                    if not start:
                        act.wait_ge(s["multiplied"], k - UN + 1)
                    col = g.tgt_sloped[:, :, :].rearrange("p h t -> p (h t)")
                    col = col[:, k:k + 1] if start else col[:, bass.ds(k, 1)]
                    row = src[:, 0, :] if first_head else src[:, bass.ds(h % 2, 1), :].rearrange("p o n -> p (o n)")
                    nc.scalar.activation(e[u][:, :], row, ACT.Identity, scale=SLOPE, bias=col).then_inc(s["sloped"], 1)
                    if u >= 2:
                        scale(h, q, k - 2, u - 2)
                    elif not start:
                        if first_group:
                            scale(h - 1, NG - 1, k - 2, u + 2)
                        else:
                            scale(h, q - 1, k - 2, u + 2)
                    if not (start and u == 0):
                        softmax(k - 1, (u - 1) % UN)
                    if first_group and u == 1 and not first_head:
                        act.wait_ge(s["acc_ready"], h)
                        act.wait_ge(s["multiplied"], h * NT)
                        for c in range(NCH):
                            lower(c)
                    if first_group and u == UN - 1 and not first_head:
                        act.wait_ge(s["lowered"], h * NCH)
                        nc.scalar.activation(low[:, :], low[:, :], ACT.Exp, scale=-1.0).then_inc(s["elu_exp"], 1)

            def lower(c):
                nc.scalar.activation(low[:, ts(c, BANK)], ps[:, c, :], ACT.Relu, scale=-1.0).then_inc(s["lowered"], 1)

            def head(h, first):
                group(h, 0, first, True)
                with act.Fori(1, NG) as q:
                    group(h, q, first, False)

            heads_and_groups(act, head)
            scale(H3 - 1, NG - 1, H3 * NT - 2, UN - 2)
            softmax(H3 * NT - 1, UN - 1)
            scale(H3 - 1, NG - 1, H3 * NT - 1, UN - 1)
            act.wait_ge(s["acc_ready"], H3)
            act.wait_ge(s["multiplied"], H3 * NT)
            for c in range(NCH + 1):
                if c < NCH:
                    lower(c)
                if c:
                    act.wait_ge(s["lowered"], (H3 - 1) * NCH + c)
                    part = low[:, ts(c - 1, BANK)]
                    nc.scalar.activation(part, part, ACT.Exp, scale=-1.0).then_inc(s["elu_exp"], 1)

        @block.vector
        def _(dve):
            def invert(k, u):
                dve.wait_ge(s["exped"], k + 1)
                nc.vector.reciprocal(inv[:, u:u + 1], total[:, u:u + 1]).then_inc(s["inv"], 1)

            def take(h, c):
                dve.wait_ge(s["lowered"], h * NCH + c + 1)
                part = acc[:, ts(c, BANK)]
                nc.vector.scalar_tensor_tensor(part, ps[:, c, :], 0.0, part, ALU.max, ALU.add).then_inc(s["taken"], 1)

            def group(h, q, first_head, first_group):
                for u in range(UN):
                    k = h * NT + q * UN + u
                    dve.wait_ge(adj_in[u % 2], (k // 2 + 1) * 16 if isinstance(k, int) else
                                (h * (NT // 2) + q * (UN // 2) + u // 2 + 1) * 16)
                    dve.wait_ge(s["sloped"], k + 1)
                    start = first_head and first_group
                    col = g.tgt[:, :, :].rearrange("p h t -> p (h t)")
                    col = col[:, k:k + 1] if start else col[:, bass.ds(k, 1)]
                    row = src[:, 0, :] if first_head else src[:, bass.ds(h % 2, 1), :].rearrange("p o n -> p (o n)")
                    nc.vector.scalar_tensor_tensor(e[u][:, :], row, col, e[u][:, :], ALU.add, ALU.max).then_inc(s["leaky"], 1)
                    dve.wait_ge(s["leaky"], k + 1)
                    if first_head and first_group and u == 0:
                        nc.vector.memset(spare[:, :], 0.0)
                    else:
                        invert(k - 1, (u - 1) % UN)
                    nc.vector.tensor_tensor_reduce(out=e[u][:, :], in0=e[u][:, :], in1=adj_sb[u % 2][:, :], scale=-1.0,
                                                   scalar=HIGHEST, op0=ALU.add, op1=ALU.min,
                                                   accum_out=neg_top[:, u:u + 1]).then_inc(s["masked"], 1)
                    if first_group and not first_head and u == 1:
                        dve.wait_ge(s["acc_ready"], h)
                        for c in range(NCH):
                            take(h - 1, c)
                if first_group and not first_head:
                    dve.wait_ge(s["elu_exp"], h)
                    dve.wait_ge(s["taken"], h * NCH)
                    nc.vector.scalar_tensor_tensor(acc[:, :], low[:, :], -1.0, acc[:, :], ALU.add, ALU.add).then_inc(s["acc_ready"], 1)

            def head(h, first):
                group(h, 0, first, True)
                with dve.Fori(1, NG) as q:
                    group(h, q, first, False)

            nc.vector.memset(acc[:, :], 0.0).then_inc(s["acc_ready"], 1)
            heads_and_groups(dve, head)
            invert(H3 * NT - 1, UN - 1)
            dve.wait_ge(s["acc_ready"], H3)
            dve.wait_ge(s["x_in"], 16)
            for c in range(NCH + 3):
                if c < NCH:
                    take(H3 - 1, c)
                if 1 <= c <= NCH:
                    dve.wait_ge(s["elu_exp"], H3 - 1 + c)
                    dve.wait_ge(s["taken"], (H3 - 1) * NCH + c)
                    part = acc[:, ts(c - 1, BANK)]
                    nc.vector.scalar_tensor_tensor(part, low[:, ts(c - 1, BANK)], -1.0, part,
                                                   ALU.add, ALU.add).then_inc(s["acc_ready"], 1)
                if c >= 3:
                    m = c - 3
                    dve.wait_ge(s["turned"], m + 1)
                    part = x[:, ts(m, TPB), :].rearrange("p t d -> p (t d)")
                    nc.vector.scalar_tensor_tensor(part, ps[:, m, :], 1.0 / H3, part, ALU.mult, ALU.add).then_inc(s["x_ready"], 1)


def build(nc, x, adj, w, out):
    adj_t = nc.dram_tensor("adj_t", [N, N], F32, kind="Internal").ap()
    proj = nc.dram_tensor("proj", [N, H3 * D], F32, kind="Internal").ap()
    src = nc.dram_tensor("src", [H3, N], F32, kind="Internal").ap()
    left = nc.dram_tensor("left", [P, NT, 2, P], F16, kind="Internal").ap()
    h2 = nc.dram_tensor("h2", [N, D], F32, kind="Internal").ap()
    x1, x2, x3 = (nc.dram_tensor(f"x{k}", [N, D], F32, kind="Internal").ap() for k in (1, 2, 3))
    first_sem = next_semaphore(nc)
    with ExitStack() as mem:
        g = Shared()
        g.identity = mem.enter_context(nc.sbuf_tensor("identity", [P, P], F32))
        g.var = mem.enter_context(nc.sbuf_tensor("var", [P, NT], F32))
        g.ones = mem.enter_context(nc.sbuf_tensor("ones", [P, P], F32))
        with nc.sbuf_tensor("rows", [P, NT, D], F32) as rows:
            g.rows = rows
            with nc.sbuf_tensor("agg_t", [P, N], F32) as agg_t:
                g.agg_t = agg_t
                with ExitStack() as m0:
                    g.blk = [m0.enter_context(nc.sbuf_tensor(f"blk{c}", [P, GR, CHT * P], F32)) for c in range(NT // CHT)]
                    g.loaded = [m0.enter_context(nc.semaphore(f"loaded{c}")) for c in range(NT // CHT)]
                    layer0_features(nc, g, x, adj)
                    layer0_aggregate(nc, g, adj, adj_t)
                layer0_combine(nc, g, w["L0_gnn_W1"], w["L0_gnn_b1"], w["L0_gnn_W2"], w["L0_gnn_b2"], x, x1)
            with ExitStack() as m1:
                attention_tiles(nc, g, m1, 1)
                g.unit_hi = m1.enter_context(nc.sbuf_tensor("unit_hi", [P, N], F16))
                g.unit_lo = m1.enter_context(nc.sbuf_tensor("unit_lo", [P, N], F16))
                g.log_row = m1.enter_context(nc.sbuf_tensor("log_row", [P, N], F32))
                g.half_log = m1.enter_context(nc.sbuf_tensor("half_log", [P, NT], F32))
                g.step = m1.enter_context(nc.sbuf_tensor("step", [P, 1], F32))
                g.neg_step = m1.enter_context(nc.sbuf_tensor("neg_step", [P, 1], F32))
                g.mask_step = m1.enter_context(nc.sbuf_tensor("mask_step", [P, 1], F32))
                layer1_features(nc, g, adj, w["L1_gnn_beta"], left)
                masked_attention(nc, g, 1, adj, x1, x2, left_dram=left, h_next_dram=h2)
            clear_semaphores(nc, first_sem, next_semaphore(nc))
            with ExitStack() as m2:
                attention_tiles(nc, g, m2, 2)
                g.neigh_row = m2.enter_context(nc.sbuf_tensor("neigh_row", [P, H2, N], F32))
                g.self_col = m2.enter_context(nc.sbuf_tensor("self_col", [P, NT, H2], F32))
                layer2_features(nc, g, adj, h2, w["L2_gnn_W"], w["L2_gnn_a_self"], w["L2_gnn_a_neigh"])
                masked_attention(nc, g, 2, adj, x2, x3, bias=w["L2_gnn_bias"])
        attention_tiles(nc, g, mem, 3)
        g.h_t = mem.enter_context(nc.sbuf_tensor("h_t", [P, N], F32))
        g.tgt = mem.enter_context(nc.sbuf_tensor("tgt", [P, H3, NT], F32))
        g.tgt_sloped = mem.enter_context(nc.sbuf_tensor("tgt_sloped", [P, H3, NT], F32))
        g.src = mem.enter_context(nc.sbuf_tensor("src_rows", [P, 2, N], F32))
        g.src0_in = mem.enter_context(nc.semaphore("src0_in"))
        layer3_features(nc, g, adj_t, x3, w["L3_gnn_W"], w["L3_gnn_a_src"], w["L3_gnn_a_tgt"], proj, src)
        layer3_attention(nc, g, adj_t, proj, src, x3, out)


_INS = ['x', 'adj', 'L0_gnn_W1', 'L0_gnn_b1', 'L0_gnn_W2', 'L0_gnn_b2', 'L1_gnn_beta', 'L2_gnn_W', 'L2_gnn_a_self',
        'L2_gnn_a_neigh', 'L2_gnn_bias', 'L3_gnn_W', 'L3_gnn_a_src', 'L3_gnn_a_tgt']


def kernel(**inputs):
    import numpy as _np
    import concourse.bacc as _bacc
    from concourse import mybir as _mybir
    from concourse.bass_utils import run_bass_kernel_spmd as _run

    nc = _bacc.Bacc("TRN2", target_bir_lowering=False, num_devices=1)
    arrays, args = {}, {}
    for name in _INS:
        a = _np.ascontiguousarray(inputs[name])
        arrays[f"in_{name}_dram"] = a
        args[name] = nc.dram_tensor(f"in_{name}_dram", a.shape, _mybir.dt.from_np(a.dtype), kind="ExternalInput").ap()
    out = nc.dram_tensor("out_0_dram", (N, D), _mybir.dt.float32, kind="ExternalOutput").ap()
    build(nc, args["x"], args["adj"], args, out)
    r = _run(nc, [arrays], core_ids=[0])
    return r.results[0]["out_0_dram"]
```
